# Optimizing a Trainium2 kernel written in Bass

```python
import numpy as np
import jax
import jax.numpy as jnp

def _softmax(x, axis=-1):
    return jax.nn.softmax(x, axis=axis)

def _gelu(x):
    return jax.nn.gelu(x, approximate=True)

def _silu(x):
    return jax.nn.silu(x)

def _sigmoid(x):
    return jax.nn.sigmoid(x)

def _layernorm(x, axis=-1, eps=1e-05):
    m = jnp.mean(x, axis=axis, keepdims=True)
    v = jnp.var(x, axis=axis, keepdims=True)
    return (x - m) / jnp.sqrt(v + eps)

def _scatter_add(tgt, idx, src, axis=0):
    return tgt.at[idx].add(src)

def _segment_sum(src, seg, n):
    return jax.ops.segment_sum(src, seg, n)
kernel_name = 'mk_adaln_d2_jaxref_r8_195ffa'

def setup_inputs(seed: int=0):
    np.random.seed(seed)
    _w = jnp.asarray

    def _L0_attn_setup():
        import jax, jax.numpy as jnp
        import numpy as np
        HIDDEN = 256
        N_HEADS = 32
        N_KV_HEADS = 8
        HEAD_DIM = HIDDEN // N_HEADS
        BATCH = 2
        SEQ = 256
        key = jax.random.key(seed)
        ks = jax.random.split(key, 5)
        scale = 1.0 / np.sqrt(HIDDEN)
        X = jax.random.normal(ks[0], (BATCH, SEQ, HIDDEN), dtype=jnp.float32)
        Wq = jax.random.normal(ks[1], (HIDDEN, N_HEADS * HEAD_DIM), dtype=jnp.float32) * scale
        Wk = jax.random.normal(ks[2], (HIDDEN, N_KV_HEADS * HEAD_DIM), dtype=jnp.float32) * scale
        Wv = jax.random.normal(ks[3], (HIDDEN, N_KV_HEADS * HEAD_DIM), dtype=jnp.float32) * scale
        Wo = jax.random.normal(ks[4], (N_HEADS * HEAD_DIM, HIDDEN), dtype=jnp.float32) * scale
        return {'X': X, 'Wq': Wq, 'Wk': Wk, 'Wv': Wv, 'Wo': Wo}
    _L0_attn_in = _L0_attn_setup()

    def _L0_ffn_setup():
        import jax, jax.numpy as jnp
        import numpy as np
        NUM_EXPERTS = 16
        TOP_K = 4
        N_GROUP = 4
        TOPK_GROUP = 2
        SCALING = 2.5

        def _route(x, gate_weight, expert_bias):
            logits = x @ gate_weight.T
            scores = jax.nn.sigmoid(logits)
            biased = scores + expert_bias[None, :]
            T = x.shape[0]
            gsz = NUM_EXPERTS // N_GROUP
            grp = biased.reshape(T, N_GROUP, gsz)
            top2, _ = jax.lax.top_k(grp, 2)
            group_scores = top2.sum(-1)
            _, gidx = jax.lax.top_k(group_scores, TOPK_GROUP)
            gmask = jax.nn.one_hot(gidx, N_GROUP, dtype=scores.dtype).sum(1)
            emask = jnp.repeat(gmask, gsz, axis=1)
            masked = jnp.where(emask > 0, biased, -jnp.inf)
            _, sel = jax.lax.top_k(masked, TOP_K)
            w = jnp.take_along_axis(scores, sel, axis=1)
            w = w / (w.sum(-1, keepdims=True) + 1e-20)
            return (w * SCALING, sel)

        def _moe(x, w, sel, gate_proj, up_proj, down_proj):
            cw = (jax.nn.one_hot(sel, NUM_EXPERTS, dtype=x.dtype) * w[..., None]).sum(1)

            def body(acc, inp):
                g, u, d, we = inp
                y = jax.nn.silu(x @ g.T) * (x @ u.T) @ d.T
                return (acc + we[:, None] * y, None)
            out, _ = jax.lax.scan(body, jnp.zeros_like(x), (gate_proj, up_proj, down_proj, cw.T))
            return out
        key = jax.random.key(seed)
        ks = jax.random.split(key, 9)
        B, S, H, I = (2, 128, 256, 128)
        w = lambda k, shape: jax.random.normal(k, shape, jnp.float32) * 0.02
        return {'hidden_states': jax.random.normal(ks[0], (B, S, H), jnp.float32), 'gate_weight': w(ks[1], (NUM_EXPERTS, H)), 'expert_bias': jnp.zeros((NUM_EXPERTS,), jnp.float32), 'gate_proj': w(ks[2], (NUM_EXPERTS, I, H)), 'up_proj': w(ks[3], (NUM_EXPERTS, I, H)), 'down_proj': w(ks[4], (NUM_EXPERTS, H, I)), 'shared_gate': w(ks[5], (I, H)), 'shared_up': w(ks[6], (I, H)), 'shared_down': w(ks[7], (H, I))}
    _L0_ffn_in = _L0_ffn_setup()
    _L0_c = _w((lambda *s: np.random.randn(*s).astype(np.float32) * 0.05)(1, 256))
    _L0_wmod = _w((lambda *s: np.random.randn(*s).astype(np.float32) * 0.05)(256, 6 * 256) * 256 ** (-0.5))

    def _L1_attn_setup():
        import jax, jax.numpy as jnp
        import numpy as np
        N_LAYERS = 4
        EMBED = 256
        BATCH = 2
        SEQ = 512

        def _sdpa(q, k, v):
            scale = 1.0 / np.sqrt(q.shape[-1])
            scores = jnp.einsum('bqd,bkd->bqk', q, k).astype(jnp.float32) * scale
            probs = jax.nn.softmax(scores, axis=-1).astype(v.dtype)
            return jnp.einsum('bqk,bkd->bqd', probs, v)
        key = jax.random.key(seed)
        ks = jax.random.split(key, 9)
        dt = jnp.bfloat16
        x = jax.random.normal(ks[0], (BATCH, SEQ, EMBED), dtype=dt)
        w_scale = 0.02

        def w(k):
            return (jax.random.normal(k, (N_LAYERS, EMBED, EMBED), dtype=jnp.float32) * w_scale).astype(dt)

        def b(k):
            return jnp.zeros((N_LAYERS, EMBED), dtype=dt)
        return {'x': x, 'Wq': w(ks[1]), 'bq': b(ks[1]), 'Wk': w(ks[2]), 'bk': b(ks[2]), 'Wv': w(ks[3]), 'bv': b(ks[3]), 'Wo': w(ks[4]), 'bo': b(ks[4])}
    _L1_attn_in = _L1_attn_setup()

    def _L1_ffn_setup():
        import jax, jax.numpy as jnp
        import numpy as np
        B, S, H = (2, 64, 256)
        E, G, TOPK_G, K = (64, 8, 4, 6)
        I = 64
        SH_I = 256
        RSF = 2.5

        def relu2(x):
            r = jax.nn.relu(x)
            return r * r
        key = jax.random.key(seed)
        ks = jax.random.split(key, 7)
        s = lambda d: 1.0 / np.sqrt(d)
        return {'hidden_states': jax.random.normal(ks[0], (B, S, H), jnp.float32), 'gate_w': jax.random.normal(ks[1], (E, H), jnp.float32) * s(H), 'gate_bias': jax.random.normal(ks[2], (E,), jnp.float32) * 0.01, 'w1': jax.random.normal(ks[3], (E, I, H), jnp.float32) * s(H), 'w2': jax.random.normal(ks[4], (E, H, I), jnp.float32) * s(I), 'shared_up': jax.random.normal(ks[5], (SH_I, H), jnp.float32) * s(H), 'shared_down': jax.random.normal(ks[6], (H, SH_I), jnp.float32) * s(SH_I)}
    _L1_ffn_in = _L1_ffn_setup()
    _L1_c = _w((lambda *s: np.random.randn(*s).astype(np.float32) * 0.05)(1, 256))
    _L1_wmod = _w((lambda *s: np.random.randn(*s).astype(np.float32) * 0.05)(256, 6 * 256) * 256 ** (-0.5))
    _d = {'L0_attn_X': _L0_attn_in['X'], 'L0_attn_Wq': _L0_attn_in['Wq'], 'L0_attn_Wk': _L0_attn_in['Wk'], 'L0_attn_Wv': _L0_attn_in['Wv'], 'L0_attn_Wo': _L0_attn_in['Wo'], 'L0_ffn_gate_weight': _L0_ffn_in['gate_weight'], 'L0_ffn_expert_bias': _L0_ffn_in['expert_bias'], 'L0_ffn_gate_proj': _L0_ffn_in['gate_proj'], 'L0_ffn_up_proj': _L0_ffn_in['up_proj'], 'L0_ffn_down_proj': _L0_ffn_in['down_proj'], 'L0_ffn_shared_gate': _L0_ffn_in['shared_gate'], 'L0_ffn_shared_up': _L0_ffn_in['shared_up'], 'L0_ffn_shared_down': _L0_ffn_in['shared_down'], 'L0_c': _L0_c, 'L0_wmod': _L0_wmod, 'L1_attn_Wq': _L1_attn_in['Wq'], 'L1_attn_bq': _L1_attn_in['bq'], 'L1_attn_Wk': _L1_attn_in['Wk'], 'L1_attn_bk': _L1_attn_in['bk'], 'L1_attn_Wv': _L1_attn_in['Wv'], 'L1_attn_bv': _L1_attn_in['bv'], 'L1_attn_Wo': _L1_attn_in['Wo'], 'L1_attn_bo': _L1_attn_in['bo'], 'L1_ffn_gate_w': _L1_ffn_in['gate_w'], 'L1_ffn_gate_bias': _L1_ffn_in['gate_bias'], 'L1_ffn_w1': _L1_ffn_in['w1'], 'L1_ffn_w2': _L1_ffn_in['w2'], 'L1_ffn_shared_up': _L1_ffn_in['shared_up'], 'L1_ffn_shared_down': _L1_ffn_in['shared_down'], 'L1_c': _L1_c, 'L1_wmod': _L1_wmod}
    _x0 = _d['L0_attn_X']
    _d['L0_attn_X'] = jax.random.normal(jax.random.fold_in(jax.random.key(seed), 1), (1, 1024, 256), dtype=_x0.dtype)
    del _x0
    return _d

def reference(L0_attn_X, L0_attn_Wq, L0_attn_Wk, L0_attn_Wv, L0_attn_Wo, L0_ffn_gate_weight, L0_ffn_expert_bias, L0_ffn_gate_proj, L0_ffn_up_proj, L0_ffn_down_proj, L0_ffn_shared_gate, L0_ffn_shared_up, L0_ffn_shared_down, L0_c, L0_wmod, L1_attn_Wq, L1_attn_bq, L1_attn_Wk, L1_attn_bk, L1_attn_Wv, L1_attn_bv, L1_attn_Wo, L1_attn_bo, L1_ffn_gate_w, L1_ffn_gate_bias, L1_ffn_w1, L1_ffn_w2, L1_ffn_shared_up, L1_ffn_shared_down, L1_c, L1_wmod):

    def _L0_attn_ref(X, Wq, Wk, Wv, Wo):
        import jax, jax.numpy as jnp
        import numpy as np
        HIDDEN = 256
        N_HEADS = 32
        N_KV_HEADS = 8
        HEAD_DIM = HIDDEN // N_HEADS
        BATCH = 2
        SEQ = 256
        B, S, _ = X.shape
        num_groups = N_HEADS // N_KV_HEADS
        q = (X @ Wq).reshape(B, S, N_HEADS, HEAD_DIM).transpose(0, 2, 1, 3)
        k = (X @ Wk).reshape(B, S, N_KV_HEADS, HEAD_DIM).transpose(0, 2, 1, 3)
        v = (X @ Wv).reshape(B, S, N_KV_HEADS, HEAD_DIM).transpose(0, 2, 1, 3)
        k = jnp.repeat(k, num_groups, axis=1)
        v = jnp.repeat(v, num_groups, axis=1)
        scores = jnp.einsum('bhqd,bhkd->bhqk', q, k) / np.sqrt(HEAD_DIM)
        weights = jax.nn.softmax(scores, axis=-1)
        out = jnp.einsum('bhqk,bhkd->bhqd', weights, v)
        out = out.transpose(0, 2, 1, 3).reshape(B, S, N_HEADS * HEAD_DIM)
        return out @ Wo

    def _L0_ffn_ref(hidden_states, gate_weight, expert_bias, gate_proj, up_proj, down_proj, shared_gate, shared_up, shared_down):
        import jax, jax.numpy as jnp
        import numpy as np
        NUM_EXPERTS = 16
        TOP_K = 4
        N_GROUP = 4
        TOPK_GROUP = 2
        SCALING = 2.5

        def _route(x, gate_weight, expert_bias):
            logits = x @ gate_weight.T
            scores = jax.nn.sigmoid(logits)
            biased = scores + expert_bias[None, :]
            T = x.shape[0]
            gsz = NUM_EXPERTS // N_GROUP
            grp = biased.reshape(T, N_GROUP, gsz)
            top2, _ = jax.lax.top_k(grp, 2)
            group_scores = top2.sum(-1)
            _, gidx = jax.lax.top_k(group_scores, TOPK_GROUP)
            gmask = jax.nn.one_hot(gidx, N_GROUP, dtype=scores.dtype).sum(1)
            emask = jnp.repeat(gmask, gsz, axis=1)
            masked = jnp.where(emask > 0, biased, -jnp.inf)
            _, sel = jax.lax.top_k(masked, TOP_K)
            w = jnp.take_along_axis(scores, sel, axis=1)
            w = w / (w.sum(-1, keepdims=True) + 1e-20)
            return (w * SCALING, sel)

        def _moe(x, w, sel, gate_proj, up_proj, down_proj):
            cw = (jax.nn.one_hot(sel, NUM_EXPERTS, dtype=x.dtype) * w[..., None]).sum(1)

            def body(acc, inp):
                g, u, d, we = inp
                y = jax.nn.silu(x @ g.T) * (x @ u.T) @ d.T
                return (acc + we[:, None] * y, None)
            out, _ = jax.lax.scan(body, jnp.zeros_like(x), (gate_proj, up_proj, down_proj, cw.T))
            return out
        B, S, H = hidden_states.shape
        x = hidden_states.reshape(-1, H)
        w, sel = _route(x, gate_weight, expert_bias)
        out = _moe(x, w, sel, gate_proj, up_proj, down_proj)
        shared = jax.nn.silu(x @ shared_gate.T) * (x @ shared_up.T) @ shared_down.T
        return (out + shared).reshape(B, S, H)

    def _L1_attn_ref(x, Wq, bq, Wk, bk, Wv, bv, Wo, bo):
        import jax, jax.numpy as jnp
        import numpy as np
        N_LAYERS = 4
        EMBED = 256
        BATCH = 2
        SEQ = 512

        def _sdpa(q, k, v):
            scale = 1.0 / np.sqrt(q.shape[-1])
            scores = jnp.einsum('bqd,bkd->bqk', q, k).astype(jnp.float32) * scale
            probs = jax.nn.softmax(scores, axis=-1).astype(v.dtype)
            return jnp.einsum('bqk,bkd->bqd', probs, v)
        for i in range(N_LAYERS):
            q = x @ Wq[i] + bq[i]
            k = x @ Wk[i] + bk[i]
            v = x @ Wv[i] + bv[i]
            attn = _sdpa(q, k, v)
            x = attn @ Wo[i] + bo[i]
        return x

    def _L1_ffn_ref(hidden_states, gate_w, gate_bias, w1, w2, shared_up, shared_down):
        import jax, jax.numpy as jnp
        import numpy as np
        B, S, H = (2, 64, 256)
        E, G, TOPK_G, K = (64, 8, 4, 6)
        I = 64
        SH_I = 256
        RSF = 2.5

        def relu2(x):
            r = jax.nn.relu(x)
            return r * r
        x = hidden_states.reshape(-1, H)
        T = x.shape[0]
        logits = jnp.dot(x.astype(jnp.float32), gate_w.astype(jnp.float32).T)
        scores = jax.nn.sigmoid(logits)
        scores_b = scores + gate_bias
        sb_g = scores_b.reshape(T, G, E // G)
        group_scores = jnp.sum(jax.lax.top_k(sb_g, 2)[0], axis=-1)
        grp_idx = jax.lax.top_k(group_scores, TOPK_G)[1]
        grp_mask = jnp.sum(jax.nn.one_hot(grp_idx, G, dtype=jnp.float32), axis=1)
        expert_mask = jnp.repeat(grp_mask, E // G, axis=-1) > 0
        masked = jnp.where(expert_mask, scores_b, -jnp.inf)
        _, top_idx = jax.lax.top_k(masked, K)
        topw = jnp.take_along_axis(scores, top_idx, axis=1)
        topw = topw / (jnp.sum(topw, axis=-1, keepdims=True) + 1e-20) * RSF
        w_dense = jnp.zeros((T, E), jnp.float32).at[jnp.arange(T)[:, None], top_idx].add(topw)
        h = relu2(jnp.einsum('th,eih->tei', x, w1))
        h = h * w_dense[:, :, None]
        routed = jnp.einsum('tei,ehi->th', h, w2)
        shared = jnp.dot(relu2(jnp.dot(x, shared_up.T)), shared_down.T)
        out = (routed + shared).astype(hidden_states.dtype)
        return out.reshape(hidden_states.shape)
    x = L0_attn_X
    mod = (_silu(L0_c) @ L0_wmod).reshape(L0_c.shape[0], 6, 1, -1)
    sa, ca, ga, sb, cb, gb = (mod[:, 0], mod[:, 1], mod[:, 2], mod[:, 3], mod[:, 4], mod[:, 5])
    ga = (2 * (ga >= 0) - 1) * jnp.maximum(jnp.abs(ga), 0.25)
    gb = (2 * (gb >= 0) - 1) * jnp.maximum(jnp.abs(gb), 0.25)
    h = _layernorm(x, axis=-1) * (1 + ca) + sa
    x = x + ga * _L0_attn_ref(h, L0_attn_Wq, L0_attn_Wk, L0_attn_Wv, L0_attn_Wo)
    h = _layernorm(x, axis=-1) * (1 + cb) + sb
    x = x + gb * _L0_ffn_ref(h, L0_ffn_gate_weight, L0_ffn_expert_bias, L0_ffn_gate_proj, L0_ffn_up_proj, L0_ffn_down_proj, L0_ffn_shared_gate, L0_ffn_shared_up, L0_ffn_shared_down)
    mod = (_silu(L1_c) @ L1_wmod).reshape(L1_c.shape[0], 6, 1, -1)
    sa, ca, ga, sb, cb, gb = (mod[:, 0], mod[:, 1], mod[:, 2], mod[:, 3], mod[:, 4], mod[:, 5])
    ga = (2 * (ga >= 0) - 1) * jnp.maximum(jnp.abs(ga), 0.25)
    gb = (2 * (gb >= 0) - 1) * jnp.maximum(jnp.abs(gb), 0.25)
    h = _layernorm(x, axis=-1) * (1 + ca) + sa
    x = x + ga * _L1_attn_ref(h, L1_attn_Wq, L1_attn_bq, L1_attn_Wk, L1_attn_bk, L1_attn_Wv, L1_attn_bv, L1_attn_Wo, L1_attn_bo)
    h = _layernorm(x, axis=-1) * (1 + cb) + sb
    x = x + gb * _L1_ffn_ref(h, L1_ffn_gate_w, L1_ffn_gate_bias, L1_ffn_w1, L1_ffn_w2, L1_ffn_shared_up, L1_ffn_shared_down)
    return x

_drawn_inputs = setup_inputs


def setup_inputs(seed=0):
    import zlib

    import numpy as np

    out = dict(_drawn_inputs(seed))
    spreads = {'L0_ffn_expert_bias': (0.0, 0.33),
     'L1_attn_bq': (0.0, 2.0),
     'L1_attn_bk': (0.0, 2.0),
     'L1_attn_bv': (0.0, 0.1),
     'L1_attn_bo': (0.0, 0.1)}
    factors = {'L0_ffn_gate_weight': 3.457,
     'L0_ffn_gate_proj': 2.695,
     'L0_ffn_up_proj': 2.826,
     'L0_ffn_shared_gate': 3.914,
     'L0_ffn_shared_up': 4.365,
     'L0_ffn_shared_down': 3.525,
     'L1_attn_Wq': 185.41,
     'L1_attn_Wk': 190.088,
     'L1_attn_Wv': 3.747}
    for name, (base, spread) in spreads.items():
        noise = np.random.default_rng([zlib.crc32(name.encode()), seed]).standard_normal(out[name].shape)
        drawn = base * np.exp(spread * noise) if base else spread * noise
        out[name] = jnp.asarray(drawn.astype(out[name].dtype))
    for name, factor in factors.items():
        out[name] = (out[name] * factor).astype(out[name].dtype)
    return out
```

```python
import concourse.bass as bass
from concourse import mybir
from concourse.alu_op_type import AluOpType as ALU
from contextlib import ExitStack
import numpy as np

F32 = mybir.dt.float32
F32R = mybir.dt.float32r
BF16 = mybir.dt.bfloat16
ACT = mybir.ActivationFunctionType
AX = mybir.AxisListType

P = 128
T = 1024
D = 256
NJ = T // P
NC = D // P
HALF = 512
NH = T // HALF
BANKS = 8
EPS = 1e-5

HEADS, KV_HEADS, DH = 32, 8, 8
GQ = HEADS // KV_HEADS
QUAD = 32
M_HI, M_LO = 3 * DH, 3 * DH + 1
VCOLS = DH + 1
BIG = 3.0e38

E0, G0, TOPG0, K0, SCALE0 = 16, 4, 2, 4, 2.5
E1, G1, TOPG1, K1, SCALE1 = 64, 8, 4, 6, 2.5
LAYERS = 4


class Order:

    def __init__(self, eng, sem):
        self.eng, self.sem, self.done, self.peak = eng, sem, 0, 0

    def mark(self, ins):
        ins.then_inc(self.sem, 1)
        self.done = self.done + 1
        return ins

    def settle(self):
        self.eng.wait_ge(self.sem, self.done)

    def link(self, ins):
        self.mark(ins)
        self.settle()


class Chip:

    def __init__(self, nc, ctx):
        self.nc, self.ctx = nc, ctx
        self.ps = ctx.enter_context(nc.psum_tensor("ps", [P, BANKS, HALF], F32))
        self.xT = self.sb("xT", [P, NC, T])
        self.h_hi = self.sb("h_hi", [P, NC, T], F32R)
        self.h_lo = self.sb("h_lo", [P, NC, T], F32R)
        self.ident = self.sb("ident", [P, P])
        self.mods = [self.sb(f"mod{i}", [P, 12]) for i in range(2)]
        self.norm_sems = [self.sem("ln_" + s) for s in ("tok", "var", "sd", "rstd", "xna", "xnd", "back", "hi", "ord")]
        self.norms = 0

    def sb(self, name, shape, dt=F32, ctx=None):
        return (ctx or self.ctx).enter_context(self.nc.sbuf_tensor(name, shape, dt))

    def sem(self, name, ctx=None):
        return self.ctx.enter_context(self.nc.semaphore(name))


def mod_col(chip, layer, which, c):
    return chip.mods[layer][:, which * NC + c:which * NC + c + 1]


def modulation(nc, chip, layer, c_cols, wmod, extra_loads=None):
    n = f"mo{layer}_"
    with ExitStack() as ctx:
        w = chip.sb(n + "w", [P, NC, 6 * D], ctx=ctx)
        c_in = chip.sb(n + "c", [P, NC], ctx=ctx)
        c_act = chip.sb(n + "ca", [P, NC], ctx=ctx)
        tmp = chip.sb(n + "t", [P, 3, NC], ctx=ctx)
        w_in, c_done, act_done, mm_done, order_sem = (
            chip.sem(n + s, ctx) for s in ("w_in", "c_in", "act", "mm", "ord"))
        block = ctx.enter_context(nc.Block())

        @block.sync
        def _(sp):
            sp.dma_start(c_in[:], c_cols).then_inc(c_done, 16)
            sp.dma_start(w[:], wmod.rearrange("(k p) n -> p k n", p=P)).then_inc(w_in, 16)

        @block.scalar
        def _(act):
            act.wait_ge(c_done, 16)
            nc.scalar.activation(c_act[:], c_in[:], ACT.Silu).then_inc(act_done, 1)

        @block.tensor
        def _(pe):
            pe.wait_ge(act_done, 1)
            pe.wait_ge(w_in, 16)
            for m in range(6 * NC):
                for k in range(NC):
                    last = nc.tensor.matmul(chip.ps[:, 0, m:m + 1], w[:, k, m * P:(m + 1) * P],
                                            c_act[:, k:k + 1], start=(k == 0), stop=(k == NC - 1))
            last.then_inc(mm_done, 1)

        @block.vector
        def _(dve):
            order = Order(dve, order_sem)
            dve.wait_ge(mm_done, 1)
            mod = chip.mods[layer]
            order.link(nc.vector.tensor_copy(mod[:], chip.ps[:, 0, 0:6 * NC]))
            for which in (1, 4):
                cols = mod[:, which * NC:(which + 1) * NC]
                order.mark(nc.vector.tensor_scalar(cols, cols, 1.0, None, ALU.add))
            for which in (2, 5):
                cols = mod[:, which * NC:(which + 1) * NC]
                order.mark(nc.vector.tensor_scalar(tmp[:, 0, :], cols, 0.0, None, ALU.is_ge))
                order.link(nc.vector.tensor_scalar(tmp[:, 2, :], cols, -1.0, None, ALU.mult))
                order.mark(nc.vector.tensor_scalar(tmp[:, 0, :], tmp[:, 0, :], 2.0, -1.0, ALU.mult, ALU.add))
                order.link(nc.vector.tensor_tensor(tmp[:, 1, :], cols, tmp[:, 2, :], ALU.max))
                order.link(nc.vector.tensor_scalar(tmp[:, 1, :], tmp[:, 1, :], 0.25, None, ALU.max))
                order.link(nc.vector.tensor_tensor(cols, tmp[:, 0, :], tmp[:, 1, :], ALU.mult))


def first_load(nc, chip, x, ident):
    with ExitStack() as ctx:
        xt = chip.sb("x_tok", [P, NJ, D], ctx=ctx)
        x_in, id_in, turned = (chip.sem("fl_" + s, ctx) for s in ("x", "id", "turned"))
        block = ctx.enter_context(nc.Block())

        @block.sync
        def _(sp):
            sp.dma_start(chip.ident[:], ident).then_inc(id_in, 16)
            sp.dma_start(xt[:], x.rearrange("a (j p) d -> p (a j) d", p=P)).then_inc(x_in, 16)

        @block.tensor
        def _(pe):
            pe.wait_ge(id_in, 16)
            pe.wait_ge(x_in, 16)
            for half in range(NH):
                for c in range(NC):
                    for q in range(4):
                        last = nc.tensor.transpose(chip.ps[:, half * NC + c, q * P:(q + 1) * P],
                                                   xt[:, half * 4 + q, c * P:(c + 1) * P], chip.ident[:])
                    last.then_inc(turned, 1)

        @block.vector
        def _(dve):
            for half in range(NH):
                for c in range(NC):
                    dve.wait_ge(turned, half * NC + c + 1)
                    nc.vector.tensor_copy(chip.xT[:, c, half * HALF:(half + 1) * HALF],
                                          chip.ps[:, half * NC + c, :])


def norm(nc, chip, tag, layer, shift, scale):
    n = f"ln{tag}_"
    with ExitStack() as ctx:
        xn = chip.sb(n + "xn", [P, NJ, D], ctx=ctx)
        hf = chip.sb(n + "hf", [P, 2, HALF], ctx=ctx)
        st = chip.sb(n + "st", [P, NJ, 6], ctx=ctx)
        mv = chip.sb(n + "mv", [P, NJ, 2], ctx=ctx)
        var, sd, r0, r1 = (chip.sb(n + s, [P, NJ], ctx=ctx) for s in ("var", "sd", "r0", "r1"))
        rstd = chip.sb(n + "rs", [P, NJ], ctx=ctx)
        nmr = chip.sb(n + "nm", [P, NJ], ctx=ctx)
        tok_ready, var_ready, sd_ready, rstd_ready, xn_act, xn_dve, back_ready, hi_ready, order_sem = chip.norm_sems
        k = chip.norms
        chip.norms += 1
        block = ctx.enter_context(nc.Block())

        @block.tensor
        def _(pe):
            for j in range(NJ):
                for c in range(NC):
                    last = nc.tensor.transpose(chip.ps[:, j // 2, (j % 2) * D + c * P:(j % 2) * D + (c + 1) * P],
                                               chip.xT[:, c, j * P:(j + 1) * P], chip.ident[:])
                if j % 2:
                    last.then_inc(tok_ready, 1)
            for j in range(NJ):
                if j % 4 == 0:
                    pe.wait_ge(xn_act, 4 * k + j // 2 + 2)
                    pe.wait_ge(xn_dve, 4 * k + j // 2 + 2)
                for c in range(NC):
                    last = nc.tensor.transpose(chip.ps[:, 4 + (j // 4) * NC + c, (j % 4) * P:(j % 4 + 1) * P],
                                               xn[:, j, c * P:(c + 1) * P], chip.ident[:])
                if j % 4 == 3:
                    last.then_inc(back_ready, 1)

        @block.vector
        def _(dve):
            order = Order(dve, order_sem)
            order.done = k * (2 * NJ + 5 + NH * NC)
            for j in range(NJ):
                if j % 2 == 0:
                    dve.wait_ge(tok_ready, 4 * k + j // 2 + 1)
                order.mark(nc.vector.bn_stats(st[:, j, :], chip.ps[:, j // 2, (j % 2) * D:(j % 2 + 1) * D]))
            order.settle()
            for j in range(NJ):
                last = order.mark(nc.vector.bn_aggr(mv[:, j, :], st[:, j, :]))
            order.settle()
            nc.vector.tensor_scalar(var[:], mv[:, :, 1], EPS, None, ALU.add).then_inc(var_ready, 1)
            dve.wait_ge(sd_ready, k + 1)
            order.link(nc.vector.reciprocal(r0[:], sd[:]))
            order.link(nc.vector.tensor_tensor(r1[:], r0[:], r0[:], ALU.mult))
            order.link(nc.vector.tensor_tensor(r1[:], r1[:], var[:], ALU.mult))
            order.link(nc.vector.tensor_scalar(r1[:], r1[:], -0.5, 1.5, ALU.mult, ALU.add))
            order.link(nc.vector.tensor_tensor(rstd[:], r0[:], r1[:], ALU.mult))
            nc.vector.scalar_tensor_tensor(nmr[:], mv[:, :, 0], -1.0, rstd[:], ALU.mult, ALU.mult)\
                .then_inc(rstd_ready, 1)
            for j in (2, 3, 6, 7):
                nc.vector.tensor_scalar(xn[:, j, :], chip.ps[:, j // 2, (j % 2) * D:(j % 2 + 1) * D],
                                        mv[:, j, 0:1], rstd[:, j:j + 1], ALU.subtract, ALU.mult)\
                    .then_inc(xn_dve, 1)
            for i in range(NH * NC):
                half, c = i // NC, i % NC
                cols = slice(half * HALF, (half + 1) * HALF)
                dve.wait_ge(hi_ready, 4 * k + i + 1)
                order.link(nc.vector.tensor_scalar(hf[:, i % 2, :], chip.ps[:, 4 + i, :],
                                                   mod_col(chip, layer, scale, c), mod_col(chip, layer, shift, c),
                                                   ALU.mult, ALU.add))
                nc.vector.tensor_tensor(chip.h_lo[:, c, cols], hf[:, i % 2, :],
                                        chip.h_hi[:, c, cols].bitcast(F32), ALU.subtract)

        @block.scalar
        def _(act):
            act.wait_ge(var_ready, k + 1)
            nc.scalar.activation(sd[:], var[:], ACT.Sqrt).then_inc(sd_ready, 1)
            act.wait_ge(rstd_ready, k + 1)
            for j in (0, 1, 4, 5):
                nc.scalar.activation(xn[:, j, :], chip.ps[:, j // 2, (j % 2) * D:(j % 2 + 1) * D], ACT.Identity,
                                     bias=nmr[:, j:j + 1], scale=rstd[:, j:j + 1]).then_inc(xn_act, 1)
            for i in range(NH * NC):
                half, c = i // NC, i % NC
                act.wait_ge(back_ready, 2 * k + half + 1)
                nc.scalar.activation(chip.h_hi[:, c, half * HALF:(half + 1) * HALF], chip.ps[:, 4 + i, :],
                                     ACT.Identity, bias=mod_col(chip, layer, shift, c),
                                     scale=mod_col(chip, layer, scale, c)).then_inc(hi_ready, 1)


def three_parts(pe_out, nc, w_hi, w_lo, m_hi, m_lo, chunks, last_inc=None):
    n = 3 * len(chunks)
    i = 0
    for k in chunks:
        for w, m in ((w_hi, m_hi), (w_hi, m_lo), (w_lo, m_hi)):
            last = nc.tensor.matmul(pe_out, w(k), m(k), start=(i == 0), stop=(i == n - 1))
            i += 1
    return last


def attention0(nc, chip, wq, wk, wv, wo, rep_q, rep_k, lanes):
    with ExitStack() as ctx:
        qT = chip.sb("a_qT", [P, 5, T], F32R, ctx)
        krep = chip.sb("a_krep", [P, KV_HEADS, T], F32R, ctx)
        vall = chip.sb("a_vall", [P, KV_HEADS, NJ, QUAD], ctx=ctx)
        repq_r = chip.sb("a_repq_r", [P, 2, P], F32R, ctx)
        id_r = chip.sb("a_id_r", [P, P], F32R, ctx)
        attention0_project(nc, chip, wq, wk, wv, rep_q, rep_k, lanes, qT, krep, vall, repq_r, id_r)
        out = chip.sb("a_out", [P, NJ, D], ctx=ctx)
        attention0_core(nc, chip, qT, krep, vall, repq_r, id_r, out)
        attention0_output(nc, chip, wo, out)


def attention0_project(nc, chip, wq, wk, wv, rep_q, rep_k, lanes, qT, krep, vall, repq_r, id_r):
    with ExitStack() as ctx:
        wraw = chip.sb("ap_w", [P, NC, D + 2 * 64], ctx=ctx)
        wd = [chip.sb(f"ap_wd{i}", [P, NC, 5, 2, 64], F32R, ctx) for i in range(2)]
        wvp = [chip.sb(f"ap_wv{i}", [P, NC, 64], F32R, ctx) for i in range(2)]
        rk = chip.sb("ap_rk", [P, KV_HEADS, P], ctx=ctx)
        rk_r = chip.sb("ap_rk_r", [P, KV_HEADS, P], F32R, ctx)
        rq = chip.sb("ap_rq", [P, 2, P], ctx=ctx)
        lane = chip.sb("ap_lane", [P, 2], ctx=ctx)
        hi = chip.sb("ap_hi", [P, 2, HALF], F32R, ctx)
        w_in, c_in, w_split, r_ready, mm, hi_done, freed, rep_mm, v_mm, rep_a, rep_d, zeroed = (
            chip.sem("ap_" + s, ctx) for s in ("w", "c", "split", "r", "mm", "hi", "free", "rmm", "vmm",
                                               "ra", "rd", "z"))
        order_sem = chip.sem("ap_ord", ctx)
        JOBS = [(t, half) for t in (4, 0, 1, 2, 3) for half in range(NH)]
        block = ctx.enter_context(nc.Block())

        @block.sync
        def _(sp):
            for w, a, b in ((wq, 0, D), (wk, D, D + 64), (wv, D + 64, D + 128)):
                sp.dma_start(wraw[:, :, a:b], w.rearrange("(k p) n -> p k n", p=P)).then_inc(w_in, 16)
            sp.dma_start(rk[:], rep_k).then_inc(c_in, 16)
            sp.dma_start(rq[:], rep_q).then_inc(c_in, 16)
            sp.dma_start(lane[:], lanes).then_inc(c_in, 16)

        @block.gpsimd
        def _(pool):
            nc.gpsimd.memset(vall[:], 0.0).then_inc(zeroed, 1)
            pool.wait_ge(zeroed, 1)
            nc.gpsimd.memset(vall[:, :, :, DH:DH + 1], 1.0).then_inc(zeroed, 1)

        @block.vector
        def _(dve):
            order = Order(dve, order_sem)
            dve.wait_ge(w_in, 48)
            for t in range(5):
                cols = wraw[:, :, t * 64:(t + 1) * 64]
                for r in range(2):
                    order.mark(nc.vector.tensor_copy(wd[0][:, :, t, r, :], cols))
            order.mark(nc.vector.tensor_copy(wvp[0][:], wraw[:, :, 5 * 64:6 * 64]))
            order.settle()
            for t in range(5):
                cols = wraw[:, :, t * 64:(t + 1) * 64]
                for r in range(2):
                    nc.vector.tensor_tensor(wd[1][:, :, t, r, :], cols, wd[0][:, :, t, r, :].bitcast(F32),
                                            ALU.subtract)
            nc.vector.tensor_tensor(wvp[1][:], wraw[:, :, 5 * 64:6 * 64], wvp[0][:].bitcast(F32), ALU.subtract)\
                .then_inc(w_split, 1)
            dve.wait_ge(c_in, 48)
            nc.vector.tensor_copy(rk_r[:], rk[:])
            nc.vector.tensor_copy(id_r[:], chip.ident[:])
            nc.vector.tensor_copy(repq_r[:], rq[:]).then_inc(r_ready, 1)
            for n, (t, half) in enumerate(JOBS):
                dve.wait_ge(hi_done, n + 1)
                nc.vector.scalar_tensor_tensor(qT[:, t, half * HALF:(half + 1) * HALF],
                                               hi[:, n % 2, :].bitcast(F32), lane[:, 0:1], chip.ps[:, n % 2, :],
                                               ALU.mult, ALU.add).then_inc(freed, 1)
            dve.wait_ge(v_mm, 1)
            dve.wait_ge(zeroed, 2)
            nc.vector.tensor_copy(vall[:, :, :, 0:DH].rearrange("p g j d -> p j g d"),
                                  chip.ps[:, 2, :].rearrange("p (j g d) -> p j g d", j=NJ, g=KV_HEADS))
            for n in range(1, 2 * KV_HEADS, 2):
                dve.wait_ge(rep_mm, n + 1)
                nc.vector.tensor_scalar(krep[:, n // 2, HALF:T], chip.ps[:, 4 + n % 4, :], lane[:, 1:2], None,
                                        ALU.add).then_inc(rep_d, 1)

        @block.scalar
        def _(act):
            for n, (t, half) in enumerate(JOBS):
                act.wait_ge(mm, n + 1)
                if n >= 2:
                    act.wait_ge(freed, n - 1)
                nc.scalar.activation(hi[:, n % 2, :], chip.ps[:, n % 2, :], ACT.Copy).then_inc(hi_done, 1)
            act.wait_ge(r_ready, 1)
            for n in range(0, 2 * KV_HEADS, 2):
                act.wait_ge(rep_mm, n + 1)
                nc.scalar.activation(krep[:, n // 2, 0:HALF], chip.ps[:, 4 + n % 4, :], ACT.Identity,
                                     bias=lane[:, 1:2]).then_inc(rep_a, 1)

        @block.tensor
        def _(pe):
            pe.wait_ge(w_split, 1)
            for n, (t, half) in enumerate(JOBS):
                cols = slice(half * HALF, (half + 1) * HALF)
                if n >= 2:
                    pe.wait_ge(freed, n - 1)
                three_parts(chip.ps[:, n % 2, :], nc,
                            lambda k: wd[0][:, k, t, :, :], lambda k: wd[1][:, k, t, :, :],
                            lambda k: chip.h_hi[:, k, cols], lambda k: chip.h_lo[:, k, cols],
                            range(NC)).then_inc(mm, 1)
            for j in range(NJ):
                cols = slice(j * P, (j + 1) * P)
                last = three_parts(chip.ps[:, 2, j * 64:(j + 1) * 64], nc,
                                   lambda k: chip.h_hi[:, k, cols], lambda k: chip.h_lo[:, k, cols],
                                   lambda k: wvp[0][:, k, :], lambda k: wvp[1][:, k, :], range(NC))
            last.then_inc(v_mm, 1)
            pe.wait_ge(r_ready, 1)
            for n in range(2 * KV_HEADS):
                if n >= 4:
                    pe.wait_ge(rep_d if n % 2 else rep_a, (n - 4) // 2 + 1)
                nc.tensor.matmul(chip.ps[:, 4 + n % 4, :], rk_r[:, n // 2, :],
                                 qT[:, 4, (n % 2) * HALF:(n % 2 + 1) * HALF], start=True, stop=True)\
                    .then_inc(rep_mm, 1)


def attention0_core(nc, chip, qT, krep, vall, repq_r, id_r, out):
    ps = chip.ps
    STEPS = NH * NJ
    NMAX = GQ * NJ * NH
    PER = NMAX // STEPS
    MID = NJ + 1
    MAXB, PVB, TRB = 4, 6, 7
    SLOTS = 4
    SCALE = float(DH) ** -0.5
    LASTG = KV_HEADS - 1
    with ExitStack() as ctx:
        kk = [chip.sb(f"ac_kk{i}", [P, GQ, T], F32R, ctx) for i in range(2)]
        qa = [chip.sb(f"ac_qa{i}", [P, T], F32R, ctx) for i in range(2)]
        qb = [chip.sb(f"ac_qb{i}", [P, T], F32R, ctx) for i in range(2)]
        vg = [chip.sb(f"ac_vg{i}", [P, NJ, QUAD], ctx=ctx) for i in range(2)]
        probs = chip.sb("ac_p", [P, SLOTS, GQ, HALF], ctx=ctx)
        ot = chip.sb("ac_ot", [P, 2, HALF], ctx=ctx)
        mxp = chip.sb("ac_mxp", [P, NJ, GQ, NH], ctx=ctx)
        nm = chip.sb("ac_nm", [P, NJ, GQ], ctx=ctx)
        m4 = chip.sb("ac_m4", [P, NJ, P], F32R, ctx)
        rinv = chip.sb("ac_ri", [P, 4, GQ], ctx=ctx)
        names = ("score_mm", "exp_done", "pv_mm", "o_out", "o_turned", "o_done", "max_mm", "max_done", "m_ready",
                 "qa_mm", "qa_done", "qb_mm", "qb_done", "kk_done", "vg_done", "zeroed", "ord")
        (score_mm, exp_done, pv_mm, o_out, o_turned, o_done, max_mm, max_done, m_ready,
         qa_mm, qa_done, qb_mm, qb_done, kk_done, vg_done, zeroed, order_sem) = (
            chip.sem("ac_" + s, ctx) for s in names)
        m4q = m4[:].rearrange("p j (h r) -> p j h r", h=GQ)
        block = ctx.enter_context(nc.Block())

        def groups(eng, body):
            body(0, 0, 0, 1)
            with eng.Fori(0, (KV_HEADS - 2) // 2) as i:
                for u in range(2):
                    body(i * 2 + (1 + u), (1 + u) % 2, i + 1, i + (1 + (1 + u) // 2))
            body(LASTG, LASTG % 2, None, None)

        def is_first(g):
            return isinstance(g, int) and g == 0

        def is_last(g):
            return isinstance(g, int) and g == LASTG

        def block_of(n):
            qh, r = divmod(n, NMAX // 2)
            h, r = divmod(r, NMAX // 2 // GQ)
            return h, qh * (NJ // 2) + r // NH, r % NH

        def blocks_at(g, step):
            if step == 0:
                return [] if is_first(g) else [(0, n) for n in range(NMAX - PER, NMAX)]
            if is_last(g):
                return []
            return [(1, n) for n in range((step - 1) * PER, step * PER)]

        def pair_of(g, par, pair1):
            return LASTG // 2 if is_last(g) else (pair1 if par == 0 else pair1 - 1)

        @block.tensor
        def _(pe):
            def max_block(slot, n):
                h, j, half = block_of(n)
                nc.tensor.matmul(ps[:, MAXB + n % 2, :], qa[slot][:, j * P:(j + 1) * P],
                                 kk[slot][:, h, half * HALF:(half + 1) * HALF], start=True, stop=True)\
                    .then_inc(max_mm, 1)

            def spread_q(pair, par, half):
                nc.tensor.matmul(ps[:, TRB, :], repq_r[:, par, :], qT[:, pair, half * HALF:(half + 1) * HALF],
                                 start=True, stop=True).then_inc(qa_mm, 1)

            def spread_q_max(pair, par, half):
                for q in range(4):
                    cols = slice(half * HALF + q * P, half * HALF + (q + 1) * P)
                    nc.tensor.matmul(ps[:, TRB, q * P:(q + 1) * P], repq_r[:, par, :], qT[:, pair, cols],
                                     start=True, stop=False)
                    last = nc.tensor.matmul(ps[:, TRB, q * P:(q + 1) * P], m4[:, half * 4 + q, :], id_r[:],
                                            start=False, stop=True)
                last.then_inc(qb_mm, 1)

            def turn(g, qh):
                pe.wait_ge(o_out, g * NH + (qh + 1))
                for q in range(4):
                    last = nc.tensor.transpose(ps[:, TRB, q * P:(q + 1) * P], ot[:, qh, q * P:(q + 1) * P],
                                               chip.ident[:])
                last.then_inc(o_turned, 1)

            def values(g, par, s):
                pe.wait_ge(exp_done, g * (2 * STEPS) + 2 * (s + 1))
                if s == 0 and not is_first(g):
                    pe.wait_ge(o_out, g * NH)
                if s == NJ:
                    pe.wait_ge(o_out, g * NH + 1)
                if s == 0:
                    pe.wait_ge(vg_done, g + 1)
                for h in range(GQ):
                    last = nc.tensor.matmul(ps[h * QUAD:(h + 1) * QUAD, PVB, :], vg[par][:, s % NJ, :],
                                            probs[:, s % SLOTS, h, :], start=(s % NJ == 0),
                                            stop=(s % NJ == NJ - 1))
                last.then_inc(pv_mm, 1)

            for G in range(2):
                for half in range(NH):
                    if 2 * G + half:
                        pe.wait_ge(qa_done, 2 * G + half)
                    spread_q(0, G, half)
            pe.wait_ge(qa_done, 4)
            pe.wait_ge(zeroed, 3)
            for n in range(NMAX):
                if n == 0 or block_of(n)[0] > block_of(n - 1)[0]:
                    pe.wait_ge(kk_done, block_of(n)[0] + 1)
                if n >= 2:
                    pe.wait_ge(max_done, n - 1)
                max_block(0, n)
            for half in range(NH):
                pe.wait_ge(m_ready, half + 1)
                if half:
                    pe.wait_ge(qb_done, half)
                spread_q_max(0, 0, half)

            def body(g, par, pair1, pair2):
                nxt = 1 - par

                def some_max(step, lots):
                    for who, n in lots:
                        if who:
                            if n == 0:
                                pe.wait_ge(qa_done, g * 2 + 4)
                            if n < NMAX // 2 and (n == 0 or block_of(n)[0] > block_of(n - 1)[0]):
                                pe.wait_ge(kk_done, g * GQ + (GQ + block_of(n)[0] + 1))
                        pe.wait_ge(max_done, g * NMAX + (who * NMAX + n - 1))
                        max_block(nxt if who else par, n)

                for step in range(STEPS):
                    qh, kt = step // NJ, step % NJ
                    lots = blocks_at(g, step)
                    if step == 0:
                        pe.wait_ge(qb_done, g * 2 + 1)
                        pe.wait_ge(kk_done, g * GQ + GQ)
                    if step == NJ:
                        pe.wait_ge(qb_done, g * 2 + 2)
                    for pair in range(2):
                        if step or not is_first(g):
                            pe.wait_ge(exp_done, g * (2 * STEPS) + (2 * step + pair - 1))
                        for h in (2 * pair, 2 * pair + 1):
                            last = nc.tensor.matmul(ps[:, h, :], kk[par][:, h, kt * P:(kt + 1) * P],
                                                    qb[par][:, qh * HALF:(qh + 1) * HALF], start=True, stop=True)
                        last.then_inc(score_mm, 1)
                        if pair == 0:
                            some_max(step, lots[0:1])
                            if step >= 2:
                                values(g, par, step - 2)
                            elif not is_first(g):
                                values(g - 1, nxt, STEPS - 2 + step)
                            some_max(step, lots[1:2])
                        else:
                            some_max(step, lots[2:])
                    if step == 2 and not is_first(g):
                        pe.wait_ge(m_ready, g * 2 + 2)
                        pe.wait_ge(o_done, g * NH)
                        spread_q_max(pair_of(g, par, pair1), par, 1)
                    if step == 4 and not is_first(g):
                        pe.wait_ge(qb_done, g * 2 + 2)
                        turn(g - 1, 1)
                    if step == 6 and not is_last(g):
                        if is_first(g):
                            pe.wait_ge(qb_done, 2)
                        pe.wait_ge(o_done, g * NH + 1)
                        spread_q(pair2, par, 0)
                    if step == 7 and not is_last(g):
                        pe.wait_ge(qa_done, g * 2 + 5)
                        spread_q(pair2, par, 1)
                    if step == MID + 1 and not is_last(g):
                        pe.wait_ge(m_ready, g * 2 + 3)
                        pe.wait_ge(qa_done, g * 2 + 6)
                        spread_q_max(pair1, nxt, 0)
                    if step == MID + 3:
                        if not is_last(g):
                            pe.wait_ge(qb_done, g * 2 + 3)
                        else:
                            pe.wait_ge(o_done, g * NH + 1)
                        turn(g, 0)

            groups(pe, body)
            for s in (STEPS - 2, STEPS - 1):
                values(LASTG, LASTG % 2, s)
            pe.wait_ge(o_done, LASTG * NH + 2)
            turn(LASTG, 1)

        @block.scalar
        def _(act):
            def keep_q(dst, sem, done, value, half):
                act.wait_ge(sem, value)
                nc.scalar.activation(dst[:, half * HALF:(half + 1) * HALF], ps[:, TRB, :], ACT.Copy)\
                    .then_inc(done, 1)

            for G in range(2):
                for half in range(NH):
                    keep_q(qa[G], qa_mm, qa_done, 2 * G + half + 1, half)
            for half in range(NH):
                keep_q(qb[0], qb_mm, qb_done, half + 1, half)

            def values_out(g, qh):
                act.wait_ge(pv_mm, g * STEPS + (qh + 1) * NJ)
                if qh:
                    act.wait_ge(o_turned, g * NH + 1)
                elif not is_first(g):
                    act.wait_ge(o_turned, g * NH - 1)
                nc.scalar.activation(ot[:, qh, :], ps[:, PVB, :], ACT.Copy).then_inc(o_out, 1)

            def body(g, par, pair1, pair2):
                nxt = 1 - par
                for step in range(STEPS):
                    for pair in range(2):
                        act.wait_ge(score_mm, g * (2 * STEPS) + (2 * step + pair + 1))
                        if pair == 0 and (step >= SLOTS or not is_first(g)):
                            act.wait_ge(pv_mm, g * STEPS + (step - SLOTS + 1))
                        nc.scalar.activation(probs[:, step % SLOTS, 2 * pair:2 * pair + 2, :],
                                             ps[:, 2 * pair:2 * pair + 2, :], ACT.Exp, scale=SCALE)\
                            .then_inc(exp_done, 1)
                    if step == 1 and not is_first(g):
                        values_out(g - 1, 1)
                    if step == 3 and not is_first(g):
                        keep_q(qb[par], qb_mm, qb_done, g * 2 + 2, 1)
                    if step in (7, 8) and not is_last(g):
                        keep_q(qa[par], qa_mm, qa_done, g * 2 + (step - 7) + 5, step - 7)
                    if step == NJ + 1:
                        values_out(g, 0)
                    if step == MID + 2 and not is_last(g):
                        keep_q(qb[nxt], qb_mm, qb_done, g * 2 + 3, 0)

            groups(act, body)
            values_out(LASTG, 1)

        @block.vector
        def _(dve):
            order = Order(dve, order_sem)

            def find_max(base, n):
                h, j, half = block_of(n)
                dve.wait_ge(max_mm, base + (n + 1))
                nc.vector.tensor_reduce(mxp[:, j, h, half:half + 1], ps[:, MAXB + n % 2, :], AX.X, ALU.max)\
                    .then_inc(max_done, 1)

            def negate(base, qh, m4_used):
                js = slice(qh * (NJ // 2), (qh + 1) * (NJ // 2))
                dve.wait_ge(max_done, base + (qh + 1) * (NMAX // 2))
                if m4_used is not None:
                    dve.wait_ge(qb_mm, m4_used)
                order.link(nc.vector.tensor_reduce(nm[:, js], mxp[:, js], AX.X, ALU.max, negate=True))
                order.link(nc.vector.tensor_copy(m4q[:, js, :, M_HI], nm[:, js]))
                nc.vector.tensor_tensor(m4q[:, js, :, M_LO], nm[:, js], m4q[:, js, :, M_HI].bitcast(F32),
                                        ALU.subtract).then_inc(m_ready, 1)

            def outputs(g, qh):
                dve.wait_ge(o_turned, g * NH + (qh + 1))
                turned = ps[:, TRB, :].rearrange("p (q h r) -> p q h r", q=4, h=GQ)
                order.link(nc.vector.reciprocal(rinv[:], turned[:, :, :, DH]))
                cols = out[:, qh * 4:(qh + 1) * 4, bass.ds(g * (GQ * DH), GQ * DH)]
                nc.vector.tensor_tensor(cols.rearrange("p q (h d) -> p q h d", h=GQ), turned[:, :, :, 0:DH],
                                        rinv[:].unsqueeze(3).to_broadcast([P, 4, GQ, DH]), ALU.mult)\
                    .then_inc(o_done, 1)

            nc.vector.memset(m4[:].bitcast(mybir.dt.uint32), 0).then_inc(zeroed, 1)
            dve.wait_ge(zeroed, 3)
            for qh in range(2):
                for n in range(qh * (NMAX // 2), (qh + 1) * (NMAX // 2)):
                    find_max(0, n)
                negate(0, qh, None)
            nc.vector.memset(rinv[:], 0.0).then_inc(o_done, 1)
            dve.wait_ge(o_done, 1)
            base = order.done
            MARKS = 2 * 2 + 2

            def body(g, par, pair1, pair2):
                order.done = base if is_first(g) else g * MARKS + (base - 3)
                for step in range(STEPS):
                    for who, n in blocks_at(g, step):
                        find_max(g * NMAX + who * NMAX, n)
                    if step == 0 and not is_first(g):
                        negate(g * NMAX, 1, g * 2)
                    if step == 4 and not is_first(g):
                        outputs(g - 1, 1)
                    if step == MID and not is_last(g):
                        negate(g * NMAX + NMAX, 0, g * 2 + 2)
                    if step == MID + 3:
                        outputs(g, 0)

            groups(dve, body)
            outputs(LASTG, 1)

        @block.gpsimd
        def _(pool):
            nc.gpsimd.memset(kk[0][:].bitcast(mybir.dt.uint32), 0).then_inc(zeroed, 1)
            nc.gpsimd.memset(kk[1][:].bitcast(mybir.dt.uint32), 0).then_inc(zeroed, 1)
            pool.wait_ge(zeroed, 3)

            def keep_kv(G, slot):
                for h in range(GQ):
                    rows = slice(h * QUAD, (h + 1) * QUAD)
                    nc.gpsimd.tensor_copy(kk[slot][rows, h, :], krep[rows, G, :]).then_inc(kk_done, 1)

            keep_kv(0, 0)
            pool.wait_ge(kk_done, GQ)
            nc.gpsimd.tensor_copy(vg[0][:], vall[:, 0, :, :]).then_inc(vg_done, 1)

            def body(g, par, pair1, pair2):
                if not is_last(g):
                    if is_first(g):
                        pool.wait_ge(vg_done, 1)
                    else:
                        pool.wait_ge(score_mm, g * (2 * STEPS))
                        pool.wait_ge(vg_done, g + 1)
                        pool.wait_ge(zeroed, 3)
                    keep_kv(g + 1, 1 - par)
                    if not is_first(g):
                        pool.wait_ge(pv_mm, g * STEPS)
                    pool.wait_ge(kk_done, g * GQ + 2 * GQ)
                    pool.wait_ge(zeroed, 3)
                    nc.gpsimd.tensor_copy(vg[1 - par][:], vall[:, g + 1, :, :]).then_inc(vg_done, 1)

            groups(pool, body)


def attention0_output(nc, chip, wo, out):
    with ExitStack() as ctx:
        w_raw = chip.sb("ao_w", [P, NC, D], ctx=ctx)
        w_hi = chip.sb("ao_wh", [P, NC, D], F32R, ctx)
        w_lo = chip.sb("ao_wl", [P, NC, D], F32R, ctx)
        w_in, w_split, turned, hi_done, lo_done, mm, order_sem = (
            chip.sem("ao_" + s, ctx) for s in ("w", "ws", "turned", "hi", "lo", "mm", "ord"))
        block = ctx.enter_context(nc.Block())

        @block.sync
        def _(sp):
            sp.dma_start(w_raw[:], wo.rearrange("(k p) n -> p k n", p=P)).then_inc(w_in, 16)

        @block.vector
        def _(dve):
            order = Order(dve, order_sem)
            dve.wait_ge(w_in, 16)
            order.link(nc.vector.tensor_copy(w_hi[:], w_raw[:]))
            nc.vector.tensor_tensor(w_lo[:], w_raw[:], w_hi[:].bitcast(F32), ALU.subtract).then_inc(w_split, 1)
            for i in range(NH * NC):
                half, c = i // NC, i % NC
                cols = slice(half * HALF, (half + 1) * HALF)
                dve.wait_ge(hi_done, i + 1)
                nc.vector.tensor_tensor(chip.h_lo[:, c, cols], chip.ps[:, i, :], chip.h_hi[:, c, cols].bitcast(F32),
                                        ALU.subtract).then_inc(lo_done, 1)
            for i in range(NH * NC):
                half, c = i // NC, i % NC
                cols = slice(half * HALF, (half + 1) * HALF)
                dve.wait_ge(mm, i + 1)
                nc.vector.scalar_tensor_tensor(chip.xT[:, c, cols], chip.ps[:, 4 + i, :], mod_col(chip, 0, 2, c),
                                               chip.xT[:, c, cols], ALU.mult, ALU.add)

        @block.scalar
        def _(act):
            for i in range(NH * NC):
                half, c = i // NC, i % NC
                act.wait_ge(turned, i + 1)
                nc.scalar.activation(chip.h_hi[:, c, half * HALF:(half + 1) * HALF], chip.ps[:, i, :], ACT.Copy)\
                    .then_inc(hi_done, 1)

        @block.tensor
        def _(pe):
            for half in range(NH):
                for c in range(NC):
                    for q in range(4):
                        last = nc.tensor.transpose(chip.ps[:, half * NC + c, q * P:(q + 1) * P],
                                                   out[:, half * 4 + q, c * P:(c + 1) * P], chip.ident[:])
                    last.then_inc(turned, 1)
            pe.wait_ge(w_split, 1)
            for i in range(NH * NC):
                half, c = i // NC, i % NC
                cols = slice(half * HALF, (half + 1) * HALF)
                pe.wait_ge(lo_done, (half + 1) * NC)
                three_parts(chip.ps[:, 4 + i, :], nc,
                            lambda k: w_hi[:, k, c * P:(c + 1) * P], lambda k: w_lo[:, k, c * P:(c + 1) * P],
                            lambda k: chip.h_hi[:, k, cols], lambda k: chip.h_lo[:, k, cols],
                            range(NC)).then_inc(mm, 1)


def route(nc, chip, tag, gate_w, gate_b, tri, experts, n_groups, top_groups, top_k, scaling, extra, cwT):
    E, G, ES = experts, n_groups, experts // n_groups
    JG = NJ * G
    n = f"r{tag}_"
    with ExitStack() as ctx:
        w_raw = chip.sb(n + "w", [P, NC, E], ctx=ctx)
        w_hi = chip.sb(n + "wh", [P, NC, E], F32R, ctx)
        w_lo = chip.sb(n + "wl", [P, NC, E], F32R, ctx)
        bias = chip.sb(n + "b", [P, E], ctx=ctx)
        tri_t = chip.sb(n + "tri", [P, G, G], ctx=ctx)
        score = chip.sb(n + "s", [P, NJ, E], ctx=ctx)
        biased = chip.sb(n + "sb", [P, NJ, E], ctx=ctx)
        top = [[chip.sb(f"{n}t{lv}{i}", [P, JG, ES >> (lv + 1)], ctx=ctx) for i in range(4)]
               for lv in range(ES.bit_length() - 1)]
        gsum = chip.sb(n + "g", [P, NJ, G], ctx=ctx)
        cmp_a = chip.sb(n + "ca", [P, NJ, G, G], ctx=ctx)
        cmp_b = chip.sb(n + "cb", [P, NJ, G, G], ctx=ctx)
        gmask = chip.sb(n + "gm", [P, NJ, G], ctx=ctx)
        gfill = chip.sb(n + "gf", [P, NJ, G], ctx=ctx)
        masked = chip.sb(n + "m", [P, NJ, E], ctx=ctx)
        best = chip.sb(n + "v8", [P, NJ, 8], ctx=ctx)
        replaced = chip.sb(n + "rp", [P, NJ, E], ctx=ctx)
        wsum = chip.sb(n + "ws", [P, NJ], ctx=ctx)
        winv = chip.sb(n + "wi", [P, NJ], ctx=ctx)
        cw = chip.sb(n + "cw", [P, NJ, P], F32R, ctx)
        w_in, b_in, w_split, logit_mm, sig_done, cw_ready, turned, order_sem = (
            chip.sem(n + s, ctx) for s in ("w", "b", "ws", "lg", "sg", "cw", "tu", "ord"))
        block = ctx.enter_context(nc.Block())

        @block.sync
        def _(sp):
            sp.dma_start(w_raw[:], gate_w.rearrange("(k p) n -> p k n", p=P)).then_inc(w_in, 16)
            sp.dma_start(bias[:], gate_b.rearrange("(a e) -> a e", a=1).to_broadcast([P, E])).then_inc(b_in, 16)
            sp.dma_start(tri_t[:], tri[:, 0:G, 0:G]).then_inc(b_in, 16)

        @block.tensor
        def _(pe):
            pe.wait_ge(w_split, 1)
            for j in range(NJ):
                cols = slice(j * P, (j + 1) * P)
                last = three_parts(chip.ps[:, 0, j * E:(j + 1) * E], nc,
                                   lambda k: chip.h_hi[:, k, cols], lambda k: chip.h_lo[:, k, cols],
                                   lambda k: w_hi[:, k, :], lambda k: w_lo[:, k, :], range(NC))
            last.then_inc(logit_mm, 1)
            pe.wait_ge(cw_ready, 1)
            for j in range(NJ):
                last = nc.tensor.transpose(chip.ps[:, 1 + j // 4, (j % 4) * P:(j % 4 + 1) * P],
                                           cw[:, j, :].bitcast(F32), chip.ident[:])
                if j % 4 == 3:
                    last.then_inc(turned, 1)

        @block.scalar
        def _(act):
            act.wait_ge(logit_mm, 1)
            nc.scalar.activation(score[:], chip.ps[:, 0, 0:NJ * E].rearrange("p (j e) -> p j e", j=NJ), ACT.Sigmoid)\
                .then_inc(sig_done, 1)

        @block.vector
        def _(dve):
            order = Order(dve, order_sem)
            tt, ts = nc.vector.tensor_tensor, nc.vector.tensor_scalar
            dve.wait_ge(w_in, 16)
            order.link(nc.vector.tensor_copy(w_hi[:], w_raw[:]))
            tt(w_lo[:], w_raw[:], w_hi[:].bitcast(F32), ALU.subtract).then_inc(w_split, 1)
            order.mark(nc.vector.memset(cw[:].bitcast(mybir.dt.uint32), 0))
            dve.wait_ge(b_in, 32)
            dve.wait_ge(sig_done, 1)
            order.link(tt(biased[:], score[:], bias[:].unsqueeze(1).to_broadcast([P, NJ, E]), ALU.add))
            b = biased[:].rearrange("p j (g e) -> p (j g) e", g=G)
            a0, a1 = b[:, :, 0::2], b[:, :, 1::2]
            order.mark(tt(top[0][0][:], a0, a1, ALU.max))
            order.link(tt(top[0][1][:], a0, a1, ALU.min))
            for lv in range(1, len(top)):
                hi, lo = top[lv - 1][0], top[lv - 1][1]
                order.mark(tt(top[lv][2][:], hi[:, :, 0::2], hi[:, :, 1::2], ALU.min))
                order.mark(tt(top[lv][3][:], lo[:, :, 0::2], lo[:, :, 1::2], ALU.max))
                order.link(tt(top[lv][0][:], hi[:, :, 0::2], hi[:, :, 1::2], ALU.max))
                order.link(tt(top[lv][1][:], top[lv][2][:], top[lv][3][:], ALU.max))
            order.link(tt(gsum[:].rearrange("p j g -> p (j g)"), top[-1][0][:, :, 0], top[-1][1][:, :, 0], ALU.add))
            other = gsum[:].unsqueeze(2).to_broadcast([P, NJ, G, G])
            own = gsum[:].unsqueeze(3).to_broadcast([P, NJ, G, G])
            order.mark(tt(cmp_a[:], other, own, ALU.is_gt))
            order.link(tt(cmp_b[:], other, own, ALU.is_ge))
            order.link(tt(cmp_b[:], cmp_b[:], tri_t[:].unsqueeze(1).to_broadcast([P, NJ, G, G]), ALU.mult))
            order.link(tt(cmp_a[:], cmp_a[:], cmp_b[:], ALU.max))
            order.link(nc.vector.tensor_reduce(gmask[:], cmp_a[:], AX.X, ALU.add))
            order.link(ts(gmask[:], gmask[:], float(top_groups), None, ALU.is_lt))
            order.link(ts(gfill[:], gmask[:], BIG, -BIG, ALU.mult, ALU.add))
            m4 = masked[:].rearrange("p j (g e) -> p (j g) e", g=G)
            wide = [P, JG, ES]
            order.link(tt(m4, b, gmask[:].rearrange("p j g -> p (j g)").unsqueeze(2).to_broadcast(wide), ALU.mult))
            order.link(tt(m4, m4, gfill[:].rearrange("p j g -> p (j g)").unsqueeze(2).to_broadcast(wide), ALU.add))
            for j in range(NJ):
                order.mark(nc.vector.max(best[:, j, :], masked[:, j, :]))
            order.settle()
            order.link(nc.vector.memset(best[:, :, top_k:8], -BIG))
            for j in range(NJ):
                order.mark(nc.vector.match_replace(replaced[:, j, :], best[:, j, :], masked[:, j, :], -BIG))
            order.settle()
            order.link(tt(masked[:], masked[:], replaced[:], ALU.not_equal))
            order.link(tt(masked[:], masked[:], score[:], ALU.mult))
            order.link(nc.vector.tensor_reduce(wsum[:], masked[:], AX.X, ALU.add))
            order.link(ts(wsum[:], wsum[:], 1e-20, None, ALU.add))
            order.link(nc.vector.reciprocal(winv[:], wsum[:]))
            order.link(ts(winv[:], winv[:], scaling, None, ALU.mult))
            order.link(tt(masked[:], masked[:], winv[:].unsqueeze(2).to_broadcast([P, NJ, E]), ALU.mult))
            order.link(nc.vector.tensor_copy(cw[:, :, 0:E], masked[:]))
            if extra:
                order.mark(nc.vector.memset(cw[:, :, E:E + extra].bitcast(F32), 1.0))
            order.link(tt(cw[:, :, 64:64 + E], masked[:], cw[:, :, 0:E].bitcast(F32), ALU.subtract))
            nc.vector.tensor_copy(winv[:], wsum[:]).then_inc(cw_ready, 1)
            for half in range(NH):
                dve.wait_ge(turned, half + 1)
                nc.vector.tensor_copy(cwT[:, half * HALF:(half + 1) * HALF], chip.ps[:, 1 + half, :])


def experts(nc, chip, tag, weights, n_units, gated, n_plain, e2, layer, cwT):
    UPS = 2 if gated else 1
    WUP = UPS * NC * P
    WALL = WUP + D
    n = f"e{tag}_"
    with ExitStack() as ctx:
        raw = [chip.sb(f"{n}raw{i}", [P, WALL], ctx=ctx) for i in range(2)]
        w_hi = [chip.sb(f"{n}wh{i}", [P, WALL], F32R, ctx) for i in range(2)]
        w_lo = [chip.sb(f"{n}wl{i}", [P, WALL], F32R, ctx) for i in range(2)]
        pick = [chip.sb(f"{n}pk{i}", [P, P], F32R, ctx) for i in range(2)]
        e2_t = chip.sb(n + "e2", [P, 64], ctx=ctx)
        zero = chip.sb(n + "zero", [P, 1], ctx=ctx)
        a = chip.sb(n + "a", [P, 2, HALF], ctx=ctx)
        t = chip.sb(n + "t", [P, 2, HALF], ctx=ctx)
        hf = chip.sb(n + "hf", [P, 2, HALF], ctx=ctx)
        hh = chip.sb(n + "hh", [P, 2, HALF], F32R, ctx)
        hl = chip.sb(n + "hl", [P, 2, HALF], F32R, ctx)
        w_in = [chip.sem(f"{n}win{i}", ctx) for i in range(2)]
        e2_in, w_split, first_mm, up_mm, pick_mm, down_mm, a_done, t_done, hf_done, hh_done, hl_done, osem, psem = (
            chip.sem(n + s, ctx) for s in ("e2", "ws", "fm", "um", "bm", "dm", "a", "t", "hf", "hh", "hl", "o", "po"))
        LOOPS = (n_units - 2 - max(n_plain, 1)) // 2
        TAIL = range(2 * LOOPS + 2, n_units)
        block = ctx.enter_context(nc.Block())

        def units(eng, body):
            body(0, 0, False, False)
            body(1, 1, False, False)
            with eng.Fori(0, LOOPS) as i:
                for u in range(2):
                    body(i * 2 + (2 + u), u, False, False)
            for e in TAIL:
                body(e, e % 2, (not gated) and e >= n_units - n_plain, e == n_units - 1)

        def first(e):
            return isinstance(e, int) and e == 0

        @block.sync
        def _(sp):
            sp.dma_start(e2_t[:], e2).then_inc(e2_in, 16)

            def body(e, par, plain, last):
                if not (isinstance(e, int) and e < 2):
                    sp.wait_ge(w_split, e - 1)
                sp.dma_start(raw[par][:], weights[e]).then_inc(w_in[par], 16)

            units(sp, body)

        @block.gpsimd
        def _(pool):
            order = Order(pool, psem)
            order.link(nc.gpsimd.memset(zero[:], 0.0))
            pool.wait_ge(e2_in, 16)

            def body(e, par, plain, last):
                if not plain:
                    order.done = e * 2 + 1
                elif e == n_units - n_plain:
                    order.done = e * 2 + 1
                if not (isinstance(e, int) and e < 2):
                    pool.wait_ge(down_mm, e * 2 - 2)
                pool.wait_ge(w_in[par], (e - par) * 8 + 16)
                keep = lambda dst, src, shape: order.link(
                    nc.gpsimd.tensor_tensor(dst, src, zero[:].to_broadcast(shape) if len(shape) == 2 else
                                            zero[:].unsqueeze(2).to_broadcast(shape), ALU.add))
                keep(w_hi[par][:], raw[par][:], [P, WALL])
                if gated:
                    keep(pick[par][:], e2_t[:, bass.ds(e, 1)].to_broadcast([P, P]), [P, P])
                elif not plain:
                    keep(pick[par][:].rearrange("p (a b) -> p a b", a=2),
                         e2_t[:, bass.ds(e * 2, 2)].unsqueeze(2).to_broadcast([P, 2, 64]), [P, 2, 64])
                nc.gpsimd.tensor_tensor(w_lo[par][:], raw[par][:], w_hi[par][:].bitcast(F32), ALU.subtract)\
                    .then_inc(w_split, 1)
                pool.wait_ge(w_split, e + 1)

            units(pool, body)

        UPB = (4, 5) if gated else None
        PICKB = 6

        def up_bank(half):
            return UPB[1] if gated else 4 + half

        def pick_bank(half):
            return 6 if gated else 6 + half

        @block.tensor
        def _(pe):
            def up(e, par, half, plain):
                cols = slice(half * HALF, (half + 1) * HALF)
                u = e * 2 + half
                now = not first(e)
                for m in range(UPS):
                    bank = 4 if gated and m == 0 else up_bank(half)
                    if gated:
                        if now or half:
                            pe.wait_ge(a_done if m == 0 else t_done, u)
                    elif now:
                        pe.wait_ge(a_done, u - 1)
                    three_parts(chip.ps[:, bank, :], nc,
                                lambda k: w_hi[par][:, (m * NC + k) * P:(m * NC + k + 1) * P],
                                lambda k: w_lo[par][:, (m * NC + k) * P:(m * NC + k + 1) * P],
                                lambda k: chip.h_hi[:, k, cols], lambda k: chip.h_lo[:, k, cols],
                                range(NC)).then_inc(first_mm if m == 0 else up_mm, 1)
                if not plain:
                    if gated:
                        if now or half:
                            pe.wait_ge(hf_done, u)
                    elif now:
                        pe.wait_ge(t_done, u - 1)
                    nc.tensor.matmul(chip.ps[:, pick_bank(half), :], pick[par][:], cwT[:, cols],
                                     start=True, stop=True).then_inc(pick_mm, 1)

            def down(e, par, half, last):
                pe.wait_ge(hl_done, e * 2 + (half + 1))
                for c in range(NC):
                    for r, (w, h) in enumerate(((w_hi, hh), (w_hi, hl), (w_lo, hh))):
                        mm = nc.tensor.matmul(chip.ps[:, c * NH + half, :],
                                              w[par][:, WUP + c * P:WUP + (c + 1) * P], h[:, half, :],
                                              start=(first(e) and r == 0), stop=(last and r == 2),
                                              skip_group_check=True)
                mm.then_inc(down_mm, 1)

            def body(e, par, plain, last):
                pe.wait_ge(w_split, e + 1)
                up(e, par, 0, plain)
                if not first(e):
                    down(e - 1, 1 - par, 1, False)
                up(e, par, 1, plain)
                down(e, par, 0, last)

            units(pe, body)
            down(n_units - 1, (n_units - 1) % 2, 1, True)

        @block.scalar
        def _(act):
            def body(e, par, plain, last):
                for half in range(2):
                    u = e * 2 + half
                    bank = 4 if gated else 4 + half
                    act.wait_ge(first_mm, u + 1)
                    if not first(e):
                        act.wait_ge(t_done if gated else hf_done, u - 1)
                    nc.scalar.activation(a[:, half, :], chip.ps[:, bank, :], ACT.Silu if gated else ACT.Relu)\
                        .then_inc(a_done, 1)
                    act.wait_ge(hf_done, u + 1)
                    if not first(e):
                        act.wait_ge(down_mm, u - 1)
                    nc.scalar.activation(hh[:, half, :], hf[:, half, :], ACT.Copy).then_inc(hh_done, 1)

            units(act, body)

        @block.vector
        def _(dve):
            def body(e, par, plain, last):
                for half in range(2):
                    u = e * 2 + half
                    dve.wait_ge(a_done, u + 1)
                    if not first(e):
                        dve.wait_ge(hl_done, u - 1)
                    if gated:
                        dve.wait_ge(up_mm, u + 1)
                        nc.vector.tensor_tensor(t[:, half, :], a[:, half, :], chip.ps[:, 5, :], ALU.mult)\
                            .then_inc(t_done, 1)
                        dve.wait_ge(pick_mm, u + 1)
                        dve.wait_ge(t_done, u + 1)
                        nc.vector.tensor_tensor(hf[:, half, :], t[:, half, :], chip.ps[:, 6, :], ALU.mult)\
                            .then_inc(hf_done, 1)
                    elif plain:
                        nc.vector.tensor_tensor(hf[:, half, :], a[:, half, :], a[:, half, :], ALU.mult)\
                            .then_inc(hf_done, 1)
                    else:
                        dve.wait_ge(pick_mm, u + 1)
                        nc.vector.tensor_tensor(t[:, half, :], a[:, half, :], chip.ps[:, 6 + half, :], ALU.mult)\
                            .then_inc(t_done, 1)
                        dve.wait_ge(t_done, u + 1)
                        nc.vector.tensor_tensor(hf[:, half, :], t[:, half, :], a[:, half, :], ALU.mult)\
                            .then_inc(hf_done, 1)
                    dve.wait_ge(hh_done, u + 1)
                    if not first(e):
                        dve.wait_ge(down_mm, u - 1)
                    nc.vector.tensor_tensor(hl[:, half, :], hf[:, half, :], hh[:, half, :].bitcast(F32), ALU.subtract)\
                        .then_inc(hl_done, 1)

            units(dve, body)
            for half in range(NH):
                dve.wait_ge(down_mm, 2 * n_units - 1 + half)
                for c in range(NC):
                    cols = slice(half * HALF, (half + 1) * HALF)
                    nc.vector.scalar_tensor_tensor(chip.xT[:, c, cols], chip.ps[:, c * NH + half, :],
                                                   mod_col(chip, layer, 5, c), chip.xT[:, c, cols], ALU.mult, ALU.add)


def attention1(nc, chip, wq, bq, wk, bk, wv, bv, wo, bo):
    ps = chip.ps
    SCALE = float(D) ** -0.5
    KINDS = 4
    PROJ = NC * NH
    S_BANK, T_BANK, O_BANK = 0, 4, 6
    with ExitStack() as ctx:
        w_raw = chip.sb("b_wraw", [P, KINDS, NC, D], BF16, ctx)
        b_raw = chip.sb("b_braw", [P, KINDS, NC], BF16, ctx)
        w = chip.sb("b_w", [P, KINDS, NC, D], F32R, ctx)
        b = chip.sb("b_b", [P, KINDS, NC], ctx=ctx)
        qk_hi = chip.sb("b_qkh", [P, 2, NC, T], F32R, ctx)
        qk_lo = chip.sb("b_qkl", [P, 2, NC, T], F32R, ctx)
        v_hi = chip.sb("b_vh", [P, NJ, D], F32R, ctx)
        v_lo = chip.sb("b_vl", [P, NJ, D], F32R, ctx)
        mx = chip.sb("b_mx", [P, 2], ctx=ctx)
        nm = chip.sb("b_nm", [P, 2], ctx=ctx)
        rs = chip.sb("b_rs", [P, 2], ctx=ctx)
        ri = chip.sb("b_ri", [P, 2], ctx=ctx)
        pe_x = chip.sb("b_p", [P, 2, T], ctx=ctx)
        pt_hi = chip.sb("b_pth", [P, NJ, HALF], F32R, ctx)
        pt_lo = chip.sb("b_ptl", [P, NJ, HALF], F32R, ctx)
        a_hi = chip.sb("b_ah", [P, NC, T], F32R, ctx)
        a_lo = chip.sb("b_al", [P, NC, T], F32R, ctx)
        names = ("win", "bin", "wok", "pj", "pjh", "pjl", "vm", "vh", "vl", "sm", "mx", "ex", "nr", "tm", "th",
                 "tl", "om", "oh", "ol", "fm", "fh", "fl", "ord")
        (w_in, b_in, w_ready, pj_mm, pj_hi, pj_lo, v_mm, v_his, v_los, s_mm, s_max, s_exp, s_norm, t_mm, t_hi,
         t_lo, o_mm, o_hi, o_lo, f_mm, f_hi, f_lo, osem) = (chip.sem("b_" + s, ctx) for s in names)
        block = ctx.enter_context(nc.Block())

        def halfcols(half):
            return slice(half * HALF, (half + 1) * HALF)

        @block.sync
        def _(sp):
            def loads(i):
                for n, m in enumerate((wq, wk, wv, wo)):
                    sp.dma_start(w_raw[:, n], m[i].rearrange("(k p) n -> p k n", p=P)).then_inc(w_in, 16)
                for n, m in enumerate((bq, bk, bv, bo)):
                    sp.dma_start(b_raw[:, n], m[i]).then_inc(b_in, 16)

            loads(0)
            with sp.Fori(1, LAYERS) as i:
                sp.wait_ge(w_ready, i)
                loads(i)

        QK = [(m, c, half) for m in range(2) for c in range(NC) for half in range(NH)]

        def two_parts(out, lhs, rhs):
            n = len(lhs)
            for i in range(n):
                last = nc.tensor.matmul(out, lhs[i], rhs[i], start=(i == 0), stop=(i == n - 1))
            return last

        @block.tensor
        def _(pe):
            def layer(i):
                pe.wait_ge(w_ready, i + 1)
                pe.wait_ge(f_lo, i * PROJ + 1)
                for n, (m, c, half) in enumerate(QK):
                    if n >= 4:
                        pe.wait_ge(pj_lo, i * len(QK) + (n - 3))
                    wc = [w[:, m, k, c * P:(c + 1) * P] for k in range(NC)]
                    two_parts(ps[:, n % 4, :], [wc[0], wc[0], wc[1], wc[1]],
                              [x[:, k, halfcols(half)] for k in range(NC) for x in (chip.h_hi, chip.h_lo)])\
                        .then_inc(pj_mm, 1)
                for jj in range(NJ // 2):
                    for j in (2 * jj, 2 * jj + 1):
                        rows = slice(j * P, (j + 1) * P)
                        last = two_parts(ps[:, 4 + jj, (j % 2) * D:(j % 2 + 1) * D],
                                         [x[:, k, rows] for k in range(NC) for x in (chip.h_hi, chip.h_lo)],
                                         [w[:, 2, 0, :], w[:, 2, 0, :], w[:, 2, 1, :], w[:, 2, 1, :]])
                    last.then_inc(v_mm, 1)

                def scores(j):
                    if j == 0:
                        pe.wait_ge(pj_lo, i * len(QK) + len(QK))
                    if j >= 2:
                        pe.wait_ge(s_exp, i * NJ + (j - 1))
                    rows = slice(j * P, (j + 1) * P)
                    for half in range(NH):
                        last = three_parts(ps[:, S_BANK + (j % 2) * 2 + half, :], nc,
                                           lambda k: qk_hi[:, 0, k, rows], lambda k: qk_lo[:, 0, k, rows],
                                           lambda k: qk_hi[:, 1, k, halfcols(half)],
                                           lambda k: qk_lo[:, 1, k, halfcols(half)], range(NC))
                    last.then_inc(s_mm, 1)

                def turn(j):
                    pe.wait_ge(s_norm, i * NJ + (j + 1))
                    if j == 0:
                        pe.wait_ge(v_los, i * (NJ // 2) + NJ // 2)
                    else:
                        pe.wait_ge(t_lo, i * NJ + j)
                    for kt in range(NJ):
                        last = nc.tensor.transpose(ps[:, T_BANK + kt // 4, (kt % 4) * P:(kt % 4 + 1) * P],
                                                   pe_x[:, j % 2, kt * P:(kt + 1) * P], chip.ident[:])
                    last.then_inc(t_mm, 1)

                def values(qh):
                    pe.wait_ge(t_lo, i * NJ + 4 * (qh + 1))
                    if qh:
                        pe.wait_ge(o_lo, i * PROJ + NC)
                    for c in range(NC):
                        cc = slice(c * P, (c + 1) * P)
                        three_parts(ps[:, O_BANK + c, :], nc,
                                    lambda k: v_hi[:, k, cc], lambda k: v_lo[:, k, cc],
                                    lambda k: pt_hi[:, k, :], lambda k: pt_lo[:, k, :], range(NJ))\
                            .then_inc(o_mm, 1)

                scores(0)
                for j in range(1, NJ):
                    scores(j)
                    turn(j - 1)
                    if j == 5:
                        values(0)
                turn(NJ - 1)
                values(1)
                for half in range(NH):
                    pe.wait_ge(o_lo, i * PROJ + NC * (half + 1))
                    for c in range(NC):
                        wc = [w[:, 3, k, c * P:(c + 1) * P] for k in range(NC)]
                        two_parts(ps[:, half * NC + c, :], [wc[0], wc[0], wc[1], wc[1]],
                                  [x[:, k, halfcols(half)] for k in range(NC) for x in (a_hi, a_lo)])\
                            .then_inc(f_mm, 1)

            with pe.Fori(0, LAYERS) as i:
                layer(i)

        @block.scalar
        def _(act):
            def layer(i):
                for n, (m, c, half) in enumerate(QK):
                    act.wait_ge(pj_mm, i * len(QK) + (n + 1))
                    nc.scalar.activation(qk_hi[:, m, c, halfcols(half)], ps[:, n % 4, :], ACT.Identity,
                                         bias=b[:, m, c:c + 1]).then_inc(pj_hi, 1)
                for jj in range(NJ // 2):
                    act.wait_ge(v_mm, i * (NJ // 2) + (jj + 1))
                    nc.scalar.activation(v_hi[:, 2 * jj:2 * jj + 2, :],
                                         ps[:, 4 + jj, :].rearrange("p (j d) -> p j d", j=2), ACT.Copy)\
                        .then_inc(v_his, 1)

                def exps(j):
                    act.wait_ge(s_max, i * NJ + (j + 1))
                    if j >= 2:
                        act.wait_ge(t_mm, i * NJ + (j - 1))
                    nc.scalar.activation(pe_x[:, j % 2, :], ps[:, S_BANK + (j % 2) * 2:S_BANK + (j % 2) * 2 + 2, :],
                                         ACT.Exp, bias=nm[:, j % 2:j % 2 + 1], scale=SCALE,
                                         accum_out=rs[:, j % 2:j % 2 + 1]).then_inc(s_exp, 1)

                def keep_turned(j):
                    act.wait_ge(t_mm, i * NJ + (j + 1))
                    if j == 4:
                        act.wait_ge(o_mm, i * PROJ + NC)
                    nc.scalar.activation(pt_hi[:, :, (j % 4) * P:(j % 4 + 1) * P],
                                         ps[:, T_BANK:T_BANK + 2, :].rearrange("p b (k q) -> p (b k) q", q=P),
                                         ACT.Copy).then_inc(t_hi, 1)

                def keep_values(qh):
                    for c in range(NC):
                        act.wait_ge(o_mm, i * PROJ + (qh * NC + c + 1))
                        nc.scalar.activation(a_hi[:, c, halfcols(qh)], ps[:, O_BANK + c, :], ACT.Identity,
                                             bias=b[:, 2, c:c + 1]).then_inc(o_hi, 1)

                exps(0)
                for j in range(1, NJ):
                    exps(j)
                    keep_turned(j - 1)
                    if j == 5:
                        keep_values(0)
                keep_turned(NJ - 1)
                keep_values(1)
                for n in range(PROJ):
                    half, c = n // NC, n % NC
                    act.wait_ge(f_mm, i * PROJ + (n + 1))
                    nc.scalar.activation(chip.h_hi[:, c, halfcols(half)], ps[:, n, :], ACT.Identity,
                                         bias=b[:, 3, c:c + 1]).then_inc(f_hi, 1)

            with act.Fori(0, LAYERS) as i:
                layer(i)

        @block.vector
        def _(dve):
            order = Order(dve, osem)
            MARKS = 1 + 2 * NJ

            def low(dst, psum, bias, hi, sem):
                nc.vector.scalar_tensor_tensor(dst, psum, bias, hi.bitcast(F32), ALU.add, ALU.subtract)\
                    .then_inc(sem, 1)

            def layer(i):
                order.done = i * MARKS
                dve.wait_ge(w_in, i * (16 * KINDS) + 16 * KINDS)
                dve.wait_ge(b_in, i * (16 * KINDS) + 16 * KINDS)
                dve.wait_ge(f_lo, i * PROJ + 1)
                order.link(nc.vector.tensor_copy(b[:], b_raw[:]))
                nc.vector.tensor_copy(w[:], w_raw[:]).then_inc(w_ready, 1)
                for n, (m, c, half) in enumerate(QK):
                    dve.wait_ge(pj_hi, i * len(QK) + (n + 1))
                    low(qk_lo[:, m, c, halfcols(half)], ps[:, n % 4, :], b[:, m, c:c + 1],
                        qk_hi[:, m, c, halfcols(half)], pj_lo)
                for jj in range(NJ // 2):
                    dve.wait_ge(v_his, i * (NJ // 2) + (jj + 1))
                    nc.vector.tensor_tensor(v_lo[:, 2 * jj:2 * jj + 2, :],
                                            ps[:, 4 + jj, :].rearrange("p (j d) -> p j d", j=2),
                                            v_hi[:, 2 * jj:2 * jj + 2, :].bitcast(F32), ALU.subtract)\
                        .then_inc(v_los, 1)

                def maxima(j):
                    dve.wait_ge(s_mm, i * NJ + (j + 1))
                    order.link(nc.vector.tensor_reduce(mx[:, j % 2:j % 2 + 1],
                                                       ps[:, S_BANK + (j % 2) * 2:S_BANK + (j % 2) * 2 + 2, :],
                                                       AX.XY, ALU.max, negate=True))
                    nc.vector.tensor_scalar(nm[:, j % 2:j % 2 + 1], mx[:, j % 2:j % 2 + 1], SCALE, None, ALU.mult)\
                        .then_inc(s_max, 1)

                def normalise(j):
                    dve.wait_ge(s_exp, i * NJ + (j + 1))
                    order.link(nc.vector.reciprocal(ri[:, j % 2:j % 2 + 1], rs[:, j % 2:j % 2 + 1]))
                    nc.vector.tensor_scalar(pe_x[:, j % 2, :], pe_x[:, j % 2, :], ri[:, j % 2:j % 2 + 1], None,
                                            ALU.mult).then_inc(s_norm, 1)

                def low_turned(j):
                    dve.wait_ge(t_hi, i * NJ + (j + 1))
                    cols = slice((j % 4) * P, (j % 4 + 1) * P)
                    nc.vector.tensor_tensor(pt_lo[:, :, cols],
                                            ps[:, T_BANK:T_BANK + 2, :].rearrange("p b (k q) -> p (b k) q", q=P),
                                            pt_hi[:, :, cols].bitcast(F32), ALU.subtract).then_inc(t_lo, 1)

                def low_values(qh):
                    for c in range(NC):
                        dve.wait_ge(o_hi, i * PROJ + (qh * NC + c + 1))
                        low(a_lo[:, c, halfcols(qh)], ps[:, O_BANK + c, :], b[:, 2, c:c + 1],
                            a_hi[:, c, halfcols(qh)], o_lo)

                maxima(0)
                for j in range(1, NJ):
                    maxima(j)
                    normalise(j - 1)
                    low_turned(j - 1)
                    if j == 5:
                        low_values(0)
                normalise(NJ - 1)
                low_turned(NJ - 1)
                low_values(1)
                for n in range(PROJ):
                    half, c = n // NC, n % NC
                    dve.wait_ge(f_hi, i * PROJ + (n + 1))
                    low(chip.h_lo[:, c, halfcols(half)], ps[:, n, :], b[:, 3, c:c + 1],
                        chip.h_hi[:, c, halfcols(half)], f_lo)

            nc.vector.memset(mx[:], 0.0).then_inc(f_lo, 1)
            with dve.Fori(0, LAYERS) as i:
                layer(i)
            order.done = LAYERS * MARKS
            dve.wait_ge(f_lo, LAYERS * PROJ + 1)
            for part in (chip.h_hi, chip.h_lo):
                for c in range(NC):
                    order.mark(nc.vector.scalar_tensor_tensor(chip.xT[:, c, :], part[:, c, :].bitcast(F32),
                                                              mod_col(chip, 1, 2, c), chip.xT[:, c, :],
                                                              ALU.mult, ALU.add))
                order.settle()


def store(nc, chip, out):
    with ExitStack() as ctx:
        o = chip.sb("s_o", [P, NJ, D], ctx=ctx)
        turned, kept, stored = (chip.sem("s_" + s, ctx) for s in ("turned", "kept", "stored"))
        block = ctx.enter_context(nc.Block())
        dst = out.rearrange("a (j p) d -> p (a j) d", p=P)

        @block.tensor
        def _(pe):
            for j in range(NJ):
                for c in range(NC):
                    last = nc.tensor.transpose(chip.ps[:, j // 2, (j % 2) * D + c * P:(j % 2) * D + (c + 1) * P],
                                               chip.xT[:, c, j * P:(j + 1) * P], chip.ident[:])
                if j % 2:
                    last.then_inc(turned, 1)

        @block.vector
        def _(dve):
            for b in range(NJ // 2):
                dve.wait_ge(turned, b + 1)
                nc.vector.tensor_copy(o[:, 2 * b:2 * b + 2, :],
                                      chip.ps[:, b, :].rearrange("p (j d) -> p j d", j=2)).then_inc(kept, 1)

        @block.sync
        def _(sp):
            for b in range(2):
                sp.wait_ge(kept, 2 * b + 2)
                sp.dma_start(dst[:, 4 * b:4 * b + 4, :], o[:, 4 * b:4 * b + 4, :]).then_inc(stored, 16)
            sp.wait_ge(stored, 32)


def two_adaln_layers_kernel(nc: bass.Bass, x, c0, wmod0, wq0, wk0, wv0, wo0, router0, router_bias0, experts0,
                            c1, wmod1, wq1, bq1, wk1, bk1, wv1, bv1, wo1, bo1, router1, router_bias1, experts1,
                            ident, rep_q, rep_k, lanes, e2, tri, out):
    with ExitStack() as ctx:
        chip = Chip(nc, ctx)
        first_load(nc, chip, x, ident)
        modulation(nc, chip, 0, c0, wmod0)
        norm(nc, chip, "0a", 0, 0, 1)
        attention0(nc, chip, wq0, wk0, wv0, wo0, rep_q, rep_k, lanes)
        norm(nc, chip, "0b", 0, 3, 4)
        with ExitStack() as stage:
            cwT = chip.sb("cwT0", [P, T], F32R, stage)
            route(nc, chip, "0", router0, router_bias0, tri, E0, G0, TOPG0, K0, SCALE0, 1, cwT)
            experts(nc, chip, "0", experts0, experts0.shape[0], True, 0, e2, 0, cwT)
        modulation(nc, chip, 1, c1, wmod1)
        norm(nc, chip, "1a", 1, 0, 1)
        attention1(nc, chip, wq1, bq1, wk1, bk1, wv1, bv1, wo1, bo1)
        norm(nc, chip, "1b", 1, 3, 4)
        with ExitStack() as stage:
            cwT = chip.sb("cwT1", [P, T], F32R, stage)
            route(nc, chip, "1", router1, router_bias1, tri, E1, G1, TOPG1, K1, SCALE1, 0, cwT)
            experts(nc, chip, "1", experts1, experts1.shape[0], False, experts1.shape[0] - E1 // 2, e2, 1, cwT)
        store(nc, chip, out)


def shape_constants():
    c = {"ident": np.eye(P, dtype=np.float32)}
    rep_q = np.zeros((P, 2, P), np.float32)
    rep_k = np.zeros((P, KV_HEADS, P), np.float32)
    for h in range(GQ):
        for d in range(DH):
            for r, (q_lo, k_lo) in enumerate(((0, 0), (0, 1), (1, 0))):
                col = h * QUAD + r * DH + d
                for b in range(2):
                    rep_q[64 * q_lo + b * GQ * DH + h * DH + d, b, col] = 1
                for g in range(KV_HEADS):
                    rep_k[64 * k_lo + g * DH + d, g, col] = 1
    lanes = np.zeros((P, 2), np.float32)
    lanes[64:, 0] = -1
    for h in range(GQ):
        lanes[[h * QUAD + M_HI, h * QUAD + M_LO], 1] = 1
    e2 = (np.arange(P)[:, None] % 64 == np.arange(64)[None, :]).astype(np.float32)
    tri = np.broadcast_to(np.tril(np.ones((8, 8), np.float32), -1), (P, 8, 8)).copy()
    return c | {"rep_q": rep_q, "rep_k": rep_k, "lanes": lanes, "e2": e2, "tri": tri}


def gated_weights(gate, up, down, s_gate, s_up, s_down):
    def first(a, s):
        a = np.concatenate([a, s[None]])
        return a.transpose(0, 2, 1).reshape(len(a), NC, P, P).transpose(0, 2, 1, 3).reshape(len(a), P, NC * P)
    last = np.concatenate([down, s_down[None]]).transpose(0, 2, 1)
    return np.ascontiguousarray(np.concatenate([first(gate, s_gate), first(up, s_up), last], axis=2))


def squared_weights(w1, w2, s_up, s_down):
    i = w1.shape[1]
    up = np.concatenate([w1, s_up.reshape(-1, i, D)]).reshape(-1, P, D)
    up = up.transpose(0, 2, 1).reshape(len(up), NC, P, P).transpose(0, 2, 1, 3).reshape(len(up), P, NC * P)
    down = np.concatenate([w2.transpose(0, 2, 1), s_down.T.reshape(-1, i, D)]).reshape(-1, P, D)
    return np.ascontiguousarray(np.concatenate([up, down], axis=2))


def kernel(**inputs):
    import concourse.bacc as bacc
    from concourse.bass_utils import run_bass_kernel_spmd

    a = {k: np.asarray(v) for k, v in inputs.items()}
    cols = lambda v: v.reshape(NC, P).T
    bias = lambda v: v.reshape(LAYERS, NC, P).transpose(0, 2, 1)
    args = {
        "x": a["L0_attn_X"], "c0": cols(a["L0_c"]), "wmod0": a["L0_wmod"],
        "wq0": a["L0_attn_Wq"], "wk0": a["L0_attn_Wk"], "wv0": a["L0_attn_Wv"], "wo0": a["L0_attn_Wo"],
        "router0": a["L0_ffn_gate_weight"].T, "router_bias0": a["L0_ffn_expert_bias"],
        "experts0": gated_weights(a["L0_ffn_gate_proj"], a["L0_ffn_up_proj"], a["L0_ffn_down_proj"],
                                  a["L0_ffn_shared_gate"], a["L0_ffn_shared_up"], a["L0_ffn_shared_down"]),
        "c1": cols(a["L1_c"]), "wmod1": a["L1_wmod"],
        "wq1": a["L1_attn_Wq"], "bq1": bias(a["L1_attn_bq"]), "wk1": a["L1_attn_Wk"], "bk1": bias(a["L1_attn_bk"]),
        "wv1": a["L1_attn_Wv"], "bv1": bias(a["L1_attn_bv"]), "wo1": a["L1_attn_Wo"], "bo1": bias(a["L1_attn_bo"]),
        "router1": a["L1_ffn_gate_w"].T, "router_bias1": a["L1_ffn_gate_bias"],
        "experts1": squared_weights(a["L1_ffn_w1"], a["L1_ffn_w2"], a["L1_ffn_shared_up"], a["L1_ffn_shared_down"]),
    } | shape_constants()
    nc = bacc.Bacc("TRN2", target_bir_lowering=False, num_devices=1)
    arrays, aps = {}, {}
    for name, v in args.items():
        arrays[f"in_{name}"] = v = np.ascontiguousarray(v)
        aps[name] = nc.dram_tensor(f"in_{name}", v.shape, mybir.dt.from_np(v.dtype), kind="ExternalInput").ap()
    aps["out"] = nc.dram_tensor("out_x", (1, T, D), F32, kind="ExternalOutput").ap()
    two_adaln_layers_kernel(nc, **aps)
    r = run_bass_kernel_spmd(nc, [arrays], core_ids=[0])
    return r.results[0]["out_x"]
```

```python
import concourse.bass as bass
from concourse import mybir
from concourse.alu_op_type import AluOpType as ALU
from contextlib import ExitStack
import numpy as np

F32 = mybir.dt.float32
F32R = mybir.dt.float32r
BF16 = mybir.dt.bfloat16
ACT = mybir.ActivationFunctionType
AX = mybir.AxisListType

P = 128
T = 1024
D = 256
NJ = T // P
NC = D // P
HALF = 512
NH = T // HALF
BANKS = 8
EPS = 1e-5

HEADS, KV_HEADS, DH = 32, 8, 8
GQ = HEADS // KV_HEADS
QUAD = 32
M_HI, M_LO = 3 * DH, 3 * DH + 1
VCOLS = DH + 1
BIG = 3.0e38

E0, G0, TOPG0, K0, SCALE0 = 16, 4, 2, 4, 2.5
E1, G1, TOPG1, K1, SCALE1 = 64, 8, 4, 6, 2.5
LAYERS = 4


class Order:

    def __init__(self, eng, sem):
        self.eng, self.sem, self.done, self.peak = eng, sem, 0, 0

    def mark(self, ins):
        ins.then_inc(self.sem, 1)
        self.done = self.done + 1
        return ins

    def settle(self):
        self.eng.wait_ge(self.sem, self.done)

    def link(self, ins):
        self.mark(ins)
        self.settle()


class Chip:

    def __init__(self, nc, ctx):
        self.nc, self.ctx = nc, ctx
        self.ps = ctx.enter_context(nc.psum_tensor("ps", [P, BANKS, HALF], F32))
        self.xT = self.sb("xT", [P, NC, T])
        self.h_hi = self.sb("h_hi", [P, NC, T], F32R)
        self.h_lo = self.sb("h_lo", [P, NC, T], F32R)
        self.ident = self.sb("ident", [P, P])
        self.mods = [self.sb(f"mod{i}", [P, 12]) for i in range(2)]
        self.norm_sems = [self.sem("ln_" + s) for s in ("tok", "var", "sd", "rstd", "xna", "xnd", "back", "hi", "ord")]
        self.norms = 0

    def sb(self, name, shape, dt=F32, ctx=None):
        return (ctx or self.ctx).enter_context(self.nc.sbuf_tensor(name, shape, dt))

    def sem(self, name, ctx=None):
        return self.ctx.enter_context(self.nc.semaphore(name))


def mod_col(chip, layer, which, c):
    return chip.mods[layer][:, which * NC + c:which * NC + c + 1]


class Modulation:

    def __init__(self, nc, chip, ctx, layer, c_cols, wmod):
        n = f"mo{layer}_"
        self.nc, self.chip, self.mod, self.c_cols, self.wmod = nc, chip, chip.mods[layer], c_cols, wmod
        self.w = chip.sb(n + "w", [P, NC, 6 * D], ctx=ctx)
        self.c_in = chip.sb(n + "c", [P, NC], ctx=ctx)
        self.c_act = chip.sb(n + "ca", [P, NC], ctx=ctx)
        self.tmp = chip.sb(n + "t", [P, 3, 2, NC], ctx=ctx)
        self.w_in, self.c_done, self.act_done, self.mm_done, self.ready, self.order_sem = (
            chip.sem(n + s) for s in ("w_in", "c_in", "act", "mm", "ready", "ord"))

    def load(self, sp):
        sp.dma_start(self.c_in[:], self.c_cols).then_inc(self.c_done, 16)
        sp.dma_start(self.w[:], self.wmod.rearrange("(k p) n -> p k n", p=P)).then_inc(self.w_in, 16)

    def activate(self, act):
        act.wait_ge(self.c_done, 16)
        self.nc.scalar.activation(self.c_act[:], self.c_in[:], ACT.Silu).then_inc(self.act_done, 1)

    def products(self, pe, bank):
        pe.wait_ge(self.act_done, 1)
        pe.wait_ge(self.w_in, 16)
        for m in range(6 * NC):
            for k in range(NC):
                last = self.nc.tensor.matmul(self.chip.ps[:, bank, m:m + 1], self.w[:, k, m * P:(m + 1) * P],
                                             self.c_act[:, k:k + 1], start=(k == 0), stop=(k == NC - 1))
        last.then_inc(self.mm_done, 1)

    def columns(self, dve, bank):
        nc, tmp = self.nc, self.tmp
        order = Order(dve, self.order_sem)
        dve.wait_ge(self.mm_done, 1)
        order.link(nc.vector.tensor_copy(self.mod[:], self.chip.ps[:, bank, 0:6 * NC]))
        by_kind = self.mod[:].rearrange("p (w c) -> p w c", c=NC)
        scales, gates = by_kind[:, 1::3, :], by_kind[:, 2::3, :]
        sign, size, minus = (tmp[:, i] for i in range(3))
        order.mark(nc.vector.tensor_scalar(scales, scales, 1.0, None, ALU.add))
        order.mark(nc.vector.tensor_scalar(sign, gates, 0.0, None, ALU.is_ge))
        order.link(nc.vector.tensor_scalar(minus, gates, -1.0, None, ALU.mult))
        order.mark(nc.vector.tensor_scalar(sign, sign, 2.0, -1.0, ALU.mult, ALU.add))
        order.link(nc.vector.tensor_tensor(size, gates, minus, ALU.max))
        order.link(nc.vector.tensor_scalar(size, size, 0.25, None, ALU.max))
        nc.vector.tensor_tensor(gates, sign, size, ALU.mult).then_inc(self.ready, 1)
        dve.wait_ge(self.ready, 1)


def first_load(nc, chip, x, ident, others):
    with ExitStack() as ctx:
        xt = chip.sb("x_tok", [P, NJ, D], ctx=ctx)
        x_in = [chip.sem(f"fl_x{i}") for i in range(NH)]
        id_in, turned = (chip.sem("fl_" + s) for s in ("id", "turned"))
        block = ctx.enter_context(nc.Block())
        xv = x.rearrange("a (j p) d -> p (a j) d", p=P)

        @block.sync
        def _(sp):
            sp.dma_start(chip.ident[:], ident).then_inc(id_in, 16)
            for half in range(NH):
                sp.dma_start(xt[:, half * 4:(half + 1) * 4, :], xv[:, half * 4:(half + 1) * 4, :])\
                    .then_inc(x_in[half], 16)
            for weights in others:
                weights.load(sp)

        @block.tensor
        def _(pe):
            pe.wait_ge(id_in, 16)
            for half in range(NH):
                pe.wait_ge(x_in[half], 16)
                for c in range(NC):
                    for q in range(4):
                        last = nc.tensor.transpose(chip.ps[:, half * NC + c, q * P:(q + 1) * P],
                                                   xt[:, half * 4 + q, c * P:(c + 1) * P], chip.ident[:])
                    last.then_inc(turned, 1)

        @block.vector
        def _(dve):
            for half in range(NH):
                for c in range(NC):
                    dve.wait_ge(turned, half * NC + c + 1)
                    nc.vector.tensor_copy(chip.xT[:, c, half * HALF:(half + 1) * HALF],
                                          chip.ps[:, half * NC + c, :])


def norm(nc, chip, tag, layer, shift, scale, beside, mod=None):
    n = f"ln{tag}_"
    with ExitStack() as ctx:
        xn = chip.sb(n + "xn", [P, NJ, D], ctx=ctx)
        hf = chip.sb(n + "hf", [P, 2, HALF], ctx=ctx)
        st = chip.sb(n + "st", [P, NJ, 6], ctx=ctx)
        mv = chip.sb(n + "mv", [P, NJ, 2], ctx=ctx)
        var, sd, r0, r1 = (chip.sb(n + s, [P, NJ], ctx=ctx) for s in ("var", "sd", "r0", "r1"))
        rstd = chip.sb(n + "rs", [P, NJ], ctx=ctx)
        nmr = chip.sb(n + "nm", [P, NJ], ctx=ctx)
        tok_ready, var_ready, sd_ready, rstd_ready, xn_act, xn_dve, back_ready, hi_ready, order_sem = chip.norm_sems
        k = chip.norms
        chip.norms += 1
        block = ctx.enter_context(nc.Block())

        @block.sync
        def _(sp):
            if not beside.loaded:
                beside.load(sp)

        @block.gpsimd
        def _(pool):
            beside.split(pool)

        @block.tensor
        def _(pe):
            for j in range(NJ):
                for c in range(NC):
                    last = nc.tensor.transpose(chip.ps[:, j // 2, (j % 2) * D + c * P:(j % 2) * D + (c + 1) * P],
                                               chip.xT[:, c, j * P:(j + 1) * P], chip.ident[:])
                if j % 2:
                    last.then_inc(tok_ready, 1)
            if mod:
                mod.products(pe, BANKS - 1)
            for j in range(NJ):
                if mod and j == 4:
                    pe.wait_ge(mod.ready, 1)
                if j % 4 == 0:
                    pe.wait_ge(xn_act, 4 * k + j // 2 + 2)
                    pe.wait_ge(xn_dve, 4 * k + j // 2 + 2)
                for c in range(NC):
                    last = nc.tensor.transpose(chip.ps[:, 4 + (j // 4) * NC + c, (j % 4) * P:(j % 4 + 1) * P],
                                               xn[:, j, c * P:(c + 1) * P], chip.ident[:])
                if j % 4 == 3:
                    last.then_inc(back_ready, 1)

        @block.vector
        def _(dve):
            order = Order(dve, order_sem)
            order.done = k * (2 * NJ + 5 + NH * NC)
            for j in range(NJ):
                if j % 2 == 0:
                    dve.wait_ge(tok_ready, 4 * k + j // 2 + 1)
                order.mark(nc.vector.bn_stats(st[:, j, :], chip.ps[:, j // 2, (j % 2) * D:(j % 2 + 1) * D]))
            order.settle()
            for j in range(NJ):
                last = order.mark(nc.vector.bn_aggr(mv[:, j, :], st[:, j, :]))
            order.settle()
            nc.vector.tensor_scalar(var[:], mv[:, :, 1], EPS, None, ALU.add).then_inc(var_ready, 1)
            dve.wait_ge(sd_ready, k + 1)
            order.link(nc.vector.reciprocal(r0[:], sd[:]))
            order.link(nc.vector.tensor_tensor(r1[:], r0[:], r0[:], ALU.mult))
            order.link(nc.vector.tensor_tensor(r1[:], r1[:], var[:], ALU.mult))
            order.link(nc.vector.tensor_scalar(r1[:], r1[:], -0.5, 1.5, ALU.mult, ALU.add))
            order.link(nc.vector.tensor_tensor(rstd[:], r0[:], r1[:], ALU.mult))
            nc.vector.scalar_tensor_tensor(nmr[:], mv[:, :, 0], -1.0, rstd[:], ALU.mult, ALU.mult)\
                .then_inc(rstd_ready, 1)
            for j in (2, 3, 6, 7):
                nc.vector.tensor_scalar(xn[:, j, :], chip.ps[:, j // 2, (j % 2) * D:(j % 2 + 1) * D],
                                        mv[:, j, 0:1], rstd[:, j:j + 1], ALU.subtract, ALU.mult)\
                    .then_inc(xn_dve, 1)
            if mod:
                mod.columns(dve, BANKS - 1)
            for i in range(NH * NC):
                half, c = i // NC, i % NC
                cols = slice(half * HALF, (half + 1) * HALF)
                dve.wait_ge(hi_ready, 4 * k + i + 1)
                order.link(nc.vector.tensor_scalar(hf[:, i % 2, :], chip.ps[:, 4 + i, :],
                                                   mod_col(chip, layer, scale, c), mod_col(chip, layer, shift, c),
                                                   ALU.mult, ALU.add))
                nc.vector.tensor_tensor(chip.h_lo[:, c, cols], hf[:, i % 2, :],
                                        chip.h_hi[:, c, cols].bitcast(F32), ALU.subtract)

        @block.scalar
        def _(act):
            if mod:
                mod.activate(act)
            act.wait_ge(var_ready, k + 1)
            nc.scalar.activation(sd[:], var[:], ACT.Sqrt).then_inc(sd_ready, 1)
            act.wait_ge(rstd_ready, k + 1)
            for j in (0, 1, 4, 5):
                nc.scalar.activation(xn[:, j, :], chip.ps[:, j // 2, (j % 2) * D:(j % 2 + 1) * D], ACT.Identity,
                                     bias=nmr[:, j:j + 1], scale=rstd[:, j:j + 1]).then_inc(xn_act, 1)
            if mod:
                act.wait_ge(mod.ready, 1)
            for i in range(NH * NC):
                half, c = i // NC, i % NC
                act.wait_ge(back_ready, 2 * k + half + 1)
                nc.scalar.activation(chip.h_hi[:, c, half * HALF:(half + 1) * HALF], chip.ps[:, 4 + i, :],
                                     ACT.Identity, bias=mod_col(chip, layer, shift, c),
                                     scale=mod_col(chip, layer, scale, c)).then_inc(hi_ready, 1)


def three_parts(pe_out, nc, w_hi, w_lo, m_hi, m_lo, chunks, last_inc=None):
    n = 3 * len(chunks)
    i = 0
    for k in chunks:
        for w, m in ((w_hi, m_hi), (w_hi, m_lo), (w_lo, m_hi)):
            last = nc.tensor.matmul(pe_out, w(k), m(k), start=(i == 0), stop=(i == n - 1))
            i += 1
    return last


class Attention0Weights:
    loaded = True

    def __init__(self, nc, chip, ctx, wq, wk, wv, rep_q, rep_k, lanes):
        self.nc = nc
        self.sources = (wq, 0, D), (wk, D, D + 64), (wv, D + 64, D + 128)
        self.constants = rep_q, rep_k, lanes
        self.raw = chip.sb("ap_w", [P, NC, D + 2 * 64], ctx=ctx)
        self.wd = [chip.sb(f"ap_wd{i}", [P, NC, 5, 2, 64], F32R, ctx) for i in range(2)]
        self.wv = [chip.sb(f"ap_wv{i}", [P, NC, 64], F32R, ctx) for i in range(2)]
        self.rk = chip.sb("ap_rk", [P, KV_HEADS, P], ctx=ctx)
        self.rk_r = chip.sb("ap_rk_r", [P, KV_HEADS, P], F32R, ctx)
        self.rq = chip.sb("ap_rq", [P, 2, P], ctx=ctx)
        self.lane = chip.sb("ap_lane", [P, 2], ctx=ctx)
        self.w_in, self.c_in, self.w_split, self.r_ready, self.order_sem = (
            chip.sem("ap_" + s) for s in ("w", "c", "split", "r", "sord"))

    def load(self, sp):
        rep_q, rep_k, lanes = self.constants
        for w, a, b in self.sources:
            sp.dma_start(self.raw[:, :, a:b], w.rearrange("(k p) n -> p k n", p=P)).then_inc(self.w_in, 16)
        sp.dma_start(self.rk[:], rep_k).then_inc(self.c_in, 16)
        sp.dma_start(self.rq[:], rep_q).then_inc(self.c_in, 16)
        sp.dma_start(self.lane[:], lanes).then_inc(self.c_in, 16)

    def split(self, pool, repq_r, id_r, ident):
        nc, order = self.nc, Order(pool, self.order_sem)
        pool.wait_ge(self.w_in, 48)
        wide = [self.raw[:, k, 0:5 * 64].rearrange("p (t n) -> p t n", t=5).unsqueeze(2).to_broadcast([P, 5, 2, 64])
                for k in range(NC)]
        v = self.raw[:, :, 5 * 64:6 * 64]
        for k in range(NC):
            order.mark(nc.gpsimd.tensor_copy(self.wd[0][:, k], wide[k]))
        order.link(nc.gpsimd.tensor_copy(self.wv[0][:], v))
        for k in range(NC):
            order.mark(nc.gpsimd.tensor_tensor(self.wd[1][:, k], wide[k], self.wd[0][:, k].bitcast(F32),
                                               ALU.subtract))
        order.settle()
        nc.gpsimd.tensor_tensor(self.wv[1][:], v, self.wv[0][:].bitcast(F32), ALU.subtract)\
            .then_inc(self.w_split, 1)
        pool.wait_ge(self.c_in, 48)
        pool.wait_ge(self.w_split, 1)
        order.mark(nc.gpsimd.tensor_copy(self.rk_r[:], self.rk[:]))
        order.mark(nc.gpsimd.tensor_copy(id_r[:], ident[:]))
        order.settle()
        nc.gpsimd.tensor_copy(repq_r[:], self.rq[:]).then_inc(self.r_ready, 1)


class Attention0:
    loaded = True

    def __init__(self, nc, chip, ctx, weights_ctx, wq, wk, wv, wo, rep_q, rep_k, lanes):
        self.nc, self.chip, self.wo = nc, chip, wo
        self.qT = chip.sb("a_qT", [P, 5, T], F32R, ctx)
        self.krep = chip.sb("a_krep", [P, KV_HEADS, T], F32R, ctx)
        self.vall = chip.sb("a_vall", [P, KV_HEADS, NJ, QUAD], ctx=ctx)
        self.repq_r = chip.sb("a_repq_r", [P, 2, P], F32R, ctx)
        self.id_r = chip.sb("a_id_r", [P, P], F32R, ctx)
        self.out = chip.sb("a_out", [P, NJ, D], ctx=ctx)
        self.kk = [chip.sb(f"a_kk{i}", [P, GQ, T], F32R, ctx) for i in range(2)]
        self.wo_raw = chip.sb("a_wo", [P, NC, D], ctx=ctx)
        self.wo_in, self.zeroed = chip.sem("a_wo_in"), chip.sem("a_zeroed")
        self.weights = Attention0Weights(nc, chip, weights_ctx, wq, wk, wv, rep_q, rep_k, lanes)

    def load(self, sp):
        self.weights.load(sp)
        sp.dma_start(self.wo_raw[:], self.wo.rearrange("(k p) n -> p k n", p=P)).then_inc(self.wo_in, 16)

    def split(self, pool):
        self.weights.split(pool, self.repq_r, self.id_r, self.chip.ident)


def attention0_project(nc, chip, att):
    with ExitStack() as ctx:
        weights, qT, krep, vall = att.weights, att.qT, att.krep, att.vall
        wd, wvp, rk_r, lane = weights.wd, weights.wv, weights.rk_r, weights.lane
        hi = chip.sb("ap_hi", [P, 2, HALF], F32R, ctx)
        mm, hi_done, freed, rep_mm, v_mm, rep_a, rep_d, zeroed = (
            chip.sem("ap_" + s) for s in ("mm", "hi", "free", "rmm", "vmm", "ra", "rd", "z"))
        JOBS = [(t, half) for t in (4, 0, 1, 2, 3) for half in range(NH)]
        block = ctx.enter_context(nc.Block())

        @block.gpsimd
        def _(pool):
            nc.gpsimd.memset(vall[:], 0.0).then_inc(zeroed, 1)
            pool.wait_ge(zeroed, 1)
            nc.gpsimd.memset(vall[:, :, :, DH:DH + 1], 1.0).then_inc(zeroed, 1)
            pool.wait_ge(zeroed, 2)
            for kk in att.kk:
                nc.gpsimd.memset(kk[:].bitcast(mybir.dt.uint32), 0).then_inc(att.zeroed, 1)

        @block.vector
        def _(dve):
            for n, (t, half) in enumerate(JOBS):
                dve.wait_ge(hi_done, n + 1)
                nc.vector.scalar_tensor_tensor(qT[:, t, half * HALF:(half + 1) * HALF],
                                               hi[:, n % 2, :].bitcast(F32), lane[:, 0:1], chip.ps[:, n % 2, :],
                                               ALU.mult, ALU.add).then_inc(freed, 1)
            dve.wait_ge(v_mm, 1)
            dve.wait_ge(zeroed, 2)
            nc.vector.tensor_copy(vall[:, :, :, 0:DH].rearrange("p g j d -> p j g d"),
                                  chip.ps[:, 2, :].rearrange("p (j g d) -> p j g d", j=NJ, g=KV_HEADS))
            for n in range(1, 2 * KV_HEADS, 2):
                dve.wait_ge(rep_mm, n + 1)
                nc.vector.tensor_scalar(krep[:, n // 2, HALF:T], chip.ps[:, 4 + n % 4, :], lane[:, 1:2], None,
                                        ALU.add).then_inc(rep_d, 1)

        @block.scalar
        def _(act):
            for n, (t, half) in enumerate(JOBS):
                act.wait_ge(mm, n + 1)
                if n >= 2:
                    act.wait_ge(freed, n - 1)
                nc.scalar.activation(hi[:, n % 2, :], chip.ps[:, n % 2, :], ACT.Copy).then_inc(hi_done, 1)
            for n in range(0, 2 * KV_HEADS, 2):
                act.wait_ge(rep_mm, n + 1)
                nc.scalar.activation(krep[:, n // 2, 0:HALF], chip.ps[:, 4 + n % 4, :], ACT.Identity,
                                     bias=lane[:, 1:2]).then_inc(rep_a, 1)

        @block.tensor
        def _(pe):
            pe.wait_ge(weights.w_split, 1)
            for n, (t, half) in enumerate(JOBS):
                cols = slice(half * HALF, (half + 1) * HALF)
                if n >= 2:
                    pe.wait_ge(freed, n - 1)
                three_parts(chip.ps[:, n % 2, :], nc,
                            lambda k: wd[0][:, k, t, :, :], lambda k: wd[1][:, k, t, :, :],
                            lambda k: chip.h_hi[:, k, cols], lambda k: chip.h_lo[:, k, cols],
                            range(NC)).then_inc(mm, 1)
            for j in range(NJ):
                cols = slice(j * P, (j + 1) * P)
                last = three_parts(chip.ps[:, 2, j * 64:(j + 1) * 64], nc,
                                   lambda k: chip.h_hi[:, k, cols], lambda k: chip.h_lo[:, k, cols],
                                   lambda k: wvp[0][:, k, :], lambda k: wvp[1][:, k, :], range(NC))
            last.then_inc(v_mm, 1)
            pe.wait_ge(weights.r_ready, 1)
            for n in range(2 * KV_HEADS):
                if n >= 4:
                    pe.wait_ge(rep_d if n % 2 else rep_a, (n - 4) // 2 + 1)
                nc.tensor.matmul(chip.ps[:, 4 + n % 4, :], rk_r[:, n // 2, :],
                                 qT[:, 4, (n % 2) * HALF:(n % 2 + 1) * HALF], start=True, stop=True)\
                    .then_inc(rep_mm, 1)


def attention0_core(nc, chip, att):
    ps = chip.ps
    STEPS = NH * NJ
    NMAX = GQ * NJ * NH
    PER = NMAX // STEPS
    MID = NJ + 1
    MAXB, PVB, TRB = 4, 6, 7
    SLOTS = 4
    SCALE = float(DH) ** -0.5
    LASTG = KV_HEADS - 1
    with ExitStack() as ctx:
        qT, krep, vall, repq_r, id_r, out, kk = att.qT, att.krep, att.vall, att.repq_r, att.id_r, att.out, att.kk
        qa = [chip.sb(f"ac_qa{i}", [P, T], F32R, ctx) for i in range(2)]
        qb = [chip.sb(f"ac_qb{i}", [P, T], F32R, ctx) for i in range(2)]
        vg = [chip.sb(f"ac_vg{i}", [P, NJ, QUAD], ctx=ctx) for i in range(2)]
        probs = chip.sb("ac_p", [P, SLOTS, GQ, HALF], ctx=ctx)
        ot = chip.sb("ac_ot", [P, 2, HALF], ctx=ctx)
        mxp = chip.sb("ac_mxp", [P, NJ, GQ, NH], ctx=ctx)
        nm = chip.sb("ac_nm", [P, NJ, GQ], ctx=ctx)
        m4 = chip.sb("ac_m4", [P, NJ, P], F32R, ctx)
        rinv = chip.sb("ac_ri", [P, 4, GQ], ctx=ctx)
        names = ("score_mm", "exp_done", "pv_mm", "o_out", "o_turned", "o_done", "max_mm", "max_done", "m_ready",
                 "qa_mm", "qa_done", "qb_mm", "qb_done", "kk_done", "vg_done", "zeroed", "ord")
        (score_mm, exp_done, pv_mm, o_out, o_turned, o_done, max_mm, max_done, m_ready,
         qa_mm, qa_done, qb_mm, qb_done, kk_done, vg_done, zeroed, order_sem) = (
            chip.sem("ac_" + s, ctx) for s in names)
        m4q = m4[:].rearrange("p j (h r) -> p j h r", h=GQ)
        block = ctx.enter_context(nc.Block())

        def groups(eng, body):
            body(0, 0, 0, 1)
            with eng.Fori(0, (KV_HEADS - 2) // 2) as i:
                for u in range(2):
                    body(i * 2 + (1 + u), (1 + u) % 2, i + 1, i + (1 + (1 + u) // 2))
            body(LASTG, LASTG % 2, None, None)

        def is_first(g):
            return isinstance(g, int) and g == 0

        def is_last(g):
            return isinstance(g, int) and g == LASTG

        def block_of(n):
            qh, r = divmod(n, NMAX // 2)
            h, r = divmod(r, NMAX // 2 // GQ)
            return h, qh * (NJ // 2) + r // NH, r % NH

        def blocks_at(g, step):
            if step == 0:
                return [] if is_first(g) else [(0, n) for n in range(NMAX - PER, NMAX)]
            if is_last(g):
                return []
            return [(1, n) for n in range((step - 1) * PER, step * PER)]

        def pair_of(g, par, pair1):
            return LASTG // 2 if is_last(g) else (pair1 if par == 0 else pair1 - 1)

        @block.tensor
        def _(pe):
            def max_block(slot, n):
                h, j, half = block_of(n)
                nc.tensor.matmul(ps[:, MAXB + n % 2, :], qa[slot][:, j * P:(j + 1) * P],
                                 kk[slot][:, h, half * HALF:(half + 1) * HALF], start=True, stop=True)\
                    .then_inc(max_mm, 1)

            def spread_q(pair, par, half):
                nc.tensor.matmul(ps[:, TRB, :], repq_r[:, par, :], qT[:, pair, half * HALF:(half + 1) * HALF],
                                 start=True, stop=True).then_inc(qa_mm, 1)

            def spread_q_max(pair, par, half):
                for q in range(4):
                    cols = slice(half * HALF + q * P, half * HALF + (q + 1) * P)
                    nc.tensor.matmul(ps[:, TRB, q * P:(q + 1) * P], repq_r[:, par, :], qT[:, pair, cols],
                                     start=True, stop=False)
                    last = nc.tensor.matmul(ps[:, TRB, q * P:(q + 1) * P], m4[:, half * 4 + q, :], id_r[:],
                                            start=False, stop=True)
                last.then_inc(qb_mm, 1)

            def turn(g, qh):
                pe.wait_ge(o_out, g * NH + (qh + 1))
                for q in range(4):
                    last = nc.tensor.transpose(ps[:, TRB, q * P:(q + 1) * P], ot[:, qh, q * P:(q + 1) * P],
                                               chip.ident[:])
                last.then_inc(o_turned, 1)

            def values(g, par, s, part):
                if part == 0:
                    pe.wait_ge(exp_done, g * (2 * STEPS) + 2 * (s + 1))
                    if s == 0 and not is_first(g):
                        pe.wait_ge(o_out, g * NH)
                    if s == NJ:
                        pe.wait_ge(o_out, g * NH + 1)
                    if s == 0:
                        pe.wait_ge(vg_done, g + 1)
                cols = slice(part * (HALF // 2), (part + 1) * (HALF // 2))
                for h in range(GQ):
                    last = nc.tensor.matmul(ps[h * QUAD:(h + 1) * QUAD, PVB, cols], vg[par][:, s % NJ, :],
                                            probs[:, s % SLOTS, h, cols], start=(s % NJ == 0 and part == 0),
                                            stop=(s % NJ == NJ - 1), skip_group_check=True)
                if part:
                    last.then_inc(pv_mm, 1)

            for G in range(2):
                for half in range(NH):
                    if 2 * G + half:
                        pe.wait_ge(qa_done, 2 * G + half)
                    spread_q(0, G, half)
            pe.wait_ge(qa_done, 4)
            pe.wait_ge(zeroed, 1)
            pe.wait_ge(att.zeroed, 2)
            for n in range(NMAX):
                if n == 0 or block_of(n)[0] > block_of(n - 1)[0]:
                    pe.wait_ge(kk_done, block_of(n)[0] + 1)
                if n >= 2:
                    pe.wait_ge(max_done, n - 1)
                max_block(0, n)
            for half in range(NH):
                pe.wait_ge(m_ready, half + 1)
                if half:
                    pe.wait_ge(qb_done, half)
                spread_q_max(0, 0, half)

            def body(g, par, pair1, pair2):
                nxt = 1 - par

                def some_max(step, lots):
                    for who, n in lots:
                        if who:
                            if n == 0:
                                pe.wait_ge(qa_done, g * 2 + 4)
                            if n < NMAX // 2 and (n == 0 or block_of(n)[0] > block_of(n - 1)[0]):
                                pe.wait_ge(kk_done, g * GQ + (GQ + block_of(n)[0] + 1))
                        pe.wait_ge(max_done, g * NMAX + (who * NMAX + n - 1))
                        max_block(nxt if who else par, n)

                for step in range(STEPS):
                    qh, kt = step // NJ, step % NJ
                    lots = blocks_at(g, step)
                    if step == 0:
                        pe.wait_ge(qb_done, g * 2 + 1)
                        pe.wait_ge(kk_done, g * GQ + GQ)
                    if step == NJ:
                        pe.wait_ge(qb_done, g * 2 + 2)
                    for pair in range(2):
                        if step or not is_first(g):
                            pe.wait_ge(exp_done, g * (2 * STEPS) + (2 * step + pair - 1))
                        for h in (2 * pair, 2 * pair + 1):
                            last = nc.tensor.matmul(ps[:, h, :], kk[par][:, h, kt * P:(kt + 1) * P],
                                                    qb[par][:, qh * HALF:(qh + 1) * HALF], start=True, stop=True)
                        last.then_inc(score_mm, 1)
                        some_max(step, lots[2 * pair:2 * pair + 1])
                        if step >= 2:
                            values(g, par, step - 2, pair)
                        elif not is_first(g):
                            values(g - 1, nxt, STEPS - 2 + step, pair)
                        some_max(step, lots[2 * pair + 1:2 * pair + 2])
                    if step == 2 and not is_first(g):
                        pe.wait_ge(m_ready, g * 2 + 2)
                        pe.wait_ge(o_done, g * NH)
                        spread_q_max(pair_of(g, par, pair1), par, 1)
                    if step == 4 and not is_first(g):
                        pe.wait_ge(qb_done, g * 2 + 2)
                        turn(g - 1, 1)
                    if step == 6 and not is_last(g):
                        if is_first(g):
                            pe.wait_ge(qb_done, 2)
                        pe.wait_ge(o_done, g * NH + 1)
                        spread_q(pair2, par, 0)
                    if step == 7 and not is_last(g):
                        pe.wait_ge(qa_done, g * 2 + 5)
                        spread_q(pair2, par, 1)
                    if step == MID + 1 and not is_last(g):
                        pe.wait_ge(m_ready, g * 2 + 3)
                        pe.wait_ge(qa_done, g * 2 + 6)
                        spread_q_max(pair1, nxt, 0)
                    if step == MID + 3:
                        if not is_last(g):
                            pe.wait_ge(qb_done, g * 2 + 3)
                        else:
                            pe.wait_ge(o_done, g * NH + 1)
                        turn(g, 0)

            groups(pe, body)
            for s in (STEPS - 2, STEPS - 1):
                for part in range(2):
                    values(LASTG, LASTG % 2, s, part)
            pe.wait_ge(o_done, LASTG * NH + 2)
            turn(LASTG, 1)

        @block.scalar
        def _(act):
            def keep_q(dst, sem, done, value, half):
                act.wait_ge(sem, value)
                nc.scalar.activation(dst[:, half * HALF:(half + 1) * HALF], ps[:, TRB, :], ACT.Copy)\
                    .then_inc(done, 1)

            for G in range(2):
                for half in range(NH):
                    keep_q(qa[G], qa_mm, qa_done, 2 * G + half + 1, half)
            for half in range(NH):
                keep_q(qb[0], qb_mm, qb_done, half + 1, half)

            def values_out(g, qh):
                act.wait_ge(pv_mm, g * STEPS + (qh + 1) * NJ)
                if qh:
                    act.wait_ge(o_turned, g * NH + 1)
                elif not is_first(g):
                    act.wait_ge(o_turned, g * NH - 1)
                nc.scalar.activation(ot[:, qh, :], ps[:, PVB, :], ACT.Copy).then_inc(o_out, 1)

            def body(g, par, pair1, pair2):
                nxt = 1 - par
                for step in range(STEPS):
                    for pair in range(2):
                        act.wait_ge(score_mm, g * (2 * STEPS) + (2 * step + pair + 1))
                        if pair == 0 and (step >= SLOTS or not is_first(g)):
                            act.wait_ge(pv_mm, g * STEPS + (step - SLOTS + 1))
                        nc.scalar.activation(probs[:, step % SLOTS, 2 * pair:2 * pair + 2, :],
                                             ps[:, 2 * pair:2 * pair + 2, :], ACT.Exp, scale=SCALE)\
                            .then_inc(exp_done, 1)
                    if step == 1 and not is_first(g):
                        values_out(g - 1, 1)
                    if step == 3 and not is_first(g):
                        keep_q(qb[par], qb_mm, qb_done, g * 2 + 2, 1)
                    if step in (7, 8) and not is_last(g):
                        keep_q(qa[par], qa_mm, qa_done, g * 2 + (step - 7) + 5, step - 7)
                    if step == NJ + 1:
                        values_out(g, 0)
                    if step == MID + 2 and not is_last(g):
                        keep_q(qb[nxt], qb_mm, qb_done, g * 2 + 3, 0)

            groups(act, body)
            values_out(LASTG, 1)

        @block.vector
        def _(dve):
            order = Order(dve, order_sem)

            def find_max(base, n):
                h, j, half = block_of(n)
                dve.wait_ge(max_mm, base + (n + 1))
                nc.vector.tensor_reduce(mxp[:, j, h, half:half + 1], ps[:, MAXB + n % 2, :], AX.X, ALU.max)\
                    .then_inc(max_done, 1)

            def negate(base, qh, m4_used):
                js = slice(qh * (NJ // 2), (qh + 1) * (NJ // 2))
                dve.wait_ge(max_done, base + (qh + 1) * (NMAX // 2))
                if m4_used is not None:
                    dve.wait_ge(qb_mm, m4_used)
                order.link(nc.vector.tensor_reduce(nm[:, js], mxp[:, js], AX.X, ALU.max, negate=True))
                order.link(nc.vector.tensor_copy(m4q[:, js, :, M_HI], nm[:, js]))
                nc.vector.tensor_tensor(m4q[:, js, :, M_LO], nm[:, js], m4q[:, js, :, M_HI].bitcast(F32),
                                        ALU.subtract).then_inc(m_ready, 1)

            def outputs(g, qh):
                dve.wait_ge(o_turned, g * NH + (qh + 1))
                turned = ps[:, TRB, :].rearrange("p (q h r) -> p q h r", q=4, h=GQ)
                order.link(nc.vector.reciprocal(rinv[:], turned[:, :, :, DH]))
                cols = out[:, qh * 4:(qh + 1) * 4, bass.ds(g * (GQ * DH), GQ * DH)]
                nc.vector.tensor_tensor(cols.rearrange("p q (h d) -> p q h d", h=GQ), turned[:, :, :, 0:DH],
                                        rinv[:].unsqueeze(3).to_broadcast([P, 4, GQ, DH]), ALU.mult)\
                    .then_inc(o_done, 1)

            nc.vector.memset(m4[:].bitcast(mybir.dt.uint32), 0).then_inc(zeroed, 1)
            dve.wait_ge(zeroed, 1)
            for qh in range(2):
                for n in range(qh * (NMAX // 2), (qh + 1) * (NMAX // 2)):
                    find_max(0, n)
                negate(0, qh, None)
            nc.vector.memset(rinv[:], 0.0).then_inc(o_done, 1)
            dve.wait_ge(o_done, 1)
            base = order.done
            MARKS = 2 * 2 + 2

            def body(g, par, pair1, pair2):
                order.done = base if is_first(g) else g * MARKS + (base - 3)
                for step in range(STEPS):
                    for who, n in blocks_at(g, step):
                        find_max(g * NMAX + who * NMAX, n)
                    if step == 0 and not is_first(g):
                        negate(g * NMAX, 1, g * 2)
                    if step == 4 and not is_first(g):
                        outputs(g - 1, 1)
                    if step == MID and not is_last(g):
                        negate(g * NMAX + NMAX, 0, g * 2 + 2)
                    if step == MID + 3:
                        outputs(g, 0)

            groups(dve, body)
            outputs(LASTG, 1)

        @block.gpsimd
        def _(pool):
            pool.wait_ge(att.zeroed, 2)

            def keep_kv(G, slot):
                for h in range(GQ):
                    rows = slice(h * QUAD, (h + 1) * QUAD)
                    nc.gpsimd.tensor_copy(kk[slot][rows, h, :], krep[rows, G, :]).then_inc(kk_done, 1)

            keep_kv(0, 0)
            pool.wait_ge(kk_done, GQ)
            nc.gpsimd.tensor_copy(vg[0][:], vall[:, 0, :, :]).then_inc(vg_done, 1)

            def body(g, par, pair1, pair2):
                if not is_last(g):
                    if is_first(g):
                        pool.wait_ge(vg_done, 1)
                    else:
                        pool.wait_ge(score_mm, g * (2 * STEPS))
                        pool.wait_ge(vg_done, g + 1)
                        pool.wait_ge(att.zeroed, 2)
                    keep_kv(g + 1, 1 - par)
                    if not is_first(g):
                        pool.wait_ge(pv_mm, g * STEPS)
                    pool.wait_ge(kk_done, g * GQ + 2 * GQ)
                    pool.wait_ge(att.zeroed, 2)
                    nc.gpsimd.tensor_copy(vg[1 - par][:], vall[:, g + 1, :, :]).then_inc(vg_done, 1)

            groups(pool, body)


def attention0_output(nc, chip, att):
    with ExitStack() as ctx:
        w_raw, out = att.wo_raw, att.out
        w_hi = chip.sb("ao_wh", [P, NC, D], F32R, ctx)
        w_lo = chip.sb("ao_wl", [P, NC, D], F32R, ctx)
        w_split, turned, hi_done, lo_done, mm, order_sem = (
            chip.sem("ao_" + s, ctx) for s in ("ws", "turned", "hi", "lo", "mm", "ord"))
        block = ctx.enter_context(nc.Block())

        @block.vector
        def _(dve):
            order = Order(dve, order_sem)
            dve.wait_ge(att.wo_in, 16)
            order.link(nc.vector.tensor_copy(w_hi[:], w_raw[:]))
            nc.vector.tensor_tensor(w_lo[:], w_raw[:], w_hi[:].bitcast(F32), ALU.subtract).then_inc(w_split, 1)
            for i in range(NH * NC):
                half, c = i // NC, i % NC
                cols = slice(half * HALF, (half + 1) * HALF)
                dve.wait_ge(hi_done, i + 1)
                nc.vector.tensor_tensor(chip.h_lo[:, c, cols], chip.ps[:, i, :], chip.h_hi[:, c, cols].bitcast(F32),
                                        ALU.subtract).then_inc(lo_done, 1)
            for i in range(NH * NC):
                half, c = i // NC, i % NC
                cols = slice(half * HALF, (half + 1) * HALF)
                dve.wait_ge(mm, i + 1)
                nc.vector.scalar_tensor_tensor(chip.xT[:, c, cols], chip.ps[:, 4 + i, :], mod_col(chip, 0, 2, c),
                                               chip.xT[:, c, cols], ALU.mult, ALU.add)

        @block.scalar
        def _(act):
            for i in range(NH * NC):
                half, c = i // NC, i % NC
                act.wait_ge(turned, i + 1)
                nc.scalar.activation(chip.h_hi[:, c, half * HALF:(half + 1) * HALF], chip.ps[:, i, :], ACT.Copy)\
                    .then_inc(hi_done, 1)

        @block.tensor
        def _(pe):
            for half in range(NH):
                for c in range(NC):
                    for q in range(4):
                        last = nc.tensor.transpose(chip.ps[:, half * NC + c, q * P:(q + 1) * P],
                                                   out[:, half * 4 + q, c * P:(c + 1) * P], chip.ident[:])
                    last.then_inc(turned, 1)
            pe.wait_ge(w_split, 1)
            for i in range(NH * NC):
                half, c = i // NC, i % NC
                cols = slice(half * HALF, (half + 1) * HALF)
                pe.wait_ge(lo_done, (half + 1) * NC)
                three_parts(chip.ps[:, 4 + i, :], nc,
                            lambda k: w_hi[:, k, c * P:(c + 1) * P], lambda k: w_lo[:, k, c * P:(c + 1) * P],
                            lambda k: chip.h_hi[:, k, cols], lambda k: chip.h_lo[:, k, cols],
                            range(NC)).then_inc(mm, 1)


class RouterWeights:
    loaded = False

    def __init__(self, nc, chip, ctx, tag, gate_w, gate_b, tri, n_experts, n_groups):
        self.nc, self.sources, E, G = nc, (gate_w, gate_b, tri), n_experts, n_groups
        n = f"r{tag}_"
        self.raw = chip.sb(n + "w", [P, NC, E], ctx=ctx)
        self.hi = chip.sb(n + "wh", [P, NC, E], F32R, ctx)
        self.lo = chip.sb(n + "wl", [P, NC, E], F32R, ctx)
        self.bias = chip.sb(n + "b", [P, E], ctx=ctx)
        self.tri = chip.sb(n + "tri", [P, G, G], ctx=ctx)
        self.w_in, self.b_in, self.w_split, self.order_sem = (chip.sem(n + s) for s in ("w", "b", "ws", "so"))

    def load(self, sp):
        gate_w, gate_b, tri = self.sources
        E, G = self.raw.shape[2], self.tri.shape[1]
        sp.dma_start(self.raw[:], gate_w.rearrange("(k p) n -> p k n", p=P)).then_inc(self.w_in, 16)
        sp.dma_start(self.bias[:], gate_b.rearrange("(a e) -> a e", a=1).to_broadcast([P, E])).then_inc(self.b_in, 16)
        sp.dma_start(self.tri[:], tri[:, 0:G, 0:G]).then_inc(self.b_in, 16)

    def split(self, pool):
        order = Order(pool, self.order_sem)
        pool.wait_ge(self.w_in, 16)
        order.link(self.nc.gpsimd.tensor_copy(self.hi[:], self.raw[:]))
        self.nc.gpsimd.tensor_tensor(self.lo[:], self.raw[:], self.hi[:].bitcast(F32), ALU.subtract)\
            .then_inc(self.w_split, 1)


def route(nc, chip, tag, weights, experts, n_groups, top_groups, top_k, scaling, extra, cwT, beside, mod=None):
    E, G, ES = experts, n_groups, experts // n_groups
    JG = NJ * G
    n = f"r{tag}_"
    with ExitStack() as ctx:
        w_hi, w_lo, bias, tri_t = weights.hi, weights.lo, weights.bias, weights.tri
        score = chip.sb(n + "s", [P, NJ, E], ctx=ctx)
        biased = chip.sb(n + "sb", [P, NJ, E], ctx=ctx)
        top = [[chip.sb(f"{n}t{lv}{i}", [P, JG, ES >> (lv + 1)], ctx=ctx) for i in range(4)]
               for lv in range(ES.bit_length() - 1)]
        gsum = chip.sb(n + "g", [P, NJ, G], ctx=ctx)
        cmp_a = chip.sb(n + "ca", [P, NJ, G, G], ctx=ctx)
        cmp_b = chip.sb(n + "cb", [P, NJ, G, G], ctx=ctx)
        gmask = chip.sb(n + "gm", [P, NJ, G], ctx=ctx)
        gfill = chip.sb(n + "gf", [P, NJ, G], ctx=ctx)
        masked = chip.sb(n + "m", [P, NJ, E], ctx=ctx)
        best = chip.sb(n + "v8", [P, NJ, 8], ctx=ctx)
        replaced = chip.sb(n + "rp", [P, NJ, E], ctx=ctx)
        wsum = chip.sb(n + "ws", [P, NJ], ctx=ctx)
        winv = chip.sb(n + "wi", [P, NJ], ctx=ctx)
        cw = chip.sb(n + "cw", [P, NJ, P], F32R, ctx)
        logit_mm, sig_done, cw_ready, turned, order_sem = (
            chip.sem(n + s) for s in ("lg", "sg", "cw", "tu", "ord"))
        block = ctx.enter_context(nc.Block())

        @block.sync
        def _(sp):
            if mod:
                mod.load(sp)
            beside.load_first(sp)

        @block.gpsimd
        def _(pool):
            beside.split_first(pool)

        @block.tensor
        def _(pe):
            pe.wait_ge(weights.w_split, 1)
            for j in range(NJ):
                cols = slice(j * P, (j + 1) * P)
                last = three_parts(chip.ps[:, 0, j * E:(j + 1) * E], nc,
                                   lambda k: chip.h_hi[:, k, cols], lambda k: chip.h_lo[:, k, cols],
                                   lambda k: w_hi[:, k, :], lambda k: w_lo[:, k, :], range(NC))
            last.then_inc(logit_mm, 1)
            if mod:
                mod.products(pe, 3)
            pe.wait_ge(cw_ready, 1)
            for j in range(NJ):
                last = nc.tensor.transpose(chip.ps[:, 1 + j // 4, (j % 4) * P:(j % 4 + 1) * P],
                                           cw[:, j, :].bitcast(F32), chip.ident[:])
                if j % 4 == 3:
                    last.then_inc(turned, 1)

        @block.scalar
        def _(act):
            if mod:
                mod.activate(act)
            act.wait_ge(logit_mm, 1)
            nc.scalar.activation(score[:], chip.ps[:, 0, 0:NJ * E].rearrange("p (j e) -> p j e", j=NJ), ACT.Sigmoid)\
                .then_inc(sig_done, 1)

        @block.vector
        def _(dve):
            order = Order(dve, order_sem)
            tt, ts = nc.vector.tensor_tensor, nc.vector.tensor_scalar
            order.mark(nc.vector.memset(cw[:].bitcast(mybir.dt.uint32), 0))
            dve.wait_ge(weights.b_in, 32)
            dve.wait_ge(sig_done, 1)
            order.link(tt(biased[:], score[:], bias[:].unsqueeze(1).to_broadcast([P, NJ, E]), ALU.add))
            b = biased[:].rearrange("p j (g e) -> p (j g) e", g=G)
            a0, a1 = b[:, :, 0::2], b[:, :, 1::2]
            order.mark(tt(top[0][0][:], a0, a1, ALU.max))
            order.link(tt(top[0][1][:], a0, a1, ALU.min))
            for lv in range(1, len(top)):
                hi, lo = top[lv - 1][0], top[lv - 1][1]
                order.mark(tt(top[lv][2][:], hi[:, :, 0::2], hi[:, :, 1::2], ALU.min))
                order.mark(tt(top[lv][3][:], lo[:, :, 0::2], lo[:, :, 1::2], ALU.max))
                order.link(tt(top[lv][0][:], hi[:, :, 0::2], hi[:, :, 1::2], ALU.max))
                order.link(tt(top[lv][1][:], top[lv][2][:], top[lv][3][:], ALU.max))
            order.link(tt(gsum[:].rearrange("p j g -> p (j g)"), top[-1][0][:, :, 0], top[-1][1][:, :, 0], ALU.add))
            other = gsum[:].unsqueeze(2).to_broadcast([P, NJ, G, G])
            own = gsum[:].unsqueeze(3).to_broadcast([P, NJ, G, G])
            order.mark(tt(cmp_a[:], other, own, ALU.is_gt))
            order.link(tt(cmp_b[:], other, own, ALU.is_ge))
            order.link(tt(cmp_b[:], cmp_b[:], tri_t[:].unsqueeze(1).to_broadcast([P, NJ, G, G]), ALU.mult))
            order.link(tt(cmp_a[:], cmp_a[:], cmp_b[:], ALU.max))
            order.link(nc.vector.tensor_reduce(gmask[:], cmp_a[:], AX.X, ALU.add))
            order.link(ts(gmask[:], gmask[:], float(top_groups), None, ALU.is_lt))
            order.link(ts(gfill[:], gmask[:], BIG, -BIG, ALU.mult, ALU.add))
            m4 = masked[:].rearrange("p j (g e) -> p (j g) e", g=G)
            wide = [P, JG, ES]
            order.link(tt(m4, b, gmask[:].rearrange("p j g -> p (j g)").unsqueeze(2).to_broadcast(wide), ALU.mult))
            order.link(tt(m4, m4, gfill[:].rearrange("p j g -> p (j g)").unsqueeze(2).to_broadcast(wide), ALU.add))
            for j in range(NJ):
                order.mark(nc.vector.max(best[:, j, :], masked[:, j, :]))
            order.settle()
            order.link(nc.vector.memset(best[:, :, top_k:8], -BIG))
            for j in range(NJ):
                order.mark(nc.vector.match_replace(replaced[:, j, :], best[:, j, :], masked[:, j, :], -BIG))
            order.settle()
            order.link(tt(masked[:], masked[:], replaced[:], ALU.not_equal))
            order.link(tt(masked[:], masked[:], score[:], ALU.mult))
            order.link(nc.vector.tensor_reduce(wsum[:], masked[:], AX.X, ALU.add))
            order.link(ts(wsum[:], wsum[:], 1e-20, None, ALU.add))
            order.link(nc.vector.reciprocal(winv[:], wsum[:]))
            order.link(ts(winv[:], winv[:], scaling, None, ALU.mult))
            order.link(tt(masked[:], masked[:], winv[:].unsqueeze(2).to_broadcast([P, NJ, E]), ALU.mult))
            order.link(nc.vector.tensor_copy(cw[:, :, 0:E], masked[:]))
            if extra:
                order.mark(nc.vector.memset(cw[:, :, E:E + extra].bitcast(F32), 1.0))
            order.link(tt(cw[:, :, 64:64 + E], masked[:], cw[:, :, 0:E].bitcast(F32), ALU.subtract))
            nc.vector.tensor_copy(winv[:], wsum[:]).then_inc(cw_ready, 1)
            for half in range(NH):
                dve.wait_ge(turned, half + 1)
                nc.vector.tensor_copy(cwT[:, half * HALF:(half + 1) * HALF], chip.ps[:, 1 + half, :])
            if mod:
                mod.columns(dve, 3)


class Experts:
    SLOTS = 3

    def __init__(self, nc, chip, ctx, tag, source, gated, n_plain, e2):
        self.nc, self.source, self.gated, self.n_plain, self.e2 = nc, source, gated, n_plain, e2
        self.n_units = source.shape[0]
        self.ups = 2 if gated else 1
        self.wup = self.ups * NC * P
        wall = self.wup + D
        n = f"e{tag}_"
        self.raw = [chip.sb(f"{n}raw{i}", [P, wall], ctx=ctx) for i in range(self.SLOTS)]
        self.w_hi = [chip.sb(f"{n}wh{i}", [P, wall], F32R, ctx) for i in range(self.SLOTS)]
        self.w_lo = [chip.sb(f"{n}wl{i}", [P, wall], F32R, ctx) for i in range(self.SLOTS)]
        self.pick = [chip.sb(f"{n}pk{i}", [P, P], F32R, ctx) for i in range(self.SLOTS)]
        self.e2_t = chip.sb(n + "e2", [P, 64], ctx=ctx)
        self.zero = chip.sb(n + "zero", [P, 1], ctx=ctx)
        self.w_in = [chip.sem(f"{n}win{i}") for i in range(self.SLOTS)]
        self.e2_in, self.w_split, self.down_mm, self.order_sem = (chip.sem(n + s) for s in ("e2", "ws", "dm", "po"))
        self.loops = (self.n_units - self.SLOTS - max(n_plain, 1)) // self.SLOTS

    def first_units(self, body):
        for e in range(self.SLOTS):
            body(e, e, 0, False)

    def later_units(self, eng, body):
        with eng.Fori(0, self.loops) as i:
            for u in range(self.SLOTS):
                body(i * self.SLOTS + (self.SLOTS + u), u, i + 1, False)
        for e in range(self.SLOTS * (self.loops + 1), self.n_units):
            body(e, e % self.SLOTS, e // self.SLOTS, (not self.gated) and e >= self.n_units - self.n_plain)

    def units(self, eng, body):
        self.first_units(body)
        self.later_units(eng, body)

    def load_unit(self, sp, e, slot, before):
        if not (isinstance(before, int) and before == 0):
            sp.wait_ge(self.w_split, e - (self.SLOTS - 1))
        sp.dma_start(self.raw[slot][:], self.source[e]).then_inc(self.w_in[slot], 16)

    def split_unit(self, pool, order, e, slot, before, plain):
        nc, n_units = self.nc, self.n_units
        raw, w_hi, w_lo, pick = self.raw[slot], self.w_hi[slot], self.w_lo[slot], self.pick[slot]
        if not plain or e == n_units - self.n_plain:
            order.done = e * 2 + 1
        if not (isinstance(before, int) and before == 0):
            pool.wait_ge(self.down_mm, e * 2 - (2 * self.SLOTS - 2))
        pool.wait_ge(self.w_in[slot], before * 16 + 16)

        def keep(dst, src, zeros):
            order.link(nc.gpsimd.tensor_tensor(dst, src, zeros, ALU.add))

        keep(w_hi[:], raw[:], self.zero[:].to_broadcast(list(raw.shape)))
        if self.gated:
            keep(pick[:], self.e2_t[:, bass.ds(e, 1)].to_broadcast([P, P]), self.zero[:].to_broadcast([P, P]))
        elif not plain:
            keep(pick[:].rearrange("p (a b) -> p a b", a=2),
                 self.e2_t[:, bass.ds(e * 2, 2)].unsqueeze(2).to_broadcast([P, 2, 64]),
                 self.zero[:].unsqueeze(2).to_broadcast([P, 2, 64]))
        nc.gpsimd.tensor_tensor(w_lo[:], raw[:], w_hi[:].bitcast(F32), ALU.subtract).then_inc(self.w_split, 1)
        pool.wait_ge(self.w_split, e + 1)

    def load_first(self, sp):
        sp.dma_start(self.e2_t[:], self.e2).then_inc(self.e2_in, 16)
        self.first_units(lambda e, slot, before, plain: self.load_unit(sp, e, slot, before))

    def split_first(self, pool):
        order = Order(pool, self.order_sem)
        order.link(self.nc.gpsimd.memset(self.zero[:], 0.0))
        pool.wait_ge(self.e2_in, 16)
        self.first_units(lambda e, slot, before, plain: self.split_unit(pool, order, e, slot, before, plain))


def experts(nc, chip, tag, exp, layer, cwT):
    gated, n_units, UPS, WUP, WSLOTS, units = exp.gated, exp.n_units, exp.ups, exp.wup, exp.SLOTS, exp.units
    w_hi, w_lo, pick, w_split, down_mm = exp.w_hi, exp.w_lo, exp.pick, exp.w_split, exp.down_mm
    n = f"e{tag}_"
    with ExitStack() as ctx:
        a = chip.sb(n + "a", [P, 2, HALF], ctx=ctx)
        t = chip.sb(n + "t", [P, 2, HALF], ctx=ctx)
        hf = chip.sb(n + "hf", [P, 2, HALF], ctx=ctx)
        hh = chip.sb(n + "hh", [P, 2, HALF], F32R, ctx)
        hl = chip.sb(n + "hl", [P, 2, HALF], F32R, ctx)
        first_mm, up_mm, pick_mm, a_done, t_done, hf_done, hh_done, hl_done = (
            chip.sem(n + s) for s in ("fm", "um", "bm", "a", "t", "hf", "hh", "hl"))
        block = ctx.enter_context(nc.Block())

        def first(e):
            return isinstance(e, int) and e == 0

        @block.sync
        def _(sp):
            exp.later_units(sp, lambda e, slot, before, plain: exp.load_unit(sp, e, slot, before))

        @block.gpsimd
        def _(pool):
            order = Order(pool, exp.order_sem)
            exp.later_units(pool, lambda e, slot, before, plain:
                            exp.split_unit(pool, order, e, slot, before, plain))

        def up_bank(half):
            return 5 if gated else 4 + half

        def pick_bank(half):
            return 6 if gated else 6 + half

        @block.tensor
        def _(pe):
            def up(e, par, half, plain):
                cols = slice(half * HALF, (half + 1) * HALF)
                u = e * 2 + half
                now = not first(e)
                for m in range(UPS):
                    bank = 4 if gated and m == 0 else up_bank(half)
                    if gated:
                        if now or half:
                            pe.wait_ge(a_done if m == 0 else t_done, u)
                    elif now:
                        pe.wait_ge(a_done, u - 1)
                    three_parts(chip.ps[:, bank, :], nc,
                                lambda k: w_hi[par][:, (m * NC + k) * P:(m * NC + k + 1) * P],
                                lambda k: w_lo[par][:, (m * NC + k) * P:(m * NC + k + 1) * P],
                                lambda k: chip.h_hi[:, k, cols], lambda k: chip.h_lo[:, k, cols],
                                range(NC)).then_inc(first_mm if m == 0 else up_mm, 1)
                if not plain:
                    if gated:
                        if now or half:
                            pe.wait_ge(hf_done, u)
                    elif now:
                        pe.wait_ge(t_done, u - 1)
                    nc.tensor.matmul(chip.ps[:, pick_bank(half), :], pick[par][:], cwT[:, cols],
                                     start=True, stop=True).then_inc(pick_mm, 1)

            def down(e, par, half, last):
                pe.wait_ge(hl_done, e * 2 + (half + 1))
                for c in range(NC):
                    for r, (w, h) in enumerate(((w_hi, hh), (w_hi, hl), (w_lo, hh))):
                        mm = nc.tensor.matmul(chip.ps[:, c * NH + half, :],
                                              w[par][:, WUP + c * P:WUP + (c + 1) * P], h[:, half, :],
                                              start=(first(e) and r == 0), stop=(last and r == 2),
                                              skip_group_check=True)
                mm.then_inc(down_mm, 1)

            def body(e, par, before, plain):
                pe.wait_ge(w_split, e + 1)
                for half in range(2):
                    up(e, par, half, plain)
                    if not first(e):
                        down(e - 1, (par - 1) % WSLOTS, half, False)

            units(pe, body)
            for half in range(2):
                down(n_units - 1, (n_units - 1) % WSLOTS, half, True)

        @block.scalar
        def _(act):
            def body(e, par, before, plain):
                for half in range(2):
                    u = e * 2 + half
                    bank = 4 if gated else 4 + half
                    act.wait_ge(first_mm, u + 1)
                    if not first(e):
                        act.wait_ge(t_done if gated else hf_done, u - 1)
                    nc.scalar.activation(a[:, half, :], chip.ps[:, bank, :], ACT.Silu if gated else ACT.Relu)\
                        .then_inc(a_done, 1)
                    act.wait_ge(hf_done, u + 1)
                    if not first(e):
                        act.wait_ge(down_mm, u - 1)
                    nc.scalar.activation(hh[:, half, :], hf[:, half, :], ACT.Copy).then_inc(hh_done, 1)

            units(act, body)

        @block.vector
        def _(dve):
            def body(e, par, before, plain):
                for half in range(2):
                    u = e * 2 + half
                    dve.wait_ge(a_done, u + 1)
                    if not first(e):
                        dve.wait_ge(hl_done, u - 1)
                    if gated:
                        dve.wait_ge(up_mm, u + 1)
                        nc.vector.tensor_tensor(t[:, half, :], a[:, half, :], chip.ps[:, 5, :], ALU.mult)\
                            .then_inc(t_done, 1)
                        dve.wait_ge(pick_mm, u + 1)
                        dve.wait_ge(t_done, u + 1)
                        nc.vector.tensor_tensor(hf[:, half, :], t[:, half, :], chip.ps[:, 6, :], ALU.mult)\
                            .then_inc(hf_done, 1)
                    elif plain:
                        nc.vector.tensor_tensor(hf[:, half, :], a[:, half, :], a[:, half, :], ALU.mult)\
                            .then_inc(hf_done, 1)
                    else:
                        dve.wait_ge(pick_mm, u + 1)
                        nc.vector.tensor_tensor(t[:, half, :], a[:, half, :], chip.ps[:, 6 + half, :], ALU.mult)\
                            .then_inc(t_done, 1)
                        dve.wait_ge(t_done, u + 1)
                        nc.vector.tensor_tensor(hf[:, half, :], t[:, half, :], a[:, half, :], ALU.mult)\
                            .then_inc(hf_done, 1)
                    dve.wait_ge(hh_done, u + 1)
                    if not first(e):
                        dve.wait_ge(down_mm, u - 1)
                    nc.vector.tensor_tensor(hl[:, half, :], hf[:, half, :], hh[:, half, :].bitcast(F32), ALU.subtract)\
                        .then_inc(hl_done, 1)

            units(dve, body)
            for half in range(NH):
                dve.wait_ge(down_mm, 2 * n_units - 1 + half)
                for c in range(NC):
                    cols = slice(half * HALF, (half + 1) * HALF)
                    nc.vector.scalar_tensor_tensor(chip.xT[:, c, cols], chip.ps[:, c * NH + half, :],
                                                   mod_col(chip, layer, 5, c), chip.xT[:, c, cols], ALU.mult, ALU.add)
class Attention1Weights:
    loaded = False
    SCALE = float(D) ** -0.5

    def __init__(self, nc, chip, ctx, matrices, biases):
        self.nc, self.matrices, self.biases = nc, matrices, biases
        self.raw = chip.sb("b_wraw", [P, 4, NC, D], BF16, ctx)
        self.b_raw = chip.sb("b_braw", [P, 4, LAYERS, NC], BF16, ctx)
        self.w = chip.sb("b_w", [P, 4, NC, D], F32R, ctx)
        self.w_in, self.wo_in, self.b_in, self.w_ready, self.order_sem = (
            chip.sem("b_" + s) for s in ("win", "woin", "bin", "wok", "sord"))

    def load_qkv(self, sp, i):
        for n in range(3):
            sp.dma_start(self.raw[:, n], self.matrices[n][i].rearrange("(k p) n -> p k n", p=P))\
                .then_inc(self.w_in, 16)

    def load_o(self, sp, i):
        sp.dma_start(self.raw[:, 3], self.matrices[3][i].rearrange("(k p) n -> p k n", p=P)).then_inc(self.wo_in, 16)

    def load(self, sp):
        self.load_qkv(sp, 0)
        for n, m in enumerate(self.biases):
            sp.dma_start(self.b_raw[:, n], m.rearrange("l p c -> p l c")).then_inc(self.b_in, 16)
        self.load_o(sp, 0)

    def split(self, pool):
        pool.wait_ge(self.w_in, 48)
        for m in (1, 0, 2):
            if m == 0:
                op = self.nc.gpsimd.tensor_scalar(self.w[:, m], self.raw[:, m], self.SCALE, None, ALU.mult)
            else:
                op = self.nc.gpsimd.tensor_copy(self.w[:, m], self.raw[:, m])
            op.then_inc(self.w_ready, 1)


def attention1(nc, chip, weights):
    ps = chip.ps
    SCALE = weights.SCALE
    LAST = LAYERS - 1
    PJ, VB, OB = 8, NJ // 2, NC * NH
    T_BANK, O_BANK = 4, 6
    FIRST, SECOND = 0, 2
    SLOTS = 3
    with ExitStack() as ctx:
        w_raw, b_raw, w = weights.raw, weights.b_raw, weights.w
        b_all = chip.sb("b_ball", [P, 4, LAYERS, NC], ctx=ctx)
        b = chip.sb("b_b", [P, 4, NC], ctx=ctx)
        gb = chip.sb("b_gb", [P, NC], ctx=ctx)
        qk_hi = chip.sb("b_qkh", [P, 2, NC, T], F32R, ctx)
        qk_lo = chip.sb("b_qkl", [P, 2, NC, T], F32R, ctx)
        v_hi = chip.sb("b_vh", [P, NJ, D], F32R, ctx)
        v_lo = chip.sb("b_vl", [P, NJ, D], F32R, ctx)
        nm = chip.sb("b_nm", [P, SLOTS], ctx=ctx)
        rs = chip.sb("b_rs", [P, SLOTS], ctx=ctx)
        ri = chip.sb("b_ri", [P, SLOTS], ctx=ctx)
        pr = chip.sb("b_p", [P, SLOTS, T], ctx=ctx)
        pt_hi = chip.sb("b_pth", [P, NJ, T], F32R, ctx)
        pt_lo = chip.sb("b_ptl", [P, NJ, T], F32R, ctx)
        a_hi = chip.sb("b_ah", [P, NC, T], F32R, ctx)
        a_lo = chip.sb("b_al", [P, NC, T], F32R, ctx)
        w_in, wo_in, b_in, w_ready = weights.w_in, weights.wo_in, weights.b_in, weights.w_ready
        names = ("wook", "bok", "pj", "pjh", "pjl", "vm", "vh", "vl", "sm", "mx", "ex",
                 "nr", "tm", "th", "tl", "om", "oh", "ol", "fm", "fh", "fl", "ord")
        (wo_ready, b_ready, pj_mm, pj_hi, pj_lo, v_mm, v_his, v_los, s_mm, s_max, s_exp,
         s_norm, t_mm, t_hi, t_lo, o_mm, o_hi, o_lo, f_mm, f_hi, f_lo, osem) = (
            chip.sem("b_" + s, ctx) for s in names)
        block = ctx.enter_context(nc.Block())

        def halfcols(half):
            return slice(half * HALF, (half + 1) * HALF)

        def score_banks(j):
            bank = FIRST if j % 2 else SECOND
            return slice(bank, bank + 2)

        K_FIRST = [(0, 1, 0, 0, FIRST), (1, 1, 1, 0, FIRST + 1)]
        Q_FIRST = [(2, 0, 0, 0, FIRST), (3, 0, 1, 0, FIRST + 1)]
        K_SECOND = [(4, 1, 0, 1, O_BANK), (5, 1, 1, 1, O_BANK + 1)]
        Q_SECOND = [(6, 0, 0, 1, FIRST), (7, 0, 1, 1, FIRST + 1)]

        @block.sync
        def _(sp):
            with sp.Fori(0, LAST) as i:
                sp.wait_ge(w_ready, i * 3 + 3)
                weights.load_qkv(sp, i + 1)
                sp.wait_ge(wo_ready, i + 1)
                weights.load_o(sp, i + 1)

        @block.tensor
        def _(pe):
            def two_parts(out, lhs, rhs):
                n = len(lhs)
                for i in range(n):
                    last = nc.tensor.matmul(out, lhs[i], rhs[i], start=(i == 0), stop=(i == n - 1))
                return last

            def project(blocks):
                for n, m, c, half, bank in blocks:
                    wc = [w[:, m, k, c * P:(c + 1) * P] for k in range(NC)]
                    two_parts(ps[:, bank, :], [wc[0], wc[0], wc[1], wc[1]],
                              [x[:, k, halfcols(half)] for k in range(NC) for x in (chip.h_hi, chip.h_lo)])\
                        .then_inc(pj_mm, 1)

            def project_v(half):
                for bank in range(2):
                    for u in range(2):
                        rows = slice((half * 4 + bank * 2 + u) * P, (half * 4 + bank * 2 + u + 1) * P)
                        last = two_parts(ps[:, T_BANK + bank, u * D:(u + 1) * D],
                                         [x[:, k, rows] for k in range(NC) for x in (chip.h_hi, chip.h_lo)],
                                         [w[:, 2, 0, :], w[:, 2, 0, :], w[:, 2, 1, :], w[:, 2, 1, :]])
                    last.then_inc(v_mm, 1)

            def layer(i, last_layer):
                def scores(j):
                    if j == 0:
                        pe.wait_ge(pj_lo, i * PJ + 6)
                    elif j == 1:
                        pe.wait_ge(pj_lo, i * PJ + PJ)
                    else:
                        pe.wait_ge(s_exp, i * NJ + (j - 1))
                    rows = slice(j * P, (j + 1) * P)
                    for half in range(NH):
                        last = three_parts(ps[:, score_banks(j).start + half, :], nc,
                                           lambda k: qk_hi[:, 0, k, rows], lambda k: qk_lo[:, 0, k, rows],
                                           lambda k: qk_hi[:, 1, k, halfcols(half)],
                                           lambda k: qk_lo[:, 1, k, halfcols(half)], range(NC))
                    last.then_inc(s_mm, 1)

                def turn(j):
                    pe.wait_ge(s_norm, i * NJ + (j + 1))
                    if j == 0:
                        pe.wait_ge(v_los, i * VB + VB)
                    else:
                        pe.wait_ge(t_lo, i * NJ + j)
                    for kt in range(NJ):
                        last = nc.tensor.transpose(ps[:, T_BANK + kt // 4, (kt % 4) * P:(kt % 4 + 1) * P],
                                                   pr[:, j % SLOTS, kt * P:(kt + 1) * P], chip.ident[:])
                    last.then_inc(t_mm, 1)

                def values(half, c):
                    pe.wait_ge(t_lo, i * NJ + 4 * (half + 1))
                    cc = slice(c * P, (c + 1) * P)
                    three_parts(ps[:, O_BANK + c, :], nc,
                                lambda k: v_hi[:, k, cc], lambda k: v_lo[:, k, cc],
                                lambda k: pt_hi[:, k, halfcols(half)], lambda k: pt_lo[:, k, halfcols(half)],
                                range(NJ)).then_inc(o_mm, 1)

                def project_out(half):
                    pe.wait_ge(o_lo, i * OB + NC * (half + 1))
                    if half:
                        pe.wait_ge(f_lo, i * OB + (1 + NC))
                    else:
                        pe.wait_ge(s_exp, i * NJ + 7)
                        pe.wait_ge(wo_ready, i + 1)
                    for c in range(NC):
                        wc = [w[:, 3, k, c * P:(c + 1) * P] for k in range(NC)]
                        two_parts(ps[:, SECOND + c, :], [wc[0], wc[0], wc[1], wc[1]],
                                  [x[:, k, halfcols(half)] for k in range(NC) for x in (a_hi, a_lo)])\
                            .then_inc(f_mm, 1)

                pe.wait_ge(f_lo, i * OB + 1)
                project(K_SECOND)
                pe.wait_ge(pj_lo, i * PJ + 4)
                project(Q_SECOND)
                pe.wait_ge(v_los, i * VB + VB // 2)
                project_v(1)
                for j in range(NJ):
                    scores(j)
                    if j >= 2:
                        turn(j - 2)
                    if j >= NJ - 2:
                        values(0, j - (NJ - 2))
                turn(NJ - 2)
                project_out(0)
                turn(NJ - 1)
                if not last_layer:
                    pe.wait_ge(w_ready, i * 3 + 6)
                    pe.wait_ge(f_lo, i * OB + (1 + NC))
                    pe.wait_ge(s_exp, i * NJ + NJ)
                    project(K_FIRST)
                values(1, 0)
                values(1, 1)
                if not last_layer:
                    project_v(0)
                project_out(1)
                if not last_layer:
                    pe.wait_ge(pj_lo, i * PJ + (PJ + 2))
                    project(Q_FIRST)

            pe.wait_ge(w_ready, 3)
            project(K_FIRST)
            project_v(0)
            pe.wait_ge(pj_lo, 2)
            project(Q_FIRST)
            with pe.Fori(0, LAST) as i:
                layer(i, False)
            layer(LAST, True)

        @block.scalar
        def _(act):
            def take_weights(m, scale, sem):
                nc.scalar.activation(w[:, m], w_raw[:, m], ACT.Copy, scale=scale).then_inc(sem, 1)

            def keep(blocks, i):
                for n, m, c, half, bank in blocks:
                    act.wait_ge(pj_mm, i * PJ + (n + 1))
                    nc.scalar.activation(qk_hi[:, m, c, halfcols(half)], ps[:, bank, :], ACT.Identity,
                                         bias=b[:, m, c:c + 1]).then_inc(pj_hi, 1)

            def keep_v(half, i):
                for bank in range(2):
                    act.wait_ge(v_mm, i * VB + (half * 2 + bank + 1))
                    j = half * 4 + bank * 2
                    nc.scalar.activation(v_hi[:, j:j + 2, :], ps[:, T_BANK + bank, :].rearrange("p (j d) -> p j d", j=2),
                                         ACT.Copy).then_inc(v_his, 1)

            def layer(i, last_layer):
                def exps(j):
                    act.wait_ge(s_max, i * NJ + (j + 1))
                    if j >= SLOTS:
                        act.wait_ge(t_mm, i * NJ + (j - SLOTS + 1))
                    u = j % SLOTS
                    nc.scalar.activation(pr[:, u, :], ps[:, score_banks(j), :], ACT.Exp,
                                         bias=nm[:, u:u + 1], accum_out=rs[:, u:u + 1]).then_inc(s_exp, 1)

                def keep_turned(j):
                    act.wait_ge(t_mm, i * NJ + (j + 1))
                    nc.scalar.activation(pt_hi[:, :, j * P:(j + 1) * P],
                                         ps[:, T_BANK:T_BANK + 2, :].rearrange("p b (k q) -> p (b k) q", q=P),
                                         ACT.Copy).then_inc(t_hi, 1)

                def keep_values(half, c):
                    if half + c == 0:
                        act.wait_ge(b_ready, i * 2 + 2)
                    act.wait_ge(o_mm, i * OB + (half * NC + c + 1))
                    nc.scalar.activation(a_hi[:, c, halfcols(half)], ps[:, O_BANK + c, :], ACT.Identity,
                                         bias=b[:, 2, c:c + 1]).then_inc(o_hi, 1)

                def keep_h(half):
                    for c in range(NC):
                        act.wait_ge(f_mm, i * OB + (half * NC + c + 1))
                        nc.scalar.activation(chip.h_hi[:, c, halfcols(half)], ps[:, SECOND + c, :], ACT.Identity,
                                             bias=b[:, 3, c:c + 1]).then_inc(f_hi, 1)

                keep(K_SECOND, i)
                keep(Q_SECOND, i)
                keep_v(1, i)
                for j in range(NJ):
                    exps(j)
                    if j >= 2:
                        keep_turned(j - 2)
                    if j == 2:
                        act.wait_ge(wo_in, i * 16 + 16)
                        take_weights(3, 1.0, wo_ready)
                    if j in (3, 4, 5) and not last_layer:
                        act.wait_ge(v_mm, i * VB + VB)
                        act.wait_ge(w_in, i * 48 + 96)
                        take_weights(j - 3, SCALE if j == 3 else 1.0, w_ready)
                    if j >= NJ - 2:
                        keep_values(0, j - (NJ - 2))
                keep_turned(NJ - 2)
                if not last_layer:
                    keep_h(0)
                keep_turned(NJ - 1)
                if not last_layer:
                    act.wait_ge(b_ready, i * 2 + 3)
                    keep(K_FIRST, i + 1)
                keep_values(1, 0)
                keep_values(1, 1)
                if not last_layer:
                    keep_v(0, i + 1)
                    keep_h(1)
                    keep(Q_FIRST, i + 1)

            act.wait_ge(b_ready, 1)
            keep(K_FIRST, 0)
            keep_v(0, 0)
            keep(Q_FIRST, 0)
            with act.Fori(0, LAST) as i:
                layer(i, False)
            layer(LAST, True)

        @block.vector
        def _(dve):
            order = Order(dve, osem)
            MARKS = NJ

            def low(dst, psum, bias, hi, sem):
                nc.vector.scalar_tensor_tensor(dst, psum, bias, hi.bitcast(F32), ALU.add, ALU.subtract)\
                    .then_inc(sem, 1)

            def keep(blocks, i):
                for n, m, c, half, bank in blocks:
                    dve.wait_ge(pj_hi, i * PJ + (n + 1))
                    low(qk_lo[:, m, c, halfcols(half)], ps[:, bank, :], b[:, m, c:c + 1],
                        qk_hi[:, m, c, halfcols(half)], pj_lo)

            def keep_v(half, i):
                for bank in range(2):
                    dve.wait_ge(v_his, i * VB + (half * 2 + bank + 1))
                    j = half * 4 + bank * 2
                    nc.vector.tensor_tensor(v_lo[:, j:j + 2, :], ps[:, T_BANK + bank, :].rearrange("p (j d) -> p j d", j=2),
                                            v_hi[:, j:j + 2, :].bitcast(F32), ALU.subtract).then_inc(v_los, 1)

            def take_biases(m, i):
                nc.vector.tensor_copy(b[:, m:m + 2, :], b_all[:, m:m + 2, i, :]).then_inc(b_ready, 1)
                dve.wait_ge(b_ready, i * 2 + (1 if m == 0 else 2))

            def layer(i, last_layer):
                order.done = i * MARKS + base

                def maxima(j):
                    dve.wait_ge(s_mm, i * NJ + (j + 1))
                    u = j % SLOTS
                    nc.vector.tensor_reduce(nm[:, u:u + 1], ps[:, score_banks(j), :], AX.XY, ALU.max, negate=True)\
                        .then_inc(s_max, 1)

                def normalise(j):
                    dve.wait_ge(s_exp, i * NJ + (j + 1))
                    u = j % SLOTS
                    order.link(nc.vector.reciprocal(ri[:, u:u + 1], rs[:, u:u + 1]))
                    nc.vector.tensor_scalar(pr[:, u, :], pr[:, u, :], ri[:, u:u + 1], None, ALU.mult)\
                        .then_inc(s_norm, 1)

                def low_turned(j):
                    dve.wait_ge(t_hi, i * NJ + (j + 1))
                    cols = slice(j * P, (j + 1) * P)
                    nc.vector.tensor_tensor(pt_lo[:, :, cols],
                                            ps[:, T_BANK:T_BANK + 2, :].rearrange("p b (k q) -> p (b k) q", q=P),
                                            pt_hi[:, :, cols].bitcast(F32), ALU.subtract).then_inc(t_lo, 1)

                def low_values(half, c):
                    dve.wait_ge(o_hi, i * OB + (half * NC + c + 1))
                    low(a_lo[:, c, halfcols(half)], ps[:, O_BANK + c, :], b[:, 2, c:c + 1],
                        a_hi[:, c, halfcols(half)], o_lo)

                def low_h(half):
                    for c in range(NC):
                        dve.wait_ge(f_hi, i * OB + (half * NC + c + 1))
                        low(chip.h_lo[:, c, halfcols(half)], ps[:, SECOND + c, :], b[:, 3, c:c + 1],
                            chip.h_hi[:, c, halfcols(half)], f_lo)

                def residual(half):
                    for c in range(NC):
                        dve.wait_ge(f_mm, i * OB + (half * NC + c + 1))
                        nc.vector.scalar_tensor_tensor(chip.xT[:, c, halfcols(half)], ps[:, SECOND + c, :],
                                                       mod_col(chip, 1, 2, c), chip.xT[:, c, halfcols(half)],
                                                       ALU.mult, ALU.add).then_inc(f_lo, 1)

                keep(K_SECOND, i)
                keep(Q_SECOND, i)
                take_biases(2, i)
                if not last_layer:
                    take_biases(0, i + 1)
                keep_v(1, i)
                maxima(0)
                for j in range(1, NJ):
                    maxima(j)
                    normalise(j - 1)
                    if j >= 2:
                        low_turned(j - 2)
                    if j == NJ - 2:
                        low_values(0, 0)
                normalise(NJ - 1)
                if last_layer:
                    order.link(nc.vector.tensor_tensor(gb[:], b[:, 3, :], chip.mods[1][:, 2 * NC:3 * NC], ALU.mult))
                    for c in range(NC):
                        order.mark(nc.vector.tensor_scalar(chip.xT[:, c, :], chip.xT[:, c, :], gb[:, c:c + 1], None,
                                                           ALU.add))
                    order.settle()
                low_values(0, 1)
                low_turned(NJ - 2)
                if last_layer:
                    residual(0)
                else:
                    low_h(0)
                low_turned(NJ - 1)
                if not last_layer:
                    keep(K_FIRST, i + 1)
                low_values(1, 0)
                low_values(1, 1)
                if last_layer:
                    residual(1)
                else:
                    keep_v(0, i + 1)
                    low_h(1)
                    keep(Q_FIRST, i + 1)

            nc.vector.memset(gb[:], 0.0).then_inc(f_lo, 1)
            dve.wait_ge(f_lo, 1)
            dve.wait_ge(b_in, 64)
            order.mark(nc.vector.tensor_scalar(b_all[:, 0], b_raw[:, 0], SCALE, None, ALU.mult))
            order.link(nc.vector.tensor_copy(b_all[:, 1:4], b_raw[:, 1:4]))
            take_biases(0, 0)
            keep(K_FIRST, 0)
            keep_v(0, 0)
            keep(Q_FIRST, 0)
            base = order.done
            with dve.Fori(0, LAST) as i:
                layer(i, False)
            layer(LAST, True)


def store(nc, chip, out):
    with ExitStack() as ctx:
        o = chip.sb("s_o", [P, NJ, D], ctx=ctx)
        turned, kept, stored = (chip.sem("s_" + s, ctx) for s in ("turned", "kept", "stored"))
        block = ctx.enter_context(nc.Block())
        dst = out.rearrange("a (j p) d -> p (a j) d", p=P)

        @block.tensor
        def _(pe):
            for j in range(NJ):
                for c in range(NC):
                    last = nc.tensor.transpose(chip.ps[:, j // 2, (j % 2) * D + c * P:(j % 2) * D + (c + 1) * P],
                                               chip.xT[:, c, j * P:(j + 1) * P], chip.ident[:])
                if j % 2:
                    last.then_inc(turned, 1)

        @block.vector
        def _(dve):
            for b in range(NJ // 2):
                dve.wait_ge(turned, b + 1)
                nc.vector.tensor_copy(o[:, 2 * b:2 * b + 2, :],
                                      chip.ps[:, b, :].rearrange("p (j d) -> p j d", j=2)).then_inc(kept, 1)

        @block.sync
        def _(sp):
            for b in range(2):
                sp.wait_ge(kept, 2 * b + 2)
                sp.dma_start(dst[:, 4 * b:4 * b + 4, :], o[:, 4 * b:4 * b + 4, :]).then_inc(stored, 16)
            sp.wait_ge(stored, 32)


def two_adaln_layers_kernel(nc: bass.Bass, x, c0, wmod0, wq0, wk0, wv0, wo0, router0, router_bias0, experts0,
                            c1, wmod1, wq1, bq1, wk1, bk1, wv1, bv1, wo1, bo1, router1, router_bias1, experts1,
                            ident, rep_q, rep_k, lanes, e2, tri, out):
    with ExitStack() as ctx:
        chip = Chip(nc, ctx)
        with ExitStack() as stage:
            with ExitStack() as start:
                att = Attention0(nc, chip, stage, start, wq0, wk0, wv0, wo0, rep_q, rep_k, lanes)
                mod = Modulation(nc, chip, start, 0, c0, wmod0)
                first_load(nc, chip, x, ident, (mod, att))
                norm(nc, chip, "0a", 0, 0, 1, att, mod)
                attention0_project(nc, chip, att)
            attention0_core(nc, chip, att)
            attention0_output(nc, chip, att)
        with ExitStack() as stage:
            cwT = chip.sb("cwT0", [P, T], F32R, stage)
            router = RouterWeights(nc, chip, stage, "0", router0, router_bias0, tri, E0, G0)
            exp = Experts(nc, chip, stage, "0", experts0, True, 0, e2)
            mod = Modulation(nc, chip, stage, 1, c1, wmod1)
            norm(nc, chip, "0b", 0, 3, 4, router)
            route(nc, chip, "0", router, E0, G0, TOPG0, K0, SCALE0, 1, cwT, exp, mod)
            experts(nc, chip, "0", exp, 0, cwT)
        with ExitStack() as stage:
            weights = Attention1Weights(nc, chip, stage, (wq1, wk1, wv1, wo1), (bq1, bk1, bv1, bo1))
            norm(nc, chip, "1a", 1, 0, 1, weights)
            attention1(nc, chip, weights)
        with ExitStack() as stage:
            cwT = chip.sb("cwT1", [P, T], F32R, stage)
            router = RouterWeights(nc, chip, stage, "1", router1, router_bias1, tri, E1, G1)
            exp = Experts(nc, chip, stage, "1", experts1, False, experts1.shape[0] - E1 // 2, e2)
            norm(nc, chip, "1b", 1, 3, 4, router)
            route(nc, chip, "1", router, E1, G1, TOPG1, K1, SCALE1, 0, cwT, exp)
            experts(nc, chip, "1", exp, 1, cwT)
        store(nc, chip, out)



def shape_constants():
    c = {"ident": np.eye(P, dtype=np.float32)}
    rep_q = np.zeros((P, 2, P), np.float32)
    rep_k = np.zeros((P, KV_HEADS, P), np.float32)
    for h in range(GQ):
        for d in range(DH):
            for r, (q_lo, k_lo) in enumerate(((0, 0), (0, 1), (1, 0))):
                col = h * QUAD + r * DH + d
                for b in range(2):
                    rep_q[64 * q_lo + b * GQ * DH + h * DH + d, b, col] = 1
                for g in range(KV_HEADS):
                    rep_k[64 * k_lo + g * DH + d, g, col] = 1
    lanes = np.zeros((P, 2), np.float32)
    lanes[64:, 0] = -1
    for h in range(GQ):
        lanes[[h * QUAD + M_HI, h * QUAD + M_LO], 1] = 1
    e2 = (np.arange(P)[:, None] % 64 == np.arange(64)[None, :]).astype(np.float32)
    tri = np.broadcast_to(np.tril(np.ones((8, 8), np.float32), -1), (P, 8, 8)).copy()
    return c | {"rep_q": rep_q, "rep_k": rep_k, "lanes": lanes, "e2": e2, "tri": tri}


def gated_weights(gate, up, down, s_gate, s_up, s_down):
    def first(a, s):
        a = np.concatenate([a, s[None]])
        return a.transpose(0, 2, 1).reshape(len(a), NC, P, P).transpose(0, 2, 1, 3).reshape(len(a), P, NC * P)
    last = np.concatenate([down, s_down[None]]).transpose(0, 2, 1)
    return np.ascontiguousarray(np.concatenate([first(gate, s_gate), first(up, s_up), last], axis=2))


def squared_weights(w1, w2, s_up, s_down):
    i = w1.shape[1]
    up = np.concatenate([w1, s_up.reshape(-1, i, D)]).reshape(-1, P, D)
    up = up.transpose(0, 2, 1).reshape(len(up), NC, P, P).transpose(0, 2, 1, 3).reshape(len(up), P, NC * P)
    down = np.concatenate([w2.transpose(0, 2, 1), s_down.T.reshape(-1, i, D)]).reshape(-1, P, D)
    return np.ascontiguousarray(np.concatenate([up, down], axis=2))


def kernel(**inputs):
    import concourse.bacc as bacc
    from concourse.bass_utils import run_bass_kernel_spmd

    a = {k: np.asarray(v) for k, v in inputs.items()}
    cols = lambda v: v.reshape(NC, P).T
    bias = lambda v: v.reshape(LAYERS, NC, P).transpose(0, 2, 1)
    args = {
        "x": a["L0_attn_X"], "c0": cols(a["L0_c"]), "wmod0": a["L0_wmod"],
        "wq0": a["L0_attn_Wq"], "wk0": a["L0_attn_Wk"], "wv0": a["L0_attn_Wv"], "wo0": a["L0_attn_Wo"],
        "router0": a["L0_ffn_gate_weight"].T, "router_bias0": a["L0_ffn_expert_bias"],
        "experts0": gated_weights(a["L0_ffn_gate_proj"], a["L0_ffn_up_proj"], a["L0_ffn_down_proj"],
                                  a["L0_ffn_shared_gate"], a["L0_ffn_shared_up"], a["L0_ffn_shared_down"]),
        "c1": cols(a["L1_c"]), "wmod1": a["L1_wmod"],
        "wq1": a["L1_attn_Wq"], "bq1": bias(a["L1_attn_bq"]), "wk1": a["L1_attn_Wk"], "bk1": bias(a["L1_attn_bk"]),
        "wv1": a["L1_attn_Wv"], "bv1": bias(a["L1_attn_bv"]), "wo1": a["L1_attn_Wo"], "bo1": bias(a["L1_attn_bo"]),
        "router1": a["L1_ffn_gate_w"].T, "router_bias1": a["L1_ffn_gate_bias"],
        "experts1": squared_weights(a["L1_ffn_w1"], a["L1_ffn_w2"], a["L1_ffn_shared_up"], a["L1_ffn_shared_down"]),
    } | shape_constants()
    nc = bacc.Bacc("TRN2", target_bir_lowering=False, num_devices=1)
    arrays, aps = {}, {}
    for name, v in args.items():
        arrays[f"in_{name}"] = v = np.ascontiguousarray(v)
        aps[name] = nc.dram_tensor(f"in_{name}", v.shape, mybir.dt.from_np(v.dtype), kind="ExternalInput").ap()
    aps["out"] = nc.dram_tensor("out_x", (1, T, D), F32, kind="ExternalOutput").ap()
    two_adaln_layers_kernel(nc, **aps)
    r = run_bass_kernel_spmd(nc, [arrays], core_ids=[0])
    return r.results[0]["out_x"]
```

```python
import concourse.bass as bass
from concourse import mybir
from concourse.alu_op_type import AluOpType as ALU
from contextlib import ExitStack
import numpy as np

F32 = mybir.dt.float32
F32R = mybir.dt.float32r
BF16 = mybir.dt.bfloat16
ACT = mybir.ActivationFunctionType
AX = mybir.AxisListType

P = 128
T = 1024
D = 256
NJ = T // P
NC = D // P
HALF = 512
NH = T // HALF
BANKS = 8
EPS = 1e-5

HEADS, KV_HEADS, DH = 32, 8, 8
GQ = HEADS // KV_HEADS
QUAD = 32
M_HI, M_LO = 3 * DH, 3 * DH + 1
VCOLS = DH + 1
BIG = 3.0e38

E0, G0, TOPG0, K0, SCALE0 = 16, 4, 2, 4, 2.5
E1, G1, TOPG1, K1, SCALE1 = 64, 8, 4, 6, 2.5
LAYERS = 4


class Order:

    def __init__(self, eng, sem):
        self.eng, self.sem, self.done, self.peak = eng, sem, 0, 0

    def mark(self, ins):
        ins.then_inc(self.sem, 1)
        self.done = self.done + 1
        return ins

    def settle(self):
        self.eng.wait_ge(self.sem, self.done)

    def link(self, ins):
        self.mark(ins)
        self.settle()


class Chip:

    def __init__(self, nc, ctx):
        self.nc, self.ctx = nc, ctx
        self.ps = ctx.enter_context(nc.psum_tensor("ps", [P, BANKS, HALF], F32))
        self.xT = self.sb("xT", [P, NC, T])
        self.h_hi = self.sb("h_hi", [P, NC, T], F32R)
        self.h_lo = self.sb("h_lo", [P, NC, T], F32R)
        self.ident = self.sb("ident", [P, P])
        self.mods = [self.sb(f"mod{i}", [P, 12]) for i in range(2)]
        self.norm_sems = [self.sem("ln_" + s) for s in ("tok", "var", "sd", "rstd", "xna", "xnd", "back", "hi", "hf", "ord")]
        self.norms = 0
        self.warm, self.warmed = self.sb("warm", [P, 16]), 0

    def sb(self, name, shape, dt=F32, ctx=None):
        return (ctx or self.ctx).enter_context(self.nc.sbuf_tensor(name, shape, dt))

    def sem(self, name):
        return self.ctx.enter_context(self.nc.semaphore(name))

    def keep_busy(self, bank, n):
        for _ in range(n):
            self.nc.tensor.matmul(self.ps[:, bank, :], self.ident[:], self.xT[:, 0, 0:HALF], start=True, stop=True)

    def warm_up(self, function):
        self.nc.scalar.activation(self.warm[:, self.warmed:self.warmed + 1], self.ident[:, 0:1], function)
        self.warmed += 1


def mod_col(chip, layer, which, c):
    return chip.mods[layer][:, which * NC + c:which * NC + c + 1]


class Modulation:
    loaded = False

    def __init__(self, nc, chip, ctx, layer, c_cols, wmod):
        n = f"mo{layer}_"
        self.nc, self.chip, self.mod, self.c_cols, self.wmod = nc, chip, chip.mods[layer], c_cols, wmod
        self.w = chip.sb(n + "w", [P, NC, 6 * D], ctx=ctx)
        self.c_in = chip.sb(n + "c", [P, NC], ctx=ctx)
        self.c_act = chip.sb(n + "ca", [P, NC], ctx=ctx)
        self.tmp = chip.sb(n + "t", [P, 3, 2, NC], ctx=ctx)
        self.w_in, self.c_done, self.act_done, self.mm_done, self.ready, self.order_sem = (
            chip.sem(n + s) for s in ("w_in", "c_in", "act", "mm", "ready", "ord"))

    def load(self, sp):
        sp.dma_start(self.c_in[:], self.c_cols).then_inc(self.c_done, 16)
        sp.dma_start(self.w[:], self.wmod.rearrange("(k p) n -> p k n", p=P)).then_inc(self.w_in, 16)

    def split(self, pool):
        pass

    def activate(self, act):
        act.wait_ge(self.c_done, 16)
        self.nc.scalar.activation(self.c_act[:], self.c_in[:], ACT.Silu).then_inc(self.act_done, 1)

    def products(self, pe, bank):
        pe.wait_ge(self.act_done, 1)
        pe.wait_ge(self.w_in, 16)
        for m in range(6 * NC):
            for k in range(NC):
                last = self.nc.tensor.matmul(self.chip.ps[:, bank, m:m + 1], self.w[:, k, m * P:(m + 1) * P],
                                             self.c_act[:, k:k + 1], start=(k == 0), stop=(k == NC - 1))
        last.then_inc(self.mm_done, 1)

    def columns(self, dve, bank):
        nc, tmp = self.nc, self.tmp
        order = Order(dve, self.order_sem)
        dve.wait_ge(self.mm_done, 1)
        order.link(nc.vector.tensor_copy(self.mod[:], self.chip.ps[:, bank, 0:6 * NC]))
        by_kind = self.mod[:].rearrange("p (w c) -> p w c", c=NC)
        scales, gates = by_kind[:, 1::3, :], by_kind[:, 2::3, :]
        sign, size, minus = (tmp[:, i] for i in range(3))
        order.mark(nc.vector.tensor_scalar(scales, scales, 1.0, None, ALU.add))
        order.mark(nc.vector.tensor_scalar(sign, gates, 0.0, None, ALU.is_ge))
        order.link(nc.vector.tensor_scalar(minus, gates, -1.0, None, ALU.mult))
        order.mark(nc.vector.tensor_scalar(sign, sign, 2.0, -1.0, ALU.mult, ALU.add))
        order.link(nc.vector.tensor_tensor(size, gates, minus, ALU.max))
        order.link(nc.vector.tensor_scalar(size, size, 0.25, None, ALU.max))
        nc.vector.tensor_tensor(gates, sign, size, ALU.mult).then_inc(self.ready, 1)
        dve.wait_ge(self.ready, 1)


def first_load(nc, chip, x, ident, others):
    with ExitStack() as ctx:
        xt = chip.sb("x_tok", [P, NJ, D], ctx=ctx)
        x_in = [chip.sem(f"fl_x{i}") for i in range(NH)]
        id_in, turned = (chip.sem("fl_" + s) for s in ("id", "turned"))
        block = ctx.enter_context(nc.Block())
        xv = x.rearrange("a (j p) d -> p (a j) d", p=P)

        @block.sync
        def _(sp):
            sp.dma_start(chip.ident[:], ident).then_inc(id_in, 16)
            for half in range(NH):
                sp.dma_start(xt[:, half * 4:(half + 1) * 4, :], xv[:, half * 4:(half + 1) * 4, :])\
                    .then_inc(x_in[half], 16)
            for weights in others:
                weights.load(sp)

        @block.tensor
        def _(pe):
            pe.wait_ge(id_in, 16)
            for half in range(NH):
                pe.wait_ge(x_in[half], 16)
                for c in range(NC):
                    for q in range(4):
                        last = nc.tensor.transpose(chip.ps[:, half * NC + c, q * P:(q + 1) * P],
                                                   xt[:, half * 4 + q, c * P:(c + 1) * P], chip.ident[:])
                    last.then_inc(turned, 1)

        @block.vector
        def _(dve):
            for half in range(NH):
                for c in range(NC):
                    dve.wait_ge(turned, half * NC + c + 1)
                    nc.vector.tensor_copy(chip.xT[:, c, half * HALF:(half + 1) * HALF],
                                          chip.ps[:, half * NC + c, :])


def norm(nc, chip, tag, layer, shift, scale, beside, mod=None):
    n = f"ln{tag}_"
    with ExitStack() as ctx:
        xn = chip.sb(n + "xn", [P, NJ, D], ctx=ctx)
        hf = chip.sb(n + "hf", [P, NH * NC, HALF], ctx=ctx)
        st = chip.sb(n + "st", [P, NJ, 6], ctx=ctx)
        mv = chip.sb(n + "mv", [P, NJ, 2], ctx=ctx)
        var, sd, r0, r1 = (chip.sb(n + s, [P, NJ], ctx=ctx) for s in ("var", "sd", "r0", "r1"))
        rstd = chip.sb(n + "rs", [P, NJ], ctx=ctx)
        nmr = chip.sb(n + "nm", [P, NJ], ctx=ctx)
        tok_ready, var_ready, sd_ready, rstd_ready, xn_act, xn_dve, back_ready, hi_ready, hf_ready, order_sem = chip.norm_sems
        k = chip.norms
        chip.norms += 1
        block = ctx.enter_context(nc.Block())

        @block.sync
        def _(sp):
            for weights in beside:
                if not weights.loaded:
                    weights.load(sp)

        @block.gpsimd
        def _(pool):
            for weights in beside:
                weights.split(pool)

        @block.tensor
        def _(pe):
            for j in range(NJ):
                for c in range(NC):
                    last = nc.tensor.transpose(chip.ps[:, j // 2, (j % 2) * D + c * P:(j % 2) * D + (c + 1) * P],
                                               chip.xT[:, c, j * P:(j + 1) * P], chip.ident[:])
                if j % 2:
                    last.then_inc(tok_ready, 1)
            if mod:
                mod.products(pe, BANKS - 1)
            else:
                chip.keep_busy(BANKS - 1, 4)
            for j in range(NJ):
                if mod and j == 4:
                    pe.wait_ge(mod.ready, 1)
                if j % 4 == 0:
                    pe.wait_ge(xn_act, 4 * k + j // 2 + 2)
                    pe.wait_ge(xn_dve, 4 * k + j // 2 + 2)
                for c in range(NC):
                    last = nc.tensor.transpose(chip.ps[:, 4 + (j // 4) * NC + c, (j % 4) * P:(j % 4 + 1) * P],
                                               xn[:, j, c * P:(c + 1) * P], chip.ident[:])
                if j % 4 == 3:
                    last.then_inc(back_ready, 1)
            chip.keep_busy(0, 3)

        @block.vector
        def _(dve):
            order = Order(dve, order_sem)
            order.done = k * (2 * NJ + 5)
            for j in range(NJ):
                if j % 2 == 0:
                    dve.wait_ge(tok_ready, 4 * k + j // 2 + 1)
                order.mark(nc.vector.bn_stats(st[:, j, :], chip.ps[:, j // 2, (j % 2) * D:(j % 2 + 1) * D]))
            order.settle()
            for j in range(NJ):
                last = order.mark(nc.vector.bn_aggr(mv[:, j, :], st[:, j, :]))
            order.settle()
            nc.vector.tensor_scalar(var[:], mv[:, :, 1], EPS, None, ALU.add).then_inc(var_ready, 1)
            dve.wait_ge(sd_ready, k + 1)
            order.link(nc.vector.reciprocal(r0[:], sd[:]))
            order.link(nc.vector.tensor_tensor(r1[:], r0[:], r0[:], ALU.mult))
            order.link(nc.vector.tensor_tensor(r1[:], r1[:], var[:], ALU.mult))
            order.link(nc.vector.tensor_scalar(r1[:], r1[:], -0.5, 1.5, ALU.mult, ALU.add))
            order.link(nc.vector.tensor_tensor(rstd[:], r0[:], r1[:], ALU.mult))
            nc.vector.scalar_tensor_tensor(nmr[:], mv[:, :, 0], -1.0, rstd[:], ALU.mult, ALU.mult)\
                .then_inc(rstd_ready, 1)
            for j in (2, 3, 6, 7):
                nc.vector.tensor_scalar(xn[:, j, :], chip.ps[:, j // 2, (j % 2) * D:(j % 2 + 1) * D],
                                        mv[:, j, 0:1], rstd[:, j:j + 1], ALU.subtract, ALU.mult)\
                    .then_inc(xn_dve, 1)
            if mod:
                mod.columns(dve, BANKS - 1)
            for i in range(NH * NC):
                half, c = i // NC, i % NC
                cols = slice(half * HALF, (half + 1) * HALF)
                if i % 2 == 0:
                    dve.wait_ge(back_ready, 2 * k + half + 1)
                    nc.vector.tensor_scalar(hf[:, i + 1, :], chip.ps[:, 4 + i + 1, :],
                                            mod_col(chip, layer, scale, 1), mod_col(chip, layer, shift, 1),
                                            ALU.mult, ALU.add).then_inc(hf_ready, 1)
                else:
                    dve.wait_ge(hf_ready, 2 * k + half + 1)
                dve.wait_ge(hi_ready, 6 * k + 3 * half + 2 + c)
                nc.vector.tensor_tensor(chip.h_lo[:, c, cols], hf[:, i, :],
                                        chip.h_hi[:, c, cols].bitcast(F32), ALU.subtract)

        @block.scalar
        def _(act):
            if mod:
                mod.activate(act)
            chip.warm_up(ACT.Sqrt)
            act.wait_ge(var_ready, k + 1)
            nc.scalar.activation(sd[:], var[:], ACT.Sqrt).then_inc(sd_ready, 1)
            act.wait_ge(rstd_ready, k + 1)
            for j in (0, 1, 4, 5):
                nc.scalar.activation(xn[:, j, :], chip.ps[:, j // 2, (j % 2) * D:(j % 2 + 1) * D], ACT.Identity,
                                     bias=nmr[:, j:j + 1], scale=rstd[:, j:j + 1]).then_inc(xn_act, 1)
            if mod:
                act.wait_ge(mod.ready, 1)
            for i in range(NH * NC):
                half, c = i // NC, i % NC
                act.wait_ge(back_ready, 2 * k + half + 1)
                if i % 2 == 0:
                    nc.scalar.activation(hf[:, i, :], chip.ps[:, 4 + i, :], ACT.Identity,
                                         bias=mod_col(chip, layer, shift, 0), scale=mod_col(chip, layer, scale, 0))\
                        .then_inc(hi_ready, 1)
                    act.wait_ge(hi_ready, 6 * k + 3 * half + 1)
                else:
                    act.wait_ge(hf_ready, 2 * k + half + 1)
                nc.scalar.activation(chip.h_hi[:, c, half * HALF:(half + 1) * HALF], hf[:, i, :], ACT.Copy)\
                    .then_inc(hi_ready, 1)


def three_parts(pe_out, nc, w_hi, w_lo, m_hi, m_lo, chunks, last_inc=None):
    n = 3 * len(chunks)
    i = 0
    for k in chunks:
        for w, m in ((w_hi, m_hi), (w_hi, m_lo), (w_lo, m_hi)):
            last = nc.tensor.matmul(pe_out, w(k), m(k), start=(i == 0), stop=(i == n - 1))
            i += 1
    return last


class Attention0Weights:
    loaded = True

    def __init__(self, nc, chip, ctx, wq, wk, wv, rep_q, rep_k, lanes):
        self.nc = nc
        self.sources = (wq, 0, D), (wk, D, D + 64), (wv, D + 64, D + 128)
        self.constants = rep_q, rep_k, lanes
        self.raw = chip.sb("ap_w", [P, NC, D + 2 * 64], ctx=ctx)
        self.wd = [chip.sb(f"ap_wd{i}", [P, NC, 5, 2, 64], F32R, ctx) for i in range(2)]
        self.wv = [chip.sb(f"ap_wv{i}", [P, NC, 64], F32R, ctx) for i in range(2)]
        self.rk = chip.sb("ap_rk", [P, KV_HEADS, P], ctx=ctx)
        self.rk_r = chip.sb("ap_rk_r", [P, KV_HEADS, P], F32R, ctx)
        self.rq = chip.sb("ap_rq", [P, 2, P], ctx=ctx)
        self.lane = chip.sb("ap_lane", [P, 2], ctx=ctx)
        self.w_in, self.c_in, self.w_split, self.r_ready, self.order_sem = (
            chip.sem("ap_" + s) for s in ("w", "c", "split", "r", "sord"))

    def load(self, sp):
        rep_q, rep_k, lanes = self.constants
        for w, a, b in self.sources:
            sp.dma_start(self.raw[:, :, a:b], w.rearrange("(k p) n -> p k n", p=P)).then_inc(self.w_in, 16)
        sp.dma_start(self.rk[:], rep_k).then_inc(self.c_in, 16)
        sp.dma_start(self.rq[:], rep_q).then_inc(self.c_in, 16)
        sp.dma_start(self.lane[:], lanes).then_inc(self.c_in, 16)

    def split(self, pool, repq_r, id_r, ident):
        nc, order = self.nc, Order(pool, self.order_sem)
        pool.wait_ge(self.w_in, 48)
        wide = [self.raw[:, k, 0:5 * 64].rearrange("p (t n) -> p t n", t=5).unsqueeze(2).to_broadcast([P, 5, 2, 64])
                for k in range(NC)]
        v = self.raw[:, :, 5 * 64:6 * 64]
        for k in range(NC):
            order.mark(nc.gpsimd.tensor_copy(self.wd[0][:, k], wide[k]))
        order.link(nc.gpsimd.tensor_copy(self.wv[0][:], v))
        for k in range(NC):
            order.mark(nc.gpsimd.tensor_tensor(self.wd[1][:, k], wide[k], self.wd[0][:, k].bitcast(F32),
                                               ALU.subtract))
        order.settle()
        nc.gpsimd.tensor_tensor(self.wv[1][:], v, self.wv[0][:].bitcast(F32), ALU.subtract)\
            .then_inc(self.w_split, 1)
        pool.wait_ge(self.c_in, 48)
        pool.wait_ge(self.w_split, 1)
        order.mark(nc.gpsimd.tensor_copy(self.rk_r[:], self.rk[:]))
        order.mark(nc.gpsimd.tensor_copy(id_r[:], ident[:]))
        order.settle()
        nc.gpsimd.tensor_copy(repq_r[:], self.rq[:]).then_inc(self.r_ready, 1)


class Attention0:
    loaded = True

    def __init__(self, nc, chip, ctx, weights_ctx, wq, wk, wv, wo, rep_q, rep_k, lanes):
        self.nc, self.chip, self.wo = nc, chip, wo
        self.qT = chip.sb("a_qT", [P, 5, T], F32R, ctx)
        self.krep = chip.sb("a_krep", [P, KV_HEADS, T], F32R, ctx)
        self.vall = chip.sb("a_vall", [P, KV_HEADS, NJ, QUAD], ctx=ctx)
        self.repq_r = chip.sb("a_repq_r", [P, 2, P], F32R, ctx)
        self.id_r = chip.sb("a_id_r", [P, P], F32R, ctx)
        self.out = chip.sb("a_out", [P, NJ, D], ctx=ctx)
        self.kk = [chip.sb(f"a_kk{i}", [P, GQ, T], F32R, ctx) for i in range(2)]
        self.wo_raw = chip.sb("a_wo", [P, NC, D], ctx=ctx)
        self.wo_in, self.zeroed, self.kk_done = (chip.sem("a_" + s) for s in ("wo_in", "zeroed", "kk_done"))
        self.weights = Attention0Weights(nc, chip, weights_ctx, wq, wk, wv, rep_q, rep_k, lanes)

    def load(self, sp):
        self.weights.load(sp)
        sp.dma_start(self.wo_raw[:], self.wo.rearrange("(k p) n -> p k n", p=P)).then_inc(self.wo_in, 16)

    def split(self, pool):
        self.weights.split(pool, self.repq_r, self.id_r, self.chip.ident)


def attention0_project(nc, chip, att):
    BANKS_QK = (0, 1, 3)
    NB = len(BANKS_QK)
    with ExitStack() as ctx:
        weights, qT, krep, vall = att.weights, att.qT, att.krep, att.vall
        wd, wvp, rk_r, lane = weights.wd, weights.wv, weights.rk_r, weights.lane
        hi = chip.sb("ap_hi", [P, len(BANKS_QK), HALF], F32R, ctx)
        mm, hi_done, freed, rep_mm, v_mm, rep_a, rep_d, zeroed = (
            chip.sem("ap_" + s) for s in ("mm", "hi", "free", "rmm", "vmm", "ra", "rd", "z"))
        JOBS = [(t, half) for t in (4, 0, 1, 2, 3) for half in range(NH)]
        block = ctx.enter_context(nc.Block())

        @block.gpsimd
        def _(pool):
            nc.gpsimd.memset(vall[:], 0.0).then_inc(zeroed, 1)
            pool.wait_ge(zeroed, 1)
            nc.gpsimd.memset(vall[:, :, :, DH:DH + 1], 1.0).then_inc(zeroed, 1)
            pool.wait_ge(zeroed, 2)
            for kk in att.kk:
                nc.gpsimd.memset(kk[:].bitcast(mybir.dt.uint32), 0).then_inc(att.zeroed, 1)
            pool.wait_ge(att.zeroed, 2)
            pool.wait_ge(rep_a, 1)
            pool.wait_ge(rep_d, 1)
            nc.gpsimd.tensor_copy(att.kk[0][0:QUAD, 0, :], krep[0:QUAD, 0, :]).then_inc(att.kk_done, 1)

        @block.vector
        def _(dve):
            for n, (t, half) in enumerate(JOBS):
                dve.wait_ge(hi_done, n + 1)
                nc.vector.scalar_tensor_tensor(qT[:, t, half * HALF:(half + 1) * HALF],
                                               hi[:, n % NB, :].bitcast(F32), lane[:, 0:1],
                                               chip.ps[:, BANKS_QK[n % NB], :],
                                               ALU.mult, ALU.add).then_inc(freed, 1)
            dve.wait_ge(v_mm, 1)
            dve.wait_ge(zeroed, 2)
            nc.vector.tensor_copy(vall[:, :, :, 0:DH].rearrange("p g j d -> p j g d"),
                                  chip.ps[:, 2, :].rearrange("p (j g d) -> p j g d", j=NJ, g=KV_HEADS))
            for n in range(1, 2 * KV_HEADS, 2):
                dve.wait_ge(rep_mm, n + 1)
                nc.vector.tensor_scalar(krep[:, n // 2, HALF:T], chip.ps[:, 4 + n % 4, :], lane[:, 1:2], None,
                                        ALU.add).then_inc(rep_d, 1)

        @block.scalar
        def _(act):
            for n, (t, half) in enumerate(JOBS):
                act.wait_ge(mm, n + 1)
                if n >= NB:
                    act.wait_ge(freed, n - NB + 1)
                nc.scalar.activation(hi[:, n % NB, :], chip.ps[:, BANKS_QK[n % NB], :], ACT.Copy).then_inc(hi_done, 1)
            for n in range(0, 2 * KV_HEADS, 2):
                act.wait_ge(rep_mm, n + 1)
                nc.scalar.activation(krep[:, n // 2, 0:HALF], chip.ps[:, 4 + n % 4, :], ACT.Identity,
                                     bias=lane[:, 1:2]).then_inc(rep_a, 1)

        @block.tensor
        def _(pe):
            pe.wait_ge(weights.w_split, 1)
            for n, (t, half) in enumerate(JOBS):
                cols = slice(half * HALF, (half + 1) * HALF)
                if n >= NB:
                    pe.wait_ge(freed, n - NB + 1)
                three_parts(chip.ps[:, BANKS_QK[n % NB], :], nc,
                            lambda k: wd[0][:, k, t, :, :], lambda k: wd[1][:, k, t, :, :],
                            lambda k: chip.h_hi[:, k, cols], lambda k: chip.h_lo[:, k, cols],
                            range(NC)).then_inc(mm, 1)
            for j in range(NJ):
                cols = slice(j * P, (j + 1) * P)
                last = three_parts(chip.ps[:, 2, j * 64:(j + 1) * 64], nc,
                                   lambda k: chip.h_hi[:, k, cols], lambda k: chip.h_lo[:, k, cols],
                                   lambda k: wvp[0][:, k, :], lambda k: wvp[1][:, k, :], range(NC))
            last.then_inc(v_mm, 1)
            pe.wait_ge(weights.r_ready, 1)
            for n in range(2 * KV_HEADS):
                if n >= 4:
                    pe.wait_ge(rep_d if n % 2 else rep_a, (n - 4) // 2 + 1)
                nc.tensor.matmul(chip.ps[:, 4 + n % 4, :], rk_r[:, n // 2, :],
                                 qT[:, 4, (n % 2) * HALF:(n % 2 + 1) * HALF], start=True, stop=True)\
                    .then_inc(rep_mm, 1)


def attention0_core(nc, chip, att):
    ps = chip.ps
    STEPS = NH * NJ
    NMAX = GQ * NJ * NH
    PER = NMAX // STEPS
    MID = NJ + 1
    MAX_BANKS, PVB, TRB = (4, 5), 6, 7
    FIRST_BANKS = (5, 4, PVB)
    SLOTS = 4
    SCALE = float(DH) ** -0.5
    LASTG = KV_HEADS - 1
    with ExitStack() as ctx:
        qT, krep, vall, repq_r, id_r, out, kk = att.qT, att.krep, att.vall, att.repq_r, att.id_r, att.out, att.kk
        qa = [chip.sb(f"ac_qa{i}", [P, T], F32R, ctx) for i in range(2)]
        qb = [chip.sb(f"ac_qb{i}", [P, T], F32R, ctx) for i in range(2)]
        vg = [chip.sb(f"ac_vg{i}", [P, NJ, QUAD], ctx=ctx) for i in range(2)]
        probs = chip.sb("ac_p", [P, SLOTS, GQ, HALF], ctx=ctx)
        ot = chip.sb("ac_ot", [P, 2, HALF], ctx=ctx)
        mxp = chip.sb("ac_mxp", [P, NJ, GQ, NH], ctx=ctx)
        nm = chip.sb("ac_nm", [P, NJ, GQ], ctx=ctx)
        m4 = chip.sb("ac_m4", [P, NJ, P], F32R, ctx)
        rinv = chip.sb("ac_ri", [P, 4, GQ], ctx=ctx)
        names = ("score_mm", "exp_done", "pv_mm", "o_out", "o_turned", "o_done", "max_mm", "max_done", "m_ready",
                 "qa_mm", "qa_done", "qb_mm", "qb_done", "vg_done", "zeroed", "ord")
        (score_mm, exp_done, pv_mm, o_out, o_turned, o_done, max_mm, max_done, m_ready,
         qa_mm, qa_done, qb_mm, qb_done, vg_done, zeroed, order_sem) = (
            chip.sem("ac_" + s) for s in names)
        kk_done = att.kk_done
        m4q = m4[:].rearrange("p j (h r) -> p j h r", h=GQ)
        block = ctx.enter_context(nc.Block())

        def groups(eng, body):
            body(0, 0, 0, 1)
            with eng.Fori(0, (KV_HEADS - 2) // 2) as i:
                for u in range(2):
                    body(i * 2 + (1 + u), (1 + u) % 2, i + 1, i + (1 + (1 + u) // 2))
            body(LASTG, LASTG % 2, None, None)

        def is_first(g):
            return isinstance(g, int) and g == 0

        def is_last(g):
            return isinstance(g, int) and g == LASTG

        def block_of(n):
            qh, r = divmod(n, NMAX // 2)
            h, r = divmod(r, NMAX // 2 // GQ)
            return h, qh * (NJ // 2) + r // NH, r % NH

        def blocks_at(g, step):
            if step == 0:
                return [] if is_first(g) else [(0, n) for n in range(NMAX - PER, NMAX)]
            if is_last(g):
                return []
            return [(1, n) for n in range((step - 1) * PER, step * PER)]

        def pair_of(g, par, pair1):
            return LASTG // 2 if is_last(g) else (pair1 if par == 0 else pair1 - 1)

        @block.tensor
        def _(pe):
            def max_block(slot, n, banks=MAX_BANKS):
                h, j, half = block_of(n)
                nc.tensor.matmul(ps[:, banks[n % len(banks)], :], qa[slot][:, j * P:(j + 1) * P],
                                 kk[slot][:, h, half * HALF:(half + 1) * HALF], start=True, stop=True)\
                    .then_inc(max_mm, 1)

            def spread_q(pair, par, half, bank=TRB):
                nc.tensor.matmul(ps[:, bank, :], repq_r[:, par, :], qT[:, pair, half * HALF:(half + 1) * HALF],
                                 start=True, stop=True).then_inc(qa_mm, 1)

            def spread_q_max(pair, par, half):
                for q in range(4):
                    cols = slice(half * HALF + q * P, half * HALF + (q + 1) * P)
                    nc.tensor.matmul(ps[:, TRB, q * P:(q + 1) * P], repq_r[:, par, :], qT[:, pair, cols],
                                     start=True, stop=False)
                    last = nc.tensor.matmul(ps[:, TRB, q * P:(q + 1) * P], m4[:, half * 4 + q, :], id_r[:],
                                            start=False, stop=True)
                last.then_inc(qb_mm, 1)

            def turn(g, qh):
                pe.wait_ge(o_out, g * NH + (qh + 1))
                for q in range(4):
                    last = nc.tensor.transpose(ps[:, TRB, q * P:(q + 1) * P], ot[:, qh, q * P:(q + 1) * P],
                                               chip.ident[:])
                last.then_inc(o_turned, 1)

            def values(g, par, s, part):
                if part == 0:
                    pe.wait_ge(exp_done, g * (2 * STEPS) + 2 * (s + 1))
                    if s == 0 and not is_first(g):
                        pe.wait_ge(o_out, g * NH)
                    if s == NJ:
                        pe.wait_ge(o_out, g * NH + 1)
                    if s == 0:
                        pe.wait_ge(vg_done, g + 1)
                cols = slice(part * (HALF // 2), (part + 1) * (HALF // 2))
                for h in range(GQ):
                    last = nc.tensor.matmul(ps[h * QUAD:(h + 1) * QUAD, PVB, cols], vg[par][:, s % NJ, :],
                                            probs[:, s % SLOTS, h, cols], start=(s % NJ == 0 and part == 0),
                                            stop=(s % NJ == NJ - 1), skip_group_check=True)
                if part:
                    last.then_inc(pv_mm, 1)

            for G in range(2):
                for half in range(NH):
                    spread_q(0, G, half, 2 * G + half)
            pe.wait_ge(qa_done, NH)
            pe.wait_ge(zeroed, 1)
            pe.wait_ge(att.zeroed, 2)
            for n in range(NMAX):
                if n == 0 or block_of(n)[0] > block_of(n - 1)[0]:
                    pe.wait_ge(kk_done, block_of(n)[0] + 1)
                if n >= len(FIRST_BANKS):
                    pe.wait_ge(max_done, n - len(FIRST_BANKS) + 1)
                max_block(0, n, FIRST_BANKS)
            for half in range(NH):
                pe.wait_ge(m_ready, half + 1)
                if half:
                    pe.wait_ge(qb_done, half)
                spread_q_max(0, 0, half)

            def body(g, par, pair1, pair2):
                nxt = 1 - par

                def some_max(step, lots):
                    for who, n in lots:
                        if who:
                            if n == 0:
                                pe.wait_ge(qa_done, g * 2 + 4)
                            if n < NMAX // 2 and (n == 0 or block_of(n)[0] > block_of(n - 1)[0]):
                                pe.wait_ge(kk_done, g * GQ + (GQ + block_of(n)[0] + 1))
                        pe.wait_ge(max_done, g * NMAX + (who * NMAX + n - 1))
                        max_block(nxt if who else par, n)

                for step in range(STEPS):
                    qh, kt = step // NJ, step % NJ
                    lots = blocks_at(g, step)
                    if step == 0:
                        pe.wait_ge(qb_done, g * 2 + 1)
                        pe.wait_ge(kk_done, g * GQ + GQ)
                    if step == NJ:
                        pe.wait_ge(qb_done, g * 2 + 2)
                    for pair in range(2):
                        if step or not is_first(g):
                            pe.wait_ge(exp_done, g * (2 * STEPS) + (2 * step + pair - 1))
                        for h in (2 * pair, 2 * pair + 1):
                            last = nc.tensor.matmul(ps[:, h, :], kk[par][:, h, kt * P:(kt + 1) * P],
                                                    qb[par][:, qh * HALF:(qh + 1) * HALF], start=True, stop=True)
                        last.then_inc(score_mm, 1)
                        some_max(step, lots[2 * pair:2 * pair + 1])
                        if step >= 2:
                            values(g, par, step - 2, pair)
                        elif not is_first(g):
                            values(g - 1, nxt, STEPS - 2 + step, pair)
                        some_max(step, lots[2 * pair + 1:2 * pair + 2])
                    if step == 2 and not is_first(g):
                        pe.wait_ge(m_ready, g * 2 + 2)
                        pe.wait_ge(o_done, g * NH)
                        spread_q_max(pair_of(g, par, pair1), par, 1)
                    if step == 4 and not is_first(g):
                        pe.wait_ge(qb_done, g * 2 + 2)
                        turn(g - 1, 1)
                    if step == 6 and not is_last(g):
                        if is_first(g):
                            pe.wait_ge(qb_done, 2)
                        pe.wait_ge(o_done, g * NH + 1)
                        spread_q(pair2, par, 0)
                    if step == 7 and not is_last(g):
                        pe.wait_ge(qa_done, g * 2 + 5)
                        spread_q(pair2, par, 1)
                    if step == MID + 1 and not is_last(g):
                        pe.wait_ge(m_ready, g * 2 + 3)
                        pe.wait_ge(qa_done, g * 2 + 6)
                        spread_q_max(pair1, nxt, 0)
                    if step == MID + 3:
                        if not is_last(g):
                            pe.wait_ge(qb_done, g * 2 + 3)
                        else:
                            pe.wait_ge(o_done, g * NH + 1)
                        turn(g, 0)

            groups(pe, body)
            for s in (STEPS - 2, STEPS - 1):
                for part in range(2):
                    values(LASTG, LASTG % 2, s, part)
            pe.wait_ge(o_done, LASTG * NH + 2)
            turn(LASTG, 1)

        @block.scalar
        def _(act):
            def keep_q(dst, sem, done, value, half, bank=TRB):
                act.wait_ge(sem, value)
                nc.scalar.activation(dst[:, half * HALF:(half + 1) * HALF], ps[:, bank, :], ACT.Copy)\
                    .then_inc(done, 1)

            chip.warm_up(ACT.Exp)
            for G in range(2):
                for half in range(NH):
                    keep_q(qa[G], qa_mm, qa_done, 2 * G + half + 1, half, 2 * G + half)
            for half in range(NH):
                keep_q(qb[0], qb_mm, qb_done, half + 1, half)

            def values_out(g, qh):
                act.wait_ge(pv_mm, g * STEPS + (qh + 1) * NJ)
                if qh:
                    act.wait_ge(o_turned, g * NH + 1)
                elif not is_first(g):
                    act.wait_ge(o_turned, g * NH - 1)
                nc.scalar.activation(ot[:, qh, :], ps[:, PVB, :], ACT.Copy).then_inc(o_out, 1)

            def body(g, par, pair1, pair2):
                nxt = 1 - par
                for step in range(STEPS):
                    for pair in range(2):
                        act.wait_ge(score_mm, g * (2 * STEPS) + (2 * step + pair + 1))
                        if pair == 0 and (step >= SLOTS or not is_first(g)):
                            act.wait_ge(pv_mm, g * STEPS + (step - SLOTS + 1))
                        nc.scalar.activation(probs[:, step % SLOTS, 2 * pair:2 * pair + 2, :],
                                             ps[:, 2 * pair:2 * pair + 2, :], ACT.Exp, scale=SCALE)\
                            .then_inc(exp_done, 1)
                    if step == 1 and not is_first(g):
                        values_out(g - 1, 1)
                    if step == 3 and not is_first(g):
                        keep_q(qb[par], qb_mm, qb_done, g * 2 + 2, 1)
                    if step in (7, 8) and not is_last(g):
                        keep_q(qa[par], qa_mm, qa_done, g * 2 + (step - 7) + 5, step - 7)
                    if step == NJ + 1:
                        values_out(g, 0)
                    if step == MID + 2 and not is_last(g):
                        keep_q(qb[nxt], qb_mm, qb_done, g * 2 + 3, 0)

            groups(act, body)
            values_out(LASTG, 1)

        @block.vector
        def _(dve):
            order = Order(dve, order_sem)

            def find_max(base, n, banks=MAX_BANKS):
                h, j, half = block_of(n)
                dve.wait_ge(max_mm, base + (n + 1))
                nc.vector.tensor_reduce(mxp[:, j, h, half:half + 1], ps[:, banks[n % len(banks)], :], AX.X, ALU.max)\
                    .then_inc(max_done, 1)

            def negate(base, qh, m4_used):
                js = slice(qh * (NJ // 2), (qh + 1) * (NJ // 2))
                dve.wait_ge(max_done, base + (qh + 1) * (NMAX // 2))
                if m4_used is not None:
                    dve.wait_ge(qb_mm, m4_used)
                order.link(nc.vector.tensor_reduce(nm[:, js], mxp[:, js], AX.X, ALU.max, negate=True))
                order.link(nc.vector.tensor_copy(m4q[:, js, :, M_HI], nm[:, js]))
                nc.vector.tensor_tensor(m4q[:, js, :, M_LO], nm[:, js], m4q[:, js, :, M_HI].bitcast(F32),
                                        ALU.subtract).then_inc(m_ready, 1)

            def outputs(g, qh):
                dve.wait_ge(o_turned, g * NH + (qh + 1))
                turned = ps[:, TRB, :].rearrange("p (q h r) -> p q h r", q=4, h=GQ)
                order.link(nc.vector.reciprocal(rinv[:], turned[:, :, :, DH]))
                cols = out[:, qh * 4:(qh + 1) * 4, bass.ds(g * (GQ * DH), GQ * DH)]
                nc.vector.tensor_tensor(cols.rearrange("p q (h d) -> p q h d", h=GQ), turned[:, :, :, 0:DH],
                                        rinv[:].unsqueeze(3).to_broadcast([P, 4, GQ, DH]), ALU.mult)\
                    .then_inc(o_done, 1)

            nc.vector.memset(m4[:].bitcast(mybir.dt.uint32), 0).then_inc(zeroed, 1)
            dve.wait_ge(zeroed, 1)
            for qh in range(2):
                for n in range(qh * (NMAX // 2), (qh + 1) * (NMAX // 2)):
                    find_max(0, n, FIRST_BANKS)
                negate(0, qh, None)
            nc.vector.memset(rinv[:], 0.0).then_inc(o_done, 1)
            dve.wait_ge(o_done, 1)
            base = order.done
            MARKS = 2 * 2 + 2

            def body(g, par, pair1, pair2):
                order.done = base if is_first(g) else g * MARKS + (base - 3)
                for step in range(STEPS):
                    for who, n in blocks_at(g, step):
                        find_max(g * NMAX + who * NMAX, n)
                    if step == 0 and not is_first(g):
                        negate(g * NMAX, 1, g * 2)
                    if step == 4 and not is_first(g):
                        outputs(g - 1, 1)
                    if step == MID and not is_last(g):
                        negate(g * NMAX + NMAX, 0, g * 2 + 2)
                    if step == MID + 3:
                        outputs(g, 0)

            groups(dve, body)
            outputs(LASTG, 1)

        @block.gpsimd
        def _(pool):
            pool.wait_ge(att.zeroed, 2)

            def keep_kv(G, slot, heads=range(GQ)):
                for h in heads:
                    rows = slice(h * QUAD, (h + 1) * QUAD)
                    nc.gpsimd.tensor_copy(kk[slot][rows, h, :], krep[rows, G, :]).then_inc(kk_done, 1)

            keep_kv(0, 0, range(1, GQ))
            pool.wait_ge(kk_done, GQ)
            nc.gpsimd.tensor_copy(vg[0][:], vall[:, 0, :, :]).then_inc(vg_done, 1)

            def body(g, par, pair1, pair2):
                if not is_last(g):
                    if is_first(g):
                        pool.wait_ge(vg_done, 1)
                    else:
                        pool.wait_ge(score_mm, g * (2 * STEPS))
                        pool.wait_ge(vg_done, g + 1)
                        pool.wait_ge(att.zeroed, 2)
                    keep_kv(g + 1, 1 - par)
                    if not is_first(g):
                        pool.wait_ge(pv_mm, g * STEPS)
                    pool.wait_ge(kk_done, g * GQ + 2 * GQ)
                    pool.wait_ge(att.zeroed, 2)
                    nc.gpsimd.tensor_copy(vg[1 - par][:], vall[:, g + 1, :, :]).then_inc(vg_done, 1)

            groups(pool, body)


def attention0_output(nc, chip, att):
    with ExitStack() as ctx:
        w_raw, out = att.wo_raw, att.out
        w_hi = chip.sb("ao_wh", [P, NC, D], F32R, ctx)
        w_lo = chip.sb("ao_wl", [P, NC, D], F32R, ctx)
        w_split, turned, hi_done, lo_done, mm, order_sem = (
            chip.sem("ao_" + s) for s in ("ws", "turned", "hi", "lo", "mm", "ord"))
        block = ctx.enter_context(nc.Block())

        @block.vector
        def _(dve):
            order = Order(dve, order_sem)
            dve.wait_ge(att.wo_in, 16)
            order.link(nc.vector.tensor_copy(w_hi[:], w_raw[:]))
            nc.vector.tensor_tensor(w_lo[:], w_raw[:], w_hi[:].bitcast(F32), ALU.subtract).then_inc(w_split, 1)
            for i in range(NH * NC):
                half, c = i // NC, i % NC
                cols = slice(half * HALF, (half + 1) * HALF)
                dve.wait_ge(hi_done, i + 1)
                nc.vector.tensor_tensor(chip.h_lo[:, c, cols], chip.ps[:, i, :], chip.h_hi[:, c, cols].bitcast(F32),
                                        ALU.subtract).then_inc(lo_done, 1)
            for i in range(NH * NC):
                half, c = i // NC, i % NC
                cols = slice(half * HALF, (half + 1) * HALF)
                dve.wait_ge(mm, i + 1)
                nc.vector.scalar_tensor_tensor(chip.xT[:, c, cols], chip.ps[:, 4 + i, :], mod_col(chip, 0, 2, c),
                                               chip.xT[:, c, cols], ALU.mult, ALU.add)

        @block.scalar
        def _(act):
            for i in range(NH * NC):
                half, c = i // NC, i % NC
                act.wait_ge(turned, i + 1)
                nc.scalar.activation(chip.h_hi[:, c, half * HALF:(half + 1) * HALF], chip.ps[:, i, :], ACT.Copy)\
                    .then_inc(hi_done, 1)

        @block.tensor
        def _(pe):
            for half in range(NH):
                for c in range(NC):
                    for q in range(4):
                        last = nc.tensor.transpose(chip.ps[:, half * NC + c, q * P:(q + 1) * P],
                                                   out[:, half * 4 + q, c * P:(c + 1) * P], chip.ident[:])
                    last.then_inc(turned, 1)
            pe.wait_ge(w_split, 1)
            for i in range(NH * NC):
                half, c = i // NC, i % NC
                cols = slice(half * HALF, (half + 1) * HALF)
                pe.wait_ge(lo_done, (half + 1) * NC)
                three_parts(chip.ps[:, 4 + i, :], nc,
                            lambda k: w_hi[:, k, c * P:(c + 1) * P], lambda k: w_lo[:, k, c * P:(c + 1) * P],
                            lambda k: chip.h_hi[:, k, cols], lambda k: chip.h_lo[:, k, cols],
                            range(NC)).then_inc(mm, 1)


class Router:
    loaded = False
    BANK = 6

    def __init__(self, nc, chip, ctx, tag, gate_w, gate_b, tri, n_experts, n_groups, top_groups, top_k, scaling):
        self.nc, self.chip, self.sources, E, G = nc, chip, (gate_w, gate_b, tri), n_experts, n_groups
        self.E, self.G, self.top_groups, self.top_k, self.scaling = E, G, top_groups, top_k, scaling
        ES, JG = E // G, NJ * G
        n = f"r{tag}_"
        sb = lambda name, shape, dt=F32: chip.sb(n + name, shape, dt, ctx)
        self.raw, self.hi, self.lo = sb("w", [P, NC, E]), sb("wh", [P, NC, E], F32R), sb("wl", [P, NC, E], F32R)
        self.bias, self.tri = sb("b", [P, E]), sb("tri", [P, G, G])
        self.cwT = sb("cwT", [P, T], F32R)
        self.score, self.biased = sb("s", [P, NJ, E]), sb("sb", [P, NJ, E])
        self.top = [[sb(f"t{lv}{i}", [P, JG, ES >> (lv + 1)]) for i in range(4)] for lv in range(ES.bit_length() - 1)]
        self.gsum, self.gmask, self.gfill = sb("g", [P, NJ, G]), sb("gm", [P, NJ, G]), sb("gf", [P, NJ, G])
        self.cmp_a, self.cmp_b = sb("ca", [P, NJ, G, G]), sb("cb", [P, NJ, G, G])
        self.masked, self.replaced, self.best = sb("m", [P, NJ, E]), sb("rp", [P, NJ, E]), sb("v8", [P, NJ, 8])
        self.wsum, self.winv = sb("ws", [P, NJ]), sb("wi", [P, NJ])
        self.cw = sb("cw", [P, NJ, P], F32R)
        self.scoreT = sb("sT", [E, T])
        (self.w_in, self.b_in, self.w_split, self.split_order, self.logit_mm, self.sig_done, self.score_turned,
         self.kept, self.cw_ready, self.turned, self.ready, self.order_sem) = (
            chip.sem(n + s) for s in ("w", "b", "ws", "so", "lg", "sg", "st", "kp", "cwr", "tu", "rdy", "ord"))

    def load(self, sp):
        gate_w, gate_b, tri = self.sources
        E, G = self.E, self.G
        sp.dma_start(self.raw[:], gate_w.rearrange("(k p) n -> p k n", p=P)).then_inc(self.w_in, 16)
        sp.dma_start(self.bias[:], gate_b.rearrange("(a e) -> a e", a=1).to_broadcast([P, E])).then_inc(self.b_in, 16)
        sp.dma_start(self.tri[:], tri[:, 0:G, 0:G]).then_inc(self.b_in, 16)

    def split(self, pool):
        order = Order(pool, self.split_order)
        pool.wait_ge(self.w_in, 16)
        order.link(self.nc.gpsimd.tensor_copy(self.hi[:], self.raw[:]))
        self.nc.gpsimd.tensor_tensor(self.lo[:], self.raw[:], self.hi[:].bitcast(F32), ALU.subtract)\
            .then_inc(self.w_split, 1)

    def logits(self, pe):
        chip, E = self.chip, self.E
        pe.wait_ge(self.w_split, 1)
        for half in range(NH):
            cols = slice(half * HALF, (half + 1) * HALF)
            three_parts(chip.ps[0:E, self.BANK + half, :], self.nc,
                        lambda k: self.hi[:, k, :], lambda k: self.lo[:, k, :],
                        lambda k: chip.h_hi[:, k, cols], lambda k: chip.h_lo[:, k, cols],
                        range(NC)).then_inc(self.logit_mm, 1)

    def turn_scores(self, pe):
        for j in range(NJ):
            if j % 4 == 0:
                pe.wait_ge(self.sig_done, j // 4 + 1)
            last = self.nc.tensor.transpose(self.chip.ps[:, self.BANK, j * self.E:(j + 1) * self.E],
                                            self.scoreT[:, j * P:(j + 1) * P], self.chip.ident[0:self.E, 0:self.E])
        last.then_inc(self.score_turned, 1)

    def turn(self, pe):
        pe.wait_ge(self.cw_ready, 1)
        for j in range(NJ):
            last = self.nc.tensor.transpose(self.chip.ps[:, self.BANK + j // 4, (j % 4) * P:(j % 4 + 1) * P],
                                            self.cw[:, j, :].bitcast(F32), self.chip.ident[:])
            if j % 4 == 3:
                last.then_inc(self.turned, 1)

    def scores(self, act):
        for half in range(NH):
            act.wait_ge(self.logit_mm, half + 1)
            self.nc.scalar.activation(self.scoreT[:, half * HALF:(half + 1) * HALF],
                                      self.chip.ps[0:self.E, self.BANK + half, :], ACT.Sigmoid)\
                .then_inc(self.sig_done, 1)

    def choose(self, dve, between):
        nc, E, G, top, top_groups, top_k, scaling = (self.nc, self.E, self.G, self.top, self.top_groups,
                                                     self.top_k, self.scaling)
        ES, JG = E // G, NJ * G
        score, biased, bias, tri_t, gsum, gmask, gfill, cmp_a, cmp_b, masked, replaced, best, wsum, winv, cw = (
            self.score, self.biased, self.bias, self.tri, self.gsum, self.gmask, self.gfill, self.cmp_a, self.cmp_b,
            self.masked, self.replaced, self.best, self.wsum, self.winv, self.cw)
        order = Order(dve, self.order_sem)
        tt, ts = nc.vector.tensor_tensor, nc.vector.tensor_scalar
        order.mark(nc.vector.memset(cw[:].bitcast(mybir.dt.uint32), 0))
        dve.wait_ge(self.b_in, 32)
        dve.wait_ge(self.score_turned, 1)
        turned = self.chip.ps[:, self.BANK, 0:NJ * E].rearrange("p (j e) -> p j e", j=NJ)
        order.link(tt(biased[:], turned, bias[:].unsqueeze(1).to_broadcast([P, NJ, E]), ALU.add))
        nc.vector.tensor_copy(score[:], turned).then_inc(self.kept, 1)
        b = biased[:].rearrange("p j (g e) -> p (j g) e", g=G)
        a0, a1 = b[:, :, 0::2], b[:, :, 1::2]
        order.mark(tt(top[0][0][:], a0, a1, ALU.max))
        order.link(tt(top[0][1][:], a0, a1, ALU.min))
        for lv in range(1, len(top)):
            hi, lo = top[lv - 1][0], top[lv - 1][1]
            order.mark(tt(top[lv][2][:], hi[:, :, 0::2], hi[:, :, 1::2], ALU.min))
            order.mark(tt(top[lv][3][:], lo[:, :, 0::2], lo[:, :, 1::2], ALU.max))
            order.link(tt(top[lv][0][:], hi[:, :, 0::2], hi[:, :, 1::2], ALU.max))
            order.link(tt(top[lv][1][:], top[lv][2][:], top[lv][3][:], ALU.max))
        between()
        order.link(tt(gsum[:].rearrange("p j g -> p (j g)"), top[-1][0][:, :, 0], top[-1][1][:, :, 0], ALU.add))
        between()
        other = gsum[:].unsqueeze(2).to_broadcast([P, NJ, G, G])
        own = gsum[:].unsqueeze(3).to_broadcast([P, NJ, G, G])
        order.mark(tt(cmp_a[:], other, own, ALU.is_gt))
        order.link(tt(cmp_b[:], other, own, ALU.is_ge))
        order.link(tt(cmp_b[:], cmp_b[:], tri_t[:].unsqueeze(1).to_broadcast([P, NJ, G, G]), ALU.mult))
        between()
        order.link(tt(cmp_a[:], cmp_a[:], cmp_b[:], ALU.max))
        order.link(nc.vector.tensor_reduce(gmask[:], cmp_a[:], AX.X, ALU.add))
        order.link(ts(gmask[:], gmask[:], float(top_groups), None, ALU.is_lt))
        between()
        order.link(ts(gfill[:], gmask[:], BIG, -BIG, ALU.mult, ALU.add))
        m4 = masked[:].rearrange("p j (g e) -> p (j g) e", g=G)
        wide = [P, JG, ES]
        order.link(tt(m4, b, gmask[:].rearrange("p j g -> p (j g)").unsqueeze(2).to_broadcast(wide), ALU.mult))
        order.link(tt(m4, m4, gfill[:].rearrange("p j g -> p (j g)").unsqueeze(2).to_broadcast(wide), ALU.add))
        between()
        for j in range(NJ):
            order.mark(nc.vector.max(best[:, j, :], masked[:, j, :]))
        order.settle()
        between()
        order.link(nc.vector.memset(best[:, :, top_k:8], -BIG))
        for j in range(NJ):
            order.mark(nc.vector.match_replace(replaced[:, j, :], best[:, j, :], masked[:, j, :], -BIG))
        order.settle()
        between()
        order.link(tt(masked[:], masked[:], replaced[:], ALU.not_equal))
        dve.wait_ge(self.kept, 1)
        order.link(tt(masked[:], masked[:], score[:], ALU.mult))
        order.link(nc.vector.tensor_reduce(wsum[:], masked[:], AX.X, ALU.add))
        order.link(ts(wsum[:], wsum[:], 1e-20, None, ALU.add))
        order.link(nc.vector.reciprocal(winv[:], wsum[:]))
        order.link(ts(winv[:], winv[:], scaling, None, ALU.mult))
        between()
        order.link(tt(masked[:], masked[:], winv[:].unsqueeze(2).to_broadcast([P, NJ, E]), ALU.mult))
        order.link(nc.vector.tensor_copy(cw[:, :, 0:E], masked[:]))
        order.link(tt(cw[:, :, 64:64 + E], masked[:], cw[:, :, 0:E].bitcast(F32), ALU.subtract))
        nc.vector.tensor_copy(winv[:], wsum[:]).then_inc(self.cw_ready, 1)

    def keep(self, dve):
        for half in range(NH):
            dve.wait_ge(self.turned, half + 1)
            self.nc.vector.tensor_copy(self.cwT[:, half * HALF:(half + 1) * HALF],
                                       self.chip.ps[:, self.BANK + half, :]).then_inc(self.ready, 1)


class Experts:
    loaded = False
    SLOTS = 3

    def __init__(self, nc, chip, ctx, tag, source, gated, n_plain, e2):
        self.nc, self.source, self.gated, self.n_plain, self.e2 = nc, source, gated, n_plain, e2
        self.n_units = source.shape[0]
        self.ups = 2 if gated else 1
        self.wup = self.ups * NC * P
        wall = self.wup + D
        n = f"e{tag}_"
        self.raw = [chip.sb(f"{n}raw{i}", [P, wall], ctx=ctx) for i in range(self.SLOTS)]
        self.w_hi = [chip.sb(f"{n}wh{i}", [P, wall], F32R, ctx) for i in range(self.SLOTS)]
        self.w_lo = [chip.sb(f"{n}wl{i}", [P, wall], F32R, ctx) for i in range(self.SLOTS)]
        self.pick = [chip.sb(f"{n}pk{i}", [P, P], F32R, ctx) for i in range(self.SLOTS)]
        self.e2_t = chip.sb(n + "e2", [P, 64], ctx=ctx)
        self.zero = chip.sb(n + "zero", [P, 1], ctx=ctx)
        self.w_in = [chip.sem(f"{n}win{i}") for i in range(self.SLOTS)]
        self.e2_in, self.w_split, self.down_mm, self.order_sem = (chip.sem(n + s) for s in ("e2", "ws", "dm", "po"))
        self.loops = (self.n_units - self.SLOTS) // self.SLOTS

    def first_units(self, body):
        for e in range(self.SLOTS):
            body(e, e, 0, e < self.n_plain)

    def later_units(self, eng, body):
        with eng.Fori(0, self.loops) as i:
            for u in range(self.SLOTS):
                body(i * self.SLOTS + (self.SLOTS + u), u, i + 1, False)
        for e in range(self.SLOTS * (self.loops + 1), self.n_units):
            body(e, e % self.SLOTS, e // self.SLOTS, False)

    def units(self, eng, body):
        self.first_units(body)
        self.later_units(eng, body)

    def load_unit(self, sp, e, slot, before):
        if not (isinstance(before, int) and before == 0):
            sp.wait_ge(self.w_split, e - (self.SLOTS - 1))
        sp.dma_start(self.raw[slot][:], self.source[e]).then_inc(self.w_in[slot], 16)

    def split_unit(self, pool, order, e, slot, before, plain):
        nc, n_plain = self.nc, self.n_plain
        raw, w_hi, w_lo, pick = self.raw[slot], self.w_hi[slot], self.w_lo[slot], self.pick[slot]
        order.done = e + 1 if plain else e * 2 - (n_plain - 1)
        if not (isinstance(before, int) and before == 0):
            pool.wait_ge(self.down_mm, e * 2 - (2 * self.SLOTS - 2))
        pool.wait_ge(self.w_in[slot], before * 16 + 16)

        def keep(dst, src, zeros):
            order.link(nc.gpsimd.tensor_tensor(dst, src, zeros, ALU.add))

        keep(w_hi[:], raw[:], self.zero[:].to_broadcast(list(raw.shape)))
        if self.gated and not plain:
            keep(pick[:], self.e2_t[:, bass.ds(e - n_plain, 1)].to_broadcast([P, P]), self.zero[:].to_broadcast([P, P]))
        elif not plain:
            keep(pick[:].rearrange("p (a b) -> p a b", a=2),
                 self.e2_t[:, bass.ds(e * 2 - 2 * n_plain, 2)].unsqueeze(2).to_broadcast([P, 2, 64]),
                 self.zero[:].unsqueeze(2).to_broadcast([P, 2, 64]))
        nc.gpsimd.tensor_tensor(w_lo[:], raw[:], w_hi[:].bitcast(F32), ALU.subtract).then_inc(self.w_split, 1)
        pool.wait_ge(self.w_split, e + 1)

    def load(self, sp):
        sp.dma_start(self.e2_t[:], self.e2).then_inc(self.e2_in, 16)
        self.first_units(lambda e, slot, before, plain: self.load_unit(sp, e, slot, before))

    def split(self, pool):
        order = Order(pool, self.order_sem)
        order.link(self.nc.gpsimd.memset(self.zero[:], 0.0))
        pool.wait_ge(self.e2_in, 16)
        for e in range(self.n_plain):
            self.split_unit(pool, order, e, e, 0, True)


def experts(nc, chip, tag, exp, layer, router, mod=None):
    NP, cwT = exp.n_plain, router.cwT
    gated, n_units, UPS, WUP, WSLOTS, units = exp.gated, exp.n_units, exp.ups, exp.wup, exp.SLOTS, exp.units
    w_hi, w_lo, pick, w_split, down_mm = exp.w_hi, exp.w_lo, exp.pick, exp.w_split, exp.down_mm
    n = f"e{tag}_"
    with ExitStack() as ctx:
        a = chip.sb(n + "a", [P, 2, HALF], ctx=ctx)
        t = chip.sb(n + "t", [P, 2, HALF], ctx=ctx)
        hf = chip.sb(n + "hf", [P, 2, HALF], ctx=ctx)
        hh = chip.sb(n + "hh", [P, 2, HALF], F32R, ctx)
        hl = chip.sb(n + "hl", [P, 2, HALF], F32R, ctx)
        first_mm, up_mm, pick_mm, a_done, t_done, hf_done, hh_done, hl_done = (
            chip.sem(n + s) for s in ("fm", "um", "bm", "a", "t", "hf", "hh", "hl"))
        block = ctx.enter_context(nc.Block())

        def first(e):
            return isinstance(e, int) and e == 0

        @block.sync
        def _(sp):
            exp.later_units(sp, lambda e, slot, before, plain: exp.load_unit(sp, e, slot, before))

        @block.gpsimd
        def _(pool):
            order = Order(pool, exp.order_sem)
            exp.split_unit(pool, order, NP, NP, 0, False)
            for u in range(2 * NP):
                pool.wait_ge(hh_done, u + 1)
                if u >= 2:
                    pool.wait_ge(down_mm, u - 1)
                nc.gpsimd.tensor_tensor(hl[:, u % 2, :], hf[:, u % 2, :], hh[:, u % 2, :].bitcast(F32), ALU.subtract)\
                    .then_inc(hl_done, 1)
            for e in range(NP + 1, WSLOTS):
                exp.split_unit(pool, order, e, e, 0, False)
            exp.later_units(pool, lambda e, slot, before, plain:
                            exp.split_unit(pool, order, e, slot, before, plain))

        def up_bank(half):
            return 5 if gated else 4 + half

        def pick_bank(half):
            return 6 if gated else 6 + half

        @block.tensor
        def _(pe):
            def up(e, par, half, plain):
                cols = slice(half * HALF, (half + 1) * HALF)
                u = e * 2 + half
                now = not first(e)
                for m in range(UPS):
                    bank = 4 if gated and m == 0 else up_bank(half)
                    if gated:
                        if now or half:
                            pe.wait_ge(a_done if m == 0 else t_done, u)
                    elif now:
                        pe.wait_ge(a_done, u - 1)
                    three_parts(chip.ps[:, bank, :], nc,
                                lambda k: w_hi[par][:, (m * NC + k) * P:(m * NC + k + 1) * P],
                                lambda k: w_lo[par][:, (m * NC + k) * P:(m * NC + k + 1) * P],
                                lambda k: chip.h_hi[:, k, cols], lambda k: chip.h_lo[:, k, cols],
                                range(NC)).then_inc(first_mm if m == 0 else up_mm, 1)
                if isinstance(e, int) and e == NP and half == 0:
                    if mod:
                        pe.wait_ge(router.kept, 1)
                        mod.products(pe, router.BANK)
                        pe.wait_ge(mod.ready, 1)
                    else:
                        chip.keep_busy(router.BANK + 1, 7)
                    router.turn(pe)
                if not plain:
                    if isinstance(e, int) and e == NP:
                        pe.wait_ge(router.ready, NH)
                    if gated:
                        pe.wait_ge(hf_done, u)
                    elif not (isinstance(e, int) and e == NP):
                        pe.wait_ge(t_done, u - (1 + 2 * NP))
                    nc.tensor.matmul(chip.ps[:, pick_bank(half), :], pick[par][:], cwT[:, cols],
                                     start=True, stop=True).then_inc(pick_mm, 1)

            def down(e, par, half, last):
                pe.wait_ge(hl_done, e * 2 + (half + 1))
                for c in range(NC):
                    for r, (w, h) in enumerate(((w_hi, hh), (w_hi, hl), (w_lo, hh))):
                        mm = nc.tensor.matmul(chip.ps[:, c * NH + half, :],
                                              w[par][:, WUP + c * P:WUP + (c + 1) * P], h[:, half, :],
                                              start=(first(e) and r == 0), stop=(last and r == 2),
                                              skip_group_check=True)
                mm.then_inc(down_mm, 1)

            def body(e, par, before, plain):
                pe.wait_ge(w_split, e + 1)
                for half in range(2):
                    up(e, par, half, plain)
                    if not first(e):
                        down(e - 1, (par - 1) % WSLOTS, half, False)

            router.logits(pe)
            router.turn_scores(pe)
            units(pe, body)
            for half in range(2):
                down(n_units - 1, (n_units - 1) % WSLOTS, half, True)

        @block.scalar
        def _(act):
            def body(e, par, before, plain):
                for half in range(2):
                    u = e * 2 + half
                    bank = 4 if gated else 4 + half
                    act.wait_ge(first_mm, u + 1)
                    if not first(e):
                        act.wait_ge(t_done if gated else hf_done, u - 1)
                    nc.scalar.activation(a[:, half, :], chip.ps[:, bank, :], ACT.Silu if gated else ACT.Relu)\
                        .then_inc(a_done, 1)
                    if plain:
                        act.wait_ge(t_done if gated else a_done, u + 1)
                        if not first(e):
                            act.wait_ge(hl_done, u - 1)
                        nc.scalar.activation(hf[:, half, :], (t if gated else a)[:, half, :],
                                             ACT.Copy if gated else ACT.Square).then_inc(hf_done, 1)
                    act.wait_ge(hf_done, u + 1)
                    if not first(e):
                        act.wait_ge(down_mm, u - 1)
                    nc.scalar.activation(hh[:, half, :], hf[:, half, :], ACT.Copy).then_inc(hh_done, 1)

            if mod:
                mod.activate(act)
            chip.warm_up(ACT.Sigmoid)
            router.scores(act)
            if gated:
                chip.warm_up(ACT.Silu)
            units(act, body)

        @block.vector
        def _(dve):
            def times_up(u, half):
                dve.wait_ge(a_done, u + 1)
                dve.wait_ge(up_mm, u + 1)
                nc.vector.tensor_tensor(t[:, half, :], a[:, half, :], chip.ps[:, 5, :], ALU.mult).then_inc(t_done, 1)

            def inner(e, half):
                u = e * 2 + half
                dve.wait_ge(hl_done, u - 1)
                if gated:
                    times_up(u, half)
                    dve.wait_ge(t_done, u + 1)
                    other, picked = t, chip.ps[:, 6, :]
                    dve.wait_ge(pick_mm, u - (2 * NP - 1))
                else:
                    dve.wait_ge(a_done, u + 1)
                    dve.wait_ge(pick_mm, u - (2 * NP - 1))
                    nc.vector.tensor_tensor(t[:, half, :], a[:, half, :], chip.ps[:, 6 + half, :], ALU.mult)\
                        .then_inc(t_done, 1)
                    dve.wait_ge(t_done, u - (2 * NP - 1))
                    other, picked = t, a[:, half, :]
                nc.vector.tensor_tensor(hf[:, half, :], other[:, half, :], picked, ALU.mult).then_inc(hf_done, 1)

            def low(e, half):
                u = e * 2 + half
                dve.wait_ge(hh_done, u + 1)
                dve.wait_ge(down_mm, u - 1)
                nc.vector.tensor_tensor(hl[:, half, :], hf[:, half, :], hh[:, half, :].bitcast(F32), ALU.subtract)\
                    .then_inc(hl_done, 1)

            def body(e, par, before, plain):
                if not plain:
                    for half in range(2):
                        inner(e, half)
                        low(e, half)

            halves = iter(range(2 * NP if gated else 0))

            def between():
                for u in halves:
                    times_up(u, u)
                    break

            router.choose(dve, between)
            if mod:
                mod.columns(dve, router.BANK)
            router.keep(dve)
            dve.wait_ge(hf_done, 2 * NP)
            dve.wait_ge(hl_done, 2 * NP)
            units(dve, body)
            for half in range(NH):
                dve.wait_ge(down_mm, 2 * n_units - 1 + half)
                for c in range(NC):
                    cols = slice(half * HALF, (half + 1) * HALF)
                    nc.vector.scalar_tensor_tensor(chip.xT[:, c, cols], chip.ps[:, c * NH + half, :],
                                                   mod_col(chip, layer, 5, c), chip.xT[:, c, cols], ALU.mult, ALU.add)
class Attention1Weights:
    loaded = False
    SCALE = float(D) ** -0.5

    def __init__(self, nc, chip, ctx, matrices, biases):
        self.nc, self.matrices, self.biases = nc, matrices, biases
        self.raw = chip.sb("b_wraw", [P, 4, NC, D], BF16, ctx)
        self.b_raw = chip.sb("b_braw", [P, 4, LAYERS, NC], BF16, ctx)
        self.w = chip.sb("b_w", [P, 4, NC, D], F32R, ctx)
        self.w_in, self.wo_in, self.b_in, self.w_ready, self.order_sem = (
            chip.sem("b_" + s) for s in ("win", "woin", "bin", "wok", "sord"))

    def load_qkv(self, sp, i):
        for n in range(3):
            sp.dma_start(self.raw[:, n], self.matrices[n][i].rearrange("(k p) n -> p k n", p=P))\
                .then_inc(self.w_in, 16)

    def load_o(self, sp, i):
        sp.dma_start(self.raw[:, 3], self.matrices[3][i].rearrange("(k p) n -> p k n", p=P)).then_inc(self.wo_in, 16)

    def load(self, sp):
        self.load_qkv(sp, 0)
        for n, m in enumerate(self.biases):
            sp.dma_start(self.b_raw[:, n], m.rearrange("l p c -> p l c")).then_inc(self.b_in, 16)
        self.load_o(sp, 0)

    def split(self, pool):
        pool.wait_ge(self.w_in, 48)
        for m in (1, 0, 2):
            if m == 0:
                op = self.nc.gpsimd.tensor_scalar(self.w[:, m], self.raw[:, m], self.SCALE, None, ALU.mult)
            else:
                op = self.nc.gpsimd.tensor_copy(self.w[:, m], self.raw[:, m])
            op.then_inc(self.w_ready, 1)


def attention1(nc, chip, weights):
    ps = chip.ps
    SCALE = weights.SCALE
    LAST = LAYERS - 1
    PJ, VB, OB = 8, NJ // 2, NC * NH
    T_BANK, O_BANK = 4, 6
    FIRST, SECOND = 0, 2
    SLOTS = 3
    with ExitStack() as ctx:
        w_raw, b_raw, w = weights.raw, weights.b_raw, weights.w
        b_all = chip.sb("b_ball", [P, 4, LAYERS, NC], ctx=ctx)
        b = chip.sb("b_b", [P, 4, NC], ctx=ctx)
        gb = chip.sb("b_gb", [P, NC], ctx=ctx)
        qk_hi = chip.sb("b_qkh", [P, 2, NC, T], F32R, ctx)
        qk_lo = chip.sb("b_qkl", [P, 2, NC, T], F32R, ctx)
        v_hi = chip.sb("b_vh", [P, NJ, D], F32R, ctx)
        v_lo = chip.sb("b_vl", [P, NJ, D], F32R, ctx)
        nm = chip.sb("b_nm", [P, SLOTS], ctx=ctx)
        rs = chip.sb("b_rs", [P, SLOTS], ctx=ctx)
        ri = chip.sb("b_ri", [P, SLOTS], ctx=ctx)
        pr = chip.sb("b_p", [P, SLOTS, T], ctx=ctx)
        pt_hi = chip.sb("b_pth", [P, NJ, T], F32R, ctx)
        pt_lo = chip.sb("b_ptl", [P, NJ, T], F32R, ctx)
        a_hi = chip.sb("b_ah", [P, NC, T], F32R, ctx)
        a_lo = chip.sb("b_al", [P, NC, T], F32R, ctx)
        w_in, wo_in, b_in, w_ready = weights.w_in, weights.wo_in, weights.b_in, weights.w_ready
        names = ("wook", "bok", "pj", "pjh", "pjl", "vm", "vh", "vl", "sm", "mx", "ex",
                 "nr", "tm", "th", "tl", "om", "oh", "ol", "fm", "fh", "fl", "ord")
        (wo_ready, b_ready, pj_mm, pj_hi, pj_lo, v_mm, v_his, v_los, s_mm, s_max, s_exp,
         s_norm, t_mm, t_hi, t_lo, o_mm, o_hi, o_lo, f_mm, f_hi, f_lo, osem) = (
            chip.sem("b_" + s) for s in names)
        block = ctx.enter_context(nc.Block())

        def halfcols(half):
            return slice(half * HALF, (half + 1) * HALF)

        def score_banks(j):
            bank = FIRST if j % 2 else SECOND
            return slice(bank, bank + 2)

        K_FIRST = [(0, 1, 0, 0, FIRST), (1, 1, 1, 0, FIRST + 1)]
        Q_FIRST = [(2, 0, 0, 0, FIRST), (3, 0, 1, 0, FIRST + 1)]
        K_SECOND = [(4, 1, 0, 1, O_BANK), (5, 1, 1, 1, O_BANK + 1)]
        Q_SECOND = [(6, 0, 0, 1, FIRST), (7, 0, 1, 1, FIRST + 1)]

        @block.sync
        def _(sp):
            with sp.Fori(0, LAST) as i:
                sp.wait_ge(w_ready, i * 3 + 3)
                weights.load_qkv(sp, i + 1)
                sp.wait_ge(wo_ready, i + 1)
                weights.load_o(sp, i + 1)

        @block.tensor
        def _(pe):
            def two_parts(out, lhs, rhs):
                n = len(lhs)
                for i in range(n):
                    last = nc.tensor.matmul(out, lhs[i], rhs[i], start=(i == 0), stop=(i == n - 1))
                return last

            def project(blocks):
                for n, m, c, half, bank in blocks:
                    wc = [w[:, m, k, c * P:(c + 1) * P] for k in range(NC)]
                    two_parts(ps[:, bank, :], [wc[0], wc[0], wc[1], wc[1]],
                              [x[:, k, halfcols(half)] for k in range(NC) for x in (chip.h_hi, chip.h_lo)])\
                        .then_inc(pj_mm, 1)

            def project_v(half):
                for bank in range(2):
                    for u in range(2):
                        rows = slice((half * 4 + bank * 2 + u) * P, (half * 4 + bank * 2 + u + 1) * P)
                        last = two_parts(ps[:, T_BANK + bank, u * D:(u + 1) * D],
                                         [x[:, k, rows] for k in range(NC) for x in (chip.h_hi, chip.h_lo)],
                                         [w[:, 2, 0, :], w[:, 2, 0, :], w[:, 2, 1, :], w[:, 2, 1, :]])
                    last.then_inc(v_mm, 1)

            def layer(i, last_layer):
                def scores(j):
                    if j == 0:
                        pe.wait_ge(pj_lo, i * PJ + 6)
                    elif j == 1:
                        pe.wait_ge(pj_lo, i * PJ + PJ)
                    else:
                        pe.wait_ge(s_exp, i * NJ + (j - 1))
                    rows = slice(j * P, (j + 1) * P)
                    for half in range(NH):
                        last = three_parts(ps[:, score_banks(j).start + half, :], nc,
                                           lambda k: qk_hi[:, 0, k, rows], lambda k: qk_lo[:, 0, k, rows],
                                           lambda k: qk_hi[:, 1, k, halfcols(half)],
                                           lambda k: qk_lo[:, 1, k, halfcols(half)], range(NC))
                    last.then_inc(s_mm, 1)

                def turn(j):
                    pe.wait_ge(s_norm, i * NJ + (j + 1))
                    if j == 0:
                        pe.wait_ge(v_los, i * VB + VB)
                    else:
                        pe.wait_ge(t_lo, i * NJ + j)
                    for kt in range(NJ):
                        last = nc.tensor.transpose(ps[:, T_BANK + kt // 4, (kt % 4) * P:(kt % 4 + 1) * P],
                                                   pr[:, j % SLOTS, kt * P:(kt + 1) * P], chip.ident[:])
                    last.then_inc(t_mm, 1)

                def values(half, c):
                    pe.wait_ge(t_lo, i * NJ + 4 * (half + 1))
                    cc = slice(c * P, (c + 1) * P)
                    three_parts(ps[:, O_BANK + c, :], nc,
                                lambda k: v_hi[:, k, cc], lambda k: v_lo[:, k, cc],
                                lambda k: pt_hi[:, k, halfcols(half)], lambda k: pt_lo[:, k, halfcols(half)],
                                range(NJ)).then_inc(o_mm, 1)

                def project_out(half):
                    pe.wait_ge(o_lo, i * OB + NC * (half + 1))
                    if half:
                        pe.wait_ge(f_lo, i * OB + (1 + NC))
                    else:
                        pe.wait_ge(s_exp, i * NJ + 7)
                        pe.wait_ge(wo_ready, i + 1)
                    for c in range(NC):
                        wc = [w[:, 3, k, c * P:(c + 1) * P] for k in range(NC)]
                        two_parts(ps[:, SECOND + c, :], [wc[0], wc[0], wc[1], wc[1]],
                                  [x[:, k, halfcols(half)] for k in range(NC) for x in (a_hi, a_lo)])\
                            .then_inc(f_mm, 1)

                pe.wait_ge(f_lo, i * OB + 1)
                project(K_SECOND)
                pe.wait_ge(pj_lo, i * PJ + 4)
                project(Q_SECOND)
                pe.wait_ge(v_los, i * VB + VB // 2)
                project_v(1)
                for j in range(NJ):
                    scores(j)
                    if j >= 2:
                        turn(j - 2)
                    if j >= NJ - 2:
                        values(0, j - (NJ - 2))
                turn(NJ - 2)
                project_out(0)
                turn(NJ - 1)
                if not last_layer:
                    pe.wait_ge(w_ready, i * 3 + 6)
                    pe.wait_ge(f_lo, i * OB + (1 + NC))
                    pe.wait_ge(s_exp, i * NJ + NJ)
                    project(K_FIRST)
                values(1, 0)
                values(1, 1)
                if not last_layer:
                    project_v(0)
                project_out(1)
                if not last_layer:
                    pe.wait_ge(pj_lo, i * PJ + (PJ + 2))
                    project(Q_FIRST)

            pe.wait_ge(w_ready, 3)
            project(K_FIRST)
            project_v(0)
            pe.wait_ge(pj_lo, 2)
            project(Q_FIRST)
            with pe.Fori(0, LAST) as i:
                layer(i, False)
            layer(LAST, True)

        @block.scalar
        def _(act):
            def take_weights(m, scale, sem):
                nc.scalar.activation(w[:, m], w_raw[:, m], ACT.Copy, scale=scale).then_inc(sem, 1)

            def keep(blocks, i):
                for n, m, c, half, bank in blocks:
                    act.wait_ge(pj_mm, i * PJ + (n + 1))
                    nc.scalar.activation(qk_hi[:, m, c, halfcols(half)], ps[:, bank, :], ACT.Identity,
                                         bias=b[:, m, c:c + 1]).then_inc(pj_hi, 1)

            def keep_v(half, i):
                for bank in range(2):
                    act.wait_ge(v_mm, i * VB + (half * 2 + bank + 1))
                    j = half * 4 + bank * 2
                    nc.scalar.activation(v_hi[:, j:j + 2, :], ps[:, T_BANK + bank, :].rearrange("p (j d) -> p j d", j=2),
                                         ACT.Copy).then_inc(v_his, 1)

            def layer(i, last_layer):
                def exps(j):
                    act.wait_ge(s_max, i * NJ + (j + 1))
                    if j >= SLOTS:
                        act.wait_ge(t_mm, i * NJ + (j - SLOTS + 1))
                    u = j % SLOTS
                    nc.scalar.activation(pr[:, u, :], ps[:, score_banks(j), :], ACT.Exp,
                                         bias=nm[:, u:u + 1], accum_out=rs[:, u:u + 1]).then_inc(s_exp, 1)

                def keep_turned(j):
                    act.wait_ge(t_mm, i * NJ + (j + 1))
                    nc.scalar.activation(pt_hi[:, :, j * P:(j + 1) * P],
                                         ps[:, T_BANK:T_BANK + 2, :].rearrange("p b (k q) -> p (b k) q", q=P),
                                         ACT.Copy).then_inc(t_hi, 1)

                def keep_values(half, c):
                    if half + c == 0:
                        act.wait_ge(b_ready, i * 2 + 2)
                    act.wait_ge(o_mm, i * OB + (half * NC + c + 1))
                    nc.scalar.activation(a_hi[:, c, halfcols(half)], ps[:, O_BANK + c, :], ACT.Identity,
                                         bias=b[:, 2, c:c + 1]).then_inc(o_hi, 1)

                def keep_h(half):
                    for c in range(NC):
                        act.wait_ge(f_mm, i * OB + (half * NC + c + 1))
                        nc.scalar.activation(chip.h_hi[:, c, halfcols(half)], ps[:, SECOND + c, :], ACT.Identity,
                                             bias=b[:, 3, c:c + 1]).then_inc(f_hi, 1)

                keep(K_SECOND, i)
                keep(Q_SECOND, i)
                keep_v(1, i)
                for j in range(NJ):
                    if j >= 2:
                        keep_turned(j - 2)
                    exps(j)
                    if j == 2:
                        act.wait_ge(wo_in, i * 16 + 16)
                        take_weights(3, 1.0, wo_ready)
                    if j in (3, 4, 5) and not last_layer:
                        act.wait_ge(v_mm, i * VB + VB)
                        act.wait_ge(w_in, i * 48 + 96)
                        take_weights(j - 3, SCALE if j == 3 else 1.0, w_ready)
                    if j >= NJ - 2:
                        keep_values(0, j - (NJ - 2))
                keep_turned(NJ - 2)
                if not last_layer:
                    keep_h(0)
                keep_turned(NJ - 1)
                if not last_layer:
                    act.wait_ge(b_ready, i * 2 + 3)
                    keep(K_FIRST, i + 1)
                keep_values(1, 0)
                keep_values(1, 1)
                if not last_layer:
                    keep_v(0, i + 1)
                    keep_h(1)
                    keep(Q_FIRST, i + 1)

            chip.warm_up(ACT.Exp)
            act.wait_ge(b_ready, 1)
            keep(K_FIRST, 0)
            keep_v(0, 0)
            keep(Q_FIRST, 0)
            with act.Fori(0, LAST) as i:
                layer(i, False)
            layer(LAST, True)

        @block.vector
        def _(dve):
            order = Order(dve, osem)
            MARKS = NJ

            def low(dst, psum, bias, hi, sem):
                nc.vector.scalar_tensor_tensor(dst, psum, bias, hi.bitcast(F32), ALU.add, ALU.subtract)\
                    .then_inc(sem, 1)

            def keep(blocks, i):
                for n, m, c, half, bank in blocks:
                    dve.wait_ge(pj_hi, i * PJ + (n + 1))
                    low(qk_lo[:, m, c, halfcols(half)], ps[:, bank, :], b[:, m, c:c + 1],
                        qk_hi[:, m, c, halfcols(half)], pj_lo)

            def keep_v(half, i):
                for bank in range(2):
                    dve.wait_ge(v_his, i * VB + (half * 2 + bank + 1))
                    j = half * 4 + bank * 2
                    nc.vector.tensor_tensor(v_lo[:, j:j + 2, :], ps[:, T_BANK + bank, :].rearrange("p (j d) -> p j d", j=2),
                                            v_hi[:, j:j + 2, :].bitcast(F32), ALU.subtract).then_inc(v_los, 1)

            def take_biases(m, i):
                nc.vector.tensor_copy(b[:, m:m + 2, :], b_all[:, m:m + 2, i, :]).then_inc(b_ready, 1)
                dve.wait_ge(b_ready, i * 2 + (1 if m == 0 else 2))

            def layer(i, last_layer):
                order.done = i * MARKS + base

                def maxima(j):
                    dve.wait_ge(s_mm, i * NJ + (j + 1))
                    u = j % SLOTS
                    nc.vector.tensor_reduce(nm[:, u:u + 1], ps[:, score_banks(j), :], AX.XY, ALU.max, negate=True)\
                        .then_inc(s_max, 1)

                def invert(j):
                    dve.wait_ge(s_exp, i * NJ + (j + 1))
                    u = j % SLOTS
                    order.mark(nc.vector.reciprocal(ri[:, u:u + 1], rs[:, u:u + 1]))

                def normalise(j):
                    u = j % SLOTS
                    order.settle()
                    nc.vector.tensor_scalar(pr[:, u, :], pr[:, u, :], ri[:, u:u + 1], None, ALU.mult)\
                        .then_inc(s_norm, 1)

                def low_turned(j):
                    dve.wait_ge(t_hi, i * NJ + (j + 1))
                    cols = slice(j * P, (j + 1) * P)
                    nc.vector.tensor_tensor(pt_lo[:, :, cols],
                                            ps[:, T_BANK:T_BANK + 2, :].rearrange("p b (k q) -> p (b k) q", q=P),
                                            pt_hi[:, :, cols].bitcast(F32), ALU.subtract).then_inc(t_lo, 1)

                def low_values(half, c):
                    dve.wait_ge(o_hi, i * OB + (half * NC + c + 1))
                    low(a_lo[:, c, halfcols(half)], ps[:, O_BANK + c, :], b[:, 2, c:c + 1],
                        a_hi[:, c, halfcols(half)], o_lo)

                def low_h(half):
                    for c in range(NC):
                        dve.wait_ge(f_hi, i * OB + (half * NC + c + 1))
                        low(chip.h_lo[:, c, halfcols(half)], ps[:, SECOND + c, :], b[:, 3, c:c + 1],
                            chip.h_hi[:, c, halfcols(half)], f_lo)

                def residual(half):
                    for c in range(NC):
                        dve.wait_ge(f_mm, i * OB + (half * NC + c + 1))
                        nc.vector.scalar_tensor_tensor(chip.xT[:, c, halfcols(half)], ps[:, SECOND + c, :],
                                                       mod_col(chip, 1, 2, c), chip.xT[:, c, halfcols(half)],
                                                       ALU.mult, ALU.add).then_inc(f_lo, 1)

                keep(K_SECOND, i)
                keep(Q_SECOND, i)
                take_biases(2, i)
                if not last_layer:
                    take_biases(0, i + 1)
                keep_v(1, i)
                maxima(0)
                for j in range(1, NJ):
                    invert(j - 1)
                    maxima(j)
                    normalise(j - 1)
                    if j >= 2:
                        low_turned(j - 2)
                    if j == NJ - 2:
                        low_values(0, 0)
                invert(NJ - 1)
                normalise(NJ - 1)
                if last_layer:
                    order.link(nc.vector.tensor_tensor(gb[:], b[:, 3, :], chip.mods[1][:, 2 * NC:3 * NC], ALU.mult))
                    for c in range(NC):
                        order.mark(nc.vector.tensor_scalar(chip.xT[:, c, :], chip.xT[:, c, :], gb[:, c:c + 1], None,
                                                           ALU.add))
                    order.settle()
                low_values(0, 1)
                low_turned(NJ - 2)
                if last_layer:
                    residual(0)
                else:
                    low_h(0)
                low_turned(NJ - 1)
                if not last_layer:
                    keep(K_FIRST, i + 1)
                low_values(1, 0)
                low_values(1, 1)
                if last_layer:
                    residual(1)
                else:
                    keep_v(0, i + 1)
                    low_h(1)
                    keep(Q_FIRST, i + 1)

            nc.vector.memset(gb[:], 0.0).then_inc(f_lo, 1)
            dve.wait_ge(f_lo, 1)
            dve.wait_ge(b_in, 64)
            order.mark(nc.vector.tensor_scalar(b_all[:, 0], b_raw[:, 0], SCALE, None, ALU.mult))
            order.link(nc.vector.tensor_copy(b_all[:, 1:4], b_raw[:, 1:4]))
            take_biases(0, 0)
            keep(K_FIRST, 0)
            keep_v(0, 0)
            keep(Q_FIRST, 0)
            base = order.done
            with dve.Fori(0, LAST) as i:
                layer(i, False)
            layer(LAST, True)


def store(nc, chip, out):
    with ExitStack() as ctx:
        o = chip.sb("s_o", [P, NJ, D], ctx=ctx)
        turned, kept, stored = (chip.sem("s_" + s) for s in ("turned", "kept", "stored"))
        block = ctx.enter_context(nc.Block())
        dst = out.rearrange("a (j p) d -> p (a j) d", p=P)

        @block.tensor
        def _(pe):
            for j in range(NJ):
                for c in range(NC):
                    last = nc.tensor.transpose(chip.ps[:, j // 2, (j % 2) * D + c * P:(j % 2) * D + (c + 1) * P],
                                               chip.xT[:, c, j * P:(j + 1) * P], chip.ident[:])
                if j % 2:
                    last.then_inc(turned, 1)

        @block.vector
        def _(dve):
            for b in range(NJ // 2):
                dve.wait_ge(turned, b + 1)
                nc.vector.tensor_copy(o[:, 2 * b:2 * b + 2, :],
                                      chip.ps[:, b, :].rearrange("p (j d) -> p j d", j=2)).then_inc(kept, 1)

        @block.sync
        def _(sp):
            for b in range(2):
                sp.wait_ge(kept, 2 * b + 2)
                sp.dma_start(dst[:, 4 * b:4 * b + 4, :], o[:, 4 * b:4 * b + 4, :]).then_inc(stored, 16)
            sp.wait_ge(stored, 32)


def two_adaln_layers_kernel(nc: bass.Bass, x, c0, wmod0, wq0, wk0, wv0, wo0, router0, router_bias0, experts0,
                            c1, wmod1, wq1, bq1, wk1, bk1, wv1, bv1, wo1, bo1, router1, router_bias1, experts1,
                            ident, rep_q, rep_k, lanes, e2, tri, out):
    with ExitStack() as ctx:
        chip = Chip(nc, ctx)
        with ExitStack() as stage:
            with ExitStack() as start:
                att = Attention0(nc, chip, stage, start, wq0, wk0, wv0, wo0, rep_q, rep_k, lanes)
                mod = Modulation(nc, chip, start, 0, c0, wmod0)
                first_load(nc, chip, x, ident, (mod, att))
                norm(nc, chip, "0a", 0, 0, 1, (att,), mod)
                attention0_project(nc, chip, att)
            attention0_core(nc, chip, att)
            attention0_output(nc, chip, att)
        with ExitStack() as stage:
            router = Router(nc, chip, stage, "0", router0, router_bias0, tri, E0, G0, TOPG0, K0, SCALE0)
            exp = Experts(nc, chip, stage, "0", experts0, True, experts0.shape[0] - E0, e2)
            mod = Modulation(nc, chip, stage, 1, c1, wmod1)
            norm(nc, chip, "0b", 0, 3, 4, (router, exp, mod))
            experts(nc, chip, "0", exp, 0, router, mod)
        with ExitStack() as stage:
            weights = Attention1Weights(nc, chip, stage, (wq1, wk1, wv1, wo1), (bq1, bk1, bv1, bo1))
            norm(nc, chip, "1a", 1, 0, 1, (weights,))
            attention1(nc, chip, weights)
        with ExitStack() as stage:
            router = Router(nc, chip, stage, "1", router1, router_bias1, tri, E1, G1, TOPG1, K1, SCALE1)
            exp = Experts(nc, chip, stage, "1", experts1, False, experts1.shape[0] - E1 // 2, e2)
            norm(nc, chip, "1b", 1, 3, 4, (router, exp))
            experts(nc, chip, "1", exp, 1, router)
        store(nc, chip, out)



def shape_constants():
    c = {"ident": np.eye(P, dtype=np.float32)}
    rep_q = np.zeros((P, 2, P), np.float32)
    rep_k = np.zeros((P, KV_HEADS, P), np.float32)
    for h in range(GQ):
        for d in range(DH):
            for r, (q_lo, k_lo) in enumerate(((0, 0), (0, 1), (1, 0))):
                col = h * QUAD + r * DH + d
                for b in range(2):
                    rep_q[64 * q_lo + b * GQ * DH + h * DH + d, b, col] = 1
                for g in range(KV_HEADS):
                    rep_k[64 * k_lo + g * DH + d, g, col] = 1
    lanes = np.zeros((P, 2), np.float32)
    lanes[64:, 0] = -1
    for h in range(GQ):
        lanes[[h * QUAD + M_HI, h * QUAD + M_LO], 1] = 1
    e2 = (np.arange(P)[:, None] % 64 == np.arange(64)[None, :]).astype(np.float32)
    tri = np.broadcast_to(np.tril(np.ones((8, 8), np.float32), -1), (P, 8, 8)).copy()
    return c | {"rep_q": rep_q, "rep_k": rep_k, "lanes": lanes, "e2": e2, "tri": tri}


def gated_weights(gate, up, down, s_gate, s_up, s_down):
    def first(a, s):
        a = np.concatenate([s[None], a])
        return a.transpose(0, 2, 1).reshape(len(a), NC, P, P).transpose(0, 2, 1, 3).reshape(len(a), P, NC * P)
    last = np.concatenate([s_down[None], down]).transpose(0, 2, 1)
    return np.ascontiguousarray(np.concatenate([first(gate, s_gate), first(up, s_up), last], axis=2))


def squared_weights(w1, w2, s_up, s_down):
    i = w1.shape[1]
    up = np.concatenate([s_up.reshape(-1, i, D), w1]).reshape(-1, P, D)
    up = up.transpose(0, 2, 1).reshape(len(up), NC, P, P).transpose(0, 2, 1, 3).reshape(len(up), P, NC * P)
    down = np.concatenate([s_down.T.reshape(-1, i, D), w2.transpose(0, 2, 1)]).reshape(-1, P, D)
    return np.ascontiguousarray(np.concatenate([up, down], axis=2))


def kernel(**inputs):
    import concourse.bacc as bacc
    from concourse.bass_utils import run_bass_kernel_spmd

    a = {k: np.asarray(v) for k, v in inputs.items()}
    cols = lambda v: v.reshape(NC, P).T
    bias = lambda v: v.reshape(LAYERS, NC, P).transpose(0, 2, 1)
    args = {
        "x": a["L0_attn_X"], "c0": cols(a["L0_c"]), "wmod0": a["L0_wmod"],
        "wq0": a["L0_attn_Wq"], "wk0": a["L0_attn_Wk"], "wv0": a["L0_attn_Wv"], "wo0": a["L0_attn_Wo"],
        "router0": a["L0_ffn_gate_weight"].T, "router_bias0": a["L0_ffn_expert_bias"],
        "experts0": gated_weights(a["L0_ffn_gate_proj"], a["L0_ffn_up_proj"], a["L0_ffn_down_proj"],
                                  a["L0_ffn_shared_gate"], a["L0_ffn_shared_up"], a["L0_ffn_shared_down"]),
        "c1": cols(a["L1_c"]), "wmod1": a["L1_wmod"],
        "wq1": a["L1_attn_Wq"], "bq1": bias(a["L1_attn_bq"]), "wk1": a["L1_attn_Wk"], "bk1": bias(a["L1_attn_bk"]),
        "wv1": a["L1_attn_Wv"], "bv1": bias(a["L1_attn_bv"]), "wo1": a["L1_attn_Wo"], "bo1": bias(a["L1_attn_bo"]),
        "router1": a["L1_ffn_gate_w"].T, "router_bias1": a["L1_ffn_gate_bias"],
        "experts1": squared_weights(a["L1_ffn_w1"], a["L1_ffn_w2"], a["L1_ffn_shared_up"], a["L1_ffn_shared_down"]),
    } | shape_constants()
    nc = bacc.Bacc("TRN2", target_bir_lowering=False, num_devices=1)
    arrays, aps = {}, {}
    for name, v in args.items():
        arrays[f"in_{name}"] = v = np.ascontiguousarray(v)
        aps[name] = nc.dram_tensor(f"in_{name}", v.shape, mybir.dt.from_np(v.dtype), kind="ExternalInput").ap()
    aps["out"] = nc.dram_tensor("out_x", (1, T, D), F32, kind="ExternalOutput").ap()
    two_adaln_layers_kernel(nc, **aps)
    r = run_bass_kernel_spmd(nc, [arrays], core_ids=[0])
    return r.results[0]["out_x"]
```
